# Optimizing a Trainium2 kernel written in Bass

```python
import numpy as np
import jax
import jax.numpy as jnp

def _softmax(x, axis=-1):
    return jax.nn.softmax(x, axis=axis)
def _gelu(x):
    return jax.nn.gelu(x, approximate=True)
def _silu(x):
    return jax.nn.silu(x)
def _sigmoid(x):
    return jax.nn.sigmoid(x)
def _layernorm(x, axis=-1, eps=1e-5):
    m = jnp.mean(x, axis=axis, keepdims=True)
    v = jnp.var(x, axis=axis, keepdims=True)
    return (x - m) / jnp.sqrt(v + eps)
def _scatter_add(tgt, idx, src, axis=0):
    return tgt.at[idx].add(src)
def _segment_sum(src, seg, n):
    return jax.ops.segment_sum(src, seg, n)

kernel_name = 'mk_conv_seq_d4_conv_nchw64_578b1a'

def setup_inputs(seed: int = 0):
    np.random.seed(seed)
    _w = jnp.asarray
    def _rec_inputs():
        import jax
        import jax.numpy as jnp
        _gk = jax.random.key(seed)
        x = -0.000929 + 1 * jax.random.normal(jax.random.fold_in(_gk, 1), (4, 64, 64, 64), jnp.float32)
        return x
    x = _rec_inputs()
    def _L0_conv_setup():
        import jax, jax.numpy as jnp
        import numpy as np
        from jax import lax
        C = 64
        D_INNER = 128
        D_STATE = 16
        D_CONV = 4
        DT_RANK = 4
        B, H, W = (4, 64, 64)

        def _mamba(h, in_proj_w, convd_w, convd_b, x_proj_w, dt_proj_w, dt_proj_b, A_log, Dp, out_proj_w):
            Bt, L, _ = h.shape
            xz = jnp.einsum('blc,dc->bld', h, in_proj_w)
            xm, z = jnp.split(xz, 2, axis=-1)
            xc = lax.conv_general_dilated(xm.transpose(0, 2, 1), convd_w, (1,), [(D_CONV - 1, 0)], feature_group_count=D_INNER, dimension_numbers=('NCH', 'OIH', 'NCH'))
            xc = jax.nn.silu(xc + convd_b[None, :, None]).transpose(0, 2, 1)
            dbc = jnp.einsum('bld,ed->ble', xc, x_proj_w)
            dt, Bm, Cm = jnp.split(dbc, [DT_RANK, DT_RANK + D_STATE], axis=-1)
            dt = jax.nn.softplus(jnp.einsum('blr,dr->bld', dt, dt_proj_w) + dt_proj_b)
            A = -jnp.exp(A_log)
            dA = jnp.exp(dt[..., None] * A)
            dBx = dt[..., None] * Bm[:, :, None, :] * xc[..., None]

            def step(hc, inp):
                dA_t, dBx_t, C_t = inp
                hc = hc * dA_t + dBx_t
                y = jnp.einsum('bds,bs->bd', hc, C_t)
                return (hc, y)
            h0 = jnp.zeros((Bt, D_INNER, D_STATE), h.dtype)
            _, ys = lax.scan(step, h0, (dA.transpose(1, 0, 2, 3), dBx.transpose(1, 0, 2, 3), Cm.transpose(1, 0, 2)))
            ys = ys.transpose(1, 0, 2)
            ys = (ys + xc * Dp) * jax.nn.silu(z)
            return jnp.einsum('bld,cd->blc', ys, out_proj_w)

        def _forward(x, dwh_w, dwh_b, dww_w, dww_b, conv_w, conv_b, bn_g, bn_b, bn_m, bn_v, ln_g, ln_b, in_proj_w, convd_w, convd_b, x_proj_w, dt_proj_w, dt_proj_b, A_log, Dp, out_proj_w):
            dn = ('NCHW', 'OIHW', 'NCHW')
            xh = lax.conv_general_dilated(x, dwh_w, (1, 1), 'SAME', feature_group_count=C, dimension_numbers=dn)
            xw = lax.conv_general_dilated(x, dww_w, (1, 1), 'SAME', feature_group_count=C, dimension_numbers=dn)
            x = x + xh + dwh_b[None, :, None, None] + xw + dww_b[None, :, None, None]
            x = lax.conv_general_dilated(x, conv_w, (1, 1), 'SAME', dimension_numbers=dn) + conv_b[None, :, None, None]
            x = (x - bn_m[None, :, None, None]) * lax.rsqrt(bn_v + 1e-05)[None, :, None, None] * bn_g[None, :, None, None] + bn_b[None, :, None, None]
            x = jax.nn.relu(x)
            Bt, Cc, Hh, Ww = x.shape
            seq = x.reshape(Bt, Cc, Hh * Ww).transpose(0, 2, 1)
            mu = seq.mean(-1, keepdims=True)
            var = ((seq - mu) ** 2).mean(-1, keepdims=True)
            hn = (seq - mu) * lax.rsqrt(var + 1e-05) * ln_g + ln_b
            y = _mamba(hn, in_proj_w, convd_w, convd_b, x_proj_w, dt_proj_w, dt_proj_b, A_log, Dp, out_proj_w)
            out = (y + seq).transpose(0, 2, 1).reshape(Bt, Cc, Hh, Ww)
            return out
        key = jax.random.key(seed)
        ks = jax.random.split(key, 22)

        def n(k, shape, s=0.05):
            return jax.random.normal(k, shape, jnp.float32) * s
        inp = {}
        inp['x'] = jax.random.normal(ks[0], (B, C, H, W), jnp.float32)
        inp['dwh_w'] = n(ks[1], (C, 1, 3, 1), 0.2)
        inp['dwh_b'] = n(ks[2], (C,))
        inp['dww_w'] = n(ks[3], (C, 1, 1, 3), 0.2)
        inp['dww_b'] = n(ks[4], (C,))
        inp['conv_w'] = n(ks[5], (C, C, 1, 1), 0.1)
        inp['conv_b'] = n(ks[6], (C,))
        inp['bn_g'] = jnp.ones((C,), jnp.float32)
        inp['bn_b'] = jnp.zeros((C,), jnp.float32)
        inp['bn_m'] = n(ks[7], (C,), 0.1)
        inp['bn_v'] = jnp.abs(n(ks[8], (C,), 0.1)) + 1.0
        inp['ln_g'] = jnp.ones((C,), jnp.float32)
        inp['ln_b'] = jnp.zeros((C,), jnp.float32)
        inp['in_proj_w'] = n(ks[9], (2 * D_INNER, C))
        inp['convd_w'] = n(ks[10], (D_INNER, 1, D_CONV), 0.2)
        inp['convd_b'] = n(ks[11], (D_INNER,))
        inp['x_proj_w'] = n(ks[12], (DT_RANK + 2 * D_STATE, D_INNER))
        inp['dt_proj_w'] = n(ks[13], (D_INNER, DT_RANK), 0.2)
        inp['dt_proj_b'] = n(ks[14], (D_INNER,), 0.5) - 4.0
        inp['A_log'] = jnp.log(jnp.tile(jnp.arange(1, D_STATE + 1, dtype=jnp.float32), (D_INNER, 1)))
        inp['Dp'] = jnp.ones((D_INNER,), jnp.float32)
        inp['out_proj_w'] = n(ks[15], (C, D_INNER))
        return inp
    _L0_conv_all = _L0_conv_setup()
    _L0_conv_in = {k: v for k, v in _L0_conv_all.items() if k in ('dwh_w', 'dwh_b', 'dww_w', 'dww_b', 'conv_w', 'conv_b', 'bn_g', 'bn_b', 'bn_m', 'bn_v', 'ln_g', 'ln_b', 'in_proj_w', 'convd_w', 'convd_b', 'x_proj_w', 'dt_proj_w', 'dt_proj_b', 'A_log', 'Dp', 'out_proj_w', )}
    del _L0_conv_all

    def _L1_conv_setup():
        import jax, jax.numpy as jnp
        import numpy as np
        D_IN = 96
        D_INT = 192
        N = 96
        DTR = 6
        K = 4
        BN_EPS = 1e-05

        def selective_scan(u, delta, A, B, C, D):
            A = jnp.clip(A, -5.0, 5.0)
            dA = jnp.einsum('bld,dn->bldn', delta, A)
            dB_u = jnp.einsum('bld,bld,bln->bldn', delta, u, B)
            c = jnp.concatenate([dA[:, 1:], jnp.zeros_like(dA[:, :1])], axis=1)
            c = jnp.flip(c, axis=1)
            c = jnp.cumsum(c, axis=1)
            c = jnp.exp(jnp.minimum(c, 15.0))
            c = jnp.flip(c, axis=1)
            x = jnp.cumsum(dB_u * c, axis=1) / (c + 1e-06)
            y = jnp.einsum('bldn,bln->bld', x, C)
            return y + u * D

        def mamba(x, in_w, conv_w, conv_b, xproj_w, dproj_w, dproj_b, A_log, Dp, out_w):
            x1, res = jnp.split(x @ in_w.T, 2, axis=-1)
            xc = jnp.transpose(x1, (0, 2, 1))
            xc = jnp.pad(xc, ((0, 0), (0, 0), (K - 1, 0)))
            xc = jax.lax.conv_general_dilated(xc, conv_w, (1,), 'VALID', dimension_numbers=('NCH', 'OIH', 'NCH'), feature_group_count=D_INT) + conv_b[None, :, None]
            x1 = jax.nn.silu(jnp.transpose(xc, (0, 2, 1)))
            A = -jnp.exp(jnp.clip(A_log, -5.0, 5.0))
            x_dbl = x1 @ xproj_w.T
            delta = jax.nn.softplus(x_dbl[..., :DTR] @ dproj_w.T + dproj_b)
            B = x_dbl[..., DTR:DTR + N]
            C = x_dbl[..., DTR + N:]
            y = selective_scan(x1, delta, A, B, C, Dp)
            return y * jax.nn.silu(res) @ out_w.T

        def bn_eval(x, gamma, beta, mean, var):
            inv = gamma / jnp.sqrt(var + BN_EPS)
            return x * inv[None, :, None, None] + (beta - mean * inv)[None, :, None, None]

        def _mamba_params(key):
            ks = jax.random.split(key, 5)
            in_w = jax.random.normal(ks[0], (2 * D_INT, D_IN)) * 0.05
            conv_w = jax.random.normal(ks[1], (D_INT, 1, K)) * 0.2
            conv_b = jnp.zeros((D_INT,), jnp.float32)
            xproj_w = jax.random.normal(ks[2], (DTR + 2 * N, D_INT)) * 0.05
            dproj_w = jax.random.normal(ks[3], (D_INT, DTR)) * 0.1
            dproj_b = jnp.zeros((D_INT,), jnp.float32)
            A_vals = jnp.arange(1, N + 1, dtype=jnp.float32) / N * 3.0
            A_log = jnp.log(jnp.broadcast_to(A_vals, (D_INT, N)))
            Dp = jnp.ones((D_INT,), jnp.float32)
            out_w = jax.random.normal(ks[4], (D_IN, D_INT)) * 0.05
            return (in_w, conv_w, conv_b, xproj_w, dproj_w, dproj_b, A_log, Dp, out_w)
        key = jax.random.key(seed)
        ks = jax.random.split(key, 8)
        C_IO = 64
        x = jax.random.normal(ks[0], (2, C_IO, 56, 56), jnp.float32)
        hm = _mamba_params(ks[1])
        wm = _mamba_params(ks[2])
        inp = {'x': x, 'hd_w': jax.random.normal(ks[3], (D_IN, C_IO)) * 0.1, 'hu_w': jax.random.normal(ks[4], (C_IO, D_IN)) * 0.1, 'wd_w': jax.random.normal(ks[5], (D_IN, C_IO)) * 0.1, 'wu_w': jax.random.normal(ks[6], (C_IO, D_IN)) * 0.1, 'hn_gamma': jnp.ones((C_IO,)), 'hn_beta': jnp.zeros((C_IO,)), 'hn_mean': jnp.zeros((C_IO,)), 'hn_var': jnp.ones((C_IO,)), 'wn_gamma': jnp.ones((C_IO,)), 'wn_beta': jnp.zeros((C_IO,)), 'wn_mean': jnp.zeros((C_IO,)), 'wn_var': jnp.ones((C_IO,))}
        names = ['in_w', 'conv_w', 'conv_b', 'xproj_w', 'dproj_w', 'dproj_b', 'A_log', 'D', 'out_w']
        for n, v in zip(names, hm):
            inp['hm_' + n] = v
        for n, v in zip(names, wm):
            inp['wm_' + n] = v
        return inp
    _L1_conv_all = _L1_conv_setup()
    _L1_conv_in = {k: v for k, v in _L1_conv_all.items() if k in ('hd_w', 'hm_in_w', 'hm_conv_w', 'hm_conv_b', 'hm_xproj_w', 'hm_dproj_w', 'hm_dproj_b', 'hm_A_log', 'hm_D', 'hm_out_w', 'hu_w', 'hn_gamma', 'hn_beta', 'hn_mean', 'hn_var', 'wd_w', 'wm_in_w', 'wm_conv_w', 'wm_conv_b', 'wm_xproj_w', 'wm_dproj_w', 'wm_dproj_b', 'wm_A_log', 'wm_D', 'wm_out_w', 'wu_w', 'wn_gamma', 'wn_beta', 'wn_mean', 'wn_var', )}
    del _L1_conv_all

    def _L2_conv_setup():
        import jax, jax.numpy as jnp
        import numpy as np
        K = 3
        PAD = K // 2
        CENTER = K * K // 2

        def _conv(x, w, b, pad):
            y = jax.lax.conv_general_dilated(x, w, window_strides=(1, 1), padding=[(pad, pad), (pad, pad)], dimension_numbers=('NCHW', 'OIHW', 'NCHW'))
            return y + b[None, :, None, None]
        key = jax.random.key(seed)
        k1, k2, k3 = jax.random.split(key, 3)
        B, C, H, W = (8, 64, 128, 128)
        x = jax.random.normal(k1, (B, C, H, W), dtype=jnp.float32)
        w1 = jax.random.normal(k2, (C // 2, C, 3, 3), dtype=jnp.float32) * 0.05
        b1 = jnp.zeros((C // 2,), dtype=jnp.float32)
        w2 = jax.random.normal(k3, (K * K, C // 2, 1, 1), dtype=jnp.float32) * 0.05
        b2 = jnp.zeros((K * K,), dtype=jnp.float32)
        return {'x': x, 'w1': w1, 'b1': b1, 'w2': w2, 'b2': b2}
    _L2_conv_all = _L2_conv_setup()
    _L2_conv_in = {k: v for k, v in _L2_conv_all.items() if k in ('w1', 'b1', 'w2', 'b2', )}
    del _L2_conv_all

    def _L3_conv_setup():
        import jax, jax.numpy as jnp
        import numpy as np
        D_STATE = 16
        D_CONV = 4
        EXPAND = 2
        LN_EPS = 1e-05

        def _mamba(u, in_proj_w, conv_w, conv_b, x_proj_w, dt_proj_w, dt_proj_b, A_log, D):
            L = u.shape[0]
            d_inner = conv_w.shape[0]
            dt_rank = dt_proj_w.shape[1]
            xz = u @ in_proj_w.T
            xh, z = (xz[:, :d_inner], xz[:, d_inner:])
            xp = jnp.pad(xh, ((D_CONV - 1, 0), (0, 0)))
            conv = conv_b
            for k in range(D_CONV):
                conv = conv + xp[k:k + L] * conv_w[:, k]
            xc = jax.nn.silu(conv)
            dbc = xc @ x_proj_w.T
            dt = dbc[:, :dt_rank]
            Bm = dbc[:, dt_rank:dt_rank + D_STATE]
            Cm = dbc[:, dt_rank + D_STATE:]
            delta = jax.nn.softplus(dt @ dt_proj_w.T + dt_proj_b)
            A = -jnp.exp(A_log)

            def step(h, t):
                d, b, c, xt = t
                h = h * jnp.exp(d[:, None] * A) + (d * xt)[:, None] * b[None, :]
                return (h, h @ c)
            h0 = jnp.zeros((d_inner, D_STATE), dtype=u.dtype)
            _, ys = jax.lax.scan(step, h0, (delta, Bm, Cm, xc))
            y = ys + xc * D
            y = y * jax.nn.silu(z)
            return y @ jnp.swapaxes(in_proj_w, 0, 1)[:0, :0].reshape(0, 0) if False else y
        key = jax.random.key(seed)
        B, C, H, W = (4, 64, 128, 128)
        d_inner = EXPAND * C
        dt_rank = (C + 15) // 16
        ks = jax.random.split(key, 12)
        g = lambda k, shape, s=0.02: jax.random.normal(k, shape, jnp.float32) * s
        A_init = jnp.broadcast_to(jnp.arange(1, D_STATE + 1, dtype=jnp.float32), (d_inner, D_STATE))
        return {'x': jax.random.normal(ks[0], (B, C, H, W), jnp.float32), 'in_proj_w': g(ks[1], (2 * d_inner, C)), 'conv_w': g(ks[2], (d_inner, D_CONV), 0.1), 'conv_b': g(ks[3], (d_inner,), 0.1), 'x_proj_w': g(ks[4], (dt_rank + 2 * D_STATE, d_inner)), 'dt_proj_w': g(ks[5], (d_inner, dt_rank), 0.1), 'dt_proj_b': g(ks[6], (d_inner,), 0.1), 'A_log': jnp.log(A_init), 'D': jnp.ones((d_inner,), jnp.float32), 'out_proj_w': g(ks[7], (C, d_inner)), 'proj_w': g(ks[8], (C, C)), 'proj_b': jnp.zeros((C,), jnp.float32), 'ln_g': jnp.ones((C,), jnp.float32), 'ln_b': jnp.zeros((C,), jnp.float32)}
    _L3_conv_all = _L3_conv_setup()
    _L3_conv_in = {k: v for k, v in _L3_conv_all.items() if k in ('in_proj_w', 'conv_w', 'conv_b', 'x_proj_w', 'dt_proj_w', 'dt_proj_b', 'A_log', 'D', 'out_proj_w', 'proj_w', 'proj_b', 'ln_g', 'ln_b', )}
    del _L3_conv_all

    return {
        "x": x,
        "L0_conv_dwh_w": _L0_conv_in["dwh_w"],
        "L0_conv_dwh_b": _L0_conv_in["dwh_b"],
        "L0_conv_dww_w": _L0_conv_in["dww_w"],
        "L0_conv_dww_b": _L0_conv_in["dww_b"],
        "L0_conv_conv_w": _L0_conv_in["conv_w"],
        "L0_conv_conv_b": _L0_conv_in["conv_b"],
        "L0_conv_bn_g": _L0_conv_in["bn_g"],
        "L0_conv_bn_b": _L0_conv_in["bn_b"],
        "L0_conv_bn_m": _L0_conv_in["bn_m"],
        "L0_conv_bn_v": _L0_conv_in["bn_v"],
        "L0_conv_ln_g": _L0_conv_in["ln_g"],
        "L0_conv_ln_b": _L0_conv_in["ln_b"],
        "L0_conv_in_proj_w": _L0_conv_in["in_proj_w"],
        "L0_conv_convd_w": _L0_conv_in["convd_w"],
        "L0_conv_convd_b": _L0_conv_in["convd_b"],
        "L0_conv_x_proj_w": _L0_conv_in["x_proj_w"],
        "L0_conv_dt_proj_w": _L0_conv_in["dt_proj_w"],
        "L0_conv_dt_proj_b": _L0_conv_in["dt_proj_b"],
        "L0_conv_A_log": _L0_conv_in["A_log"],
        "L0_conv_Dp": _L0_conv_in["Dp"],
        "L0_conv_out_proj_w": _L0_conv_in["out_proj_w"],
        "L1_conv_hd_w": _L1_conv_in["hd_w"],
        "L1_conv_hm_in_w": _L1_conv_in["hm_in_w"],
        "L1_conv_hm_conv_w": _L1_conv_in["hm_conv_w"],
        "L1_conv_hm_conv_b": _L1_conv_in["hm_conv_b"],
        "L1_conv_hm_xproj_w": _L1_conv_in["hm_xproj_w"],
        "L1_conv_hm_dproj_w": _L1_conv_in["hm_dproj_w"],
        "L1_conv_hm_dproj_b": _L1_conv_in["hm_dproj_b"],
        "L1_conv_hm_A_log": _L1_conv_in["hm_A_log"],
        "L1_conv_hm_D": _L1_conv_in["hm_D"],
        "L1_conv_hm_out_w": _L1_conv_in["hm_out_w"],
        "L1_conv_hu_w": _L1_conv_in["hu_w"],
        "L1_conv_hn_gamma": _L1_conv_in["hn_gamma"],
        "L1_conv_hn_beta": _L1_conv_in["hn_beta"],
        "L1_conv_hn_mean": _L1_conv_in["hn_mean"],
        "L1_conv_hn_var": _L1_conv_in["hn_var"],
        "L1_conv_wd_w": _L1_conv_in["wd_w"],
        "L1_conv_wm_in_w": _L1_conv_in["wm_in_w"],
        "L1_conv_wm_conv_w": _L1_conv_in["wm_conv_w"],
        "L1_conv_wm_conv_b": _L1_conv_in["wm_conv_b"],
        "L1_conv_wm_xproj_w": _L1_conv_in["wm_xproj_w"],
        "L1_conv_wm_dproj_w": _L1_conv_in["wm_dproj_w"],
        "L1_conv_wm_dproj_b": _L1_conv_in["wm_dproj_b"],
        "L1_conv_wm_A_log": _L1_conv_in["wm_A_log"],
        "L1_conv_wm_D": _L1_conv_in["wm_D"],
        "L1_conv_wm_out_w": _L1_conv_in["wm_out_w"],
        "L1_conv_wu_w": _L1_conv_in["wu_w"],
        "L1_conv_wn_gamma": _L1_conv_in["wn_gamma"],
        "L1_conv_wn_beta": _L1_conv_in["wn_beta"],
        "L1_conv_wn_mean": _L1_conv_in["wn_mean"],
        "L1_conv_wn_var": _L1_conv_in["wn_var"],
        "L2_conv_w1": _L2_conv_in["w1"],
        "L2_conv_b1": _L2_conv_in["b1"],
        "L2_conv_w2": _L2_conv_in["w2"],
        "L2_conv_b2": _L2_conv_in["b2"],
        "L3_conv_in_proj_w": _L3_conv_in["in_proj_w"],
        "L3_conv_conv_w": _L3_conv_in["conv_w"],
        "L3_conv_conv_b": _L3_conv_in["conv_b"],
        "L3_conv_x_proj_w": _L3_conv_in["x_proj_w"],
        "L3_conv_dt_proj_w": _L3_conv_in["dt_proj_w"],
        "L3_conv_dt_proj_b": _L3_conv_in["dt_proj_b"],
        "L3_conv_A_log": _L3_conv_in["A_log"],
        "L3_conv_D": _L3_conv_in["D"],
        "L3_conv_out_proj_w": _L3_conv_in["out_proj_w"],
        "L3_conv_proj_w": _L3_conv_in["proj_w"],
        "L3_conv_proj_b": _L3_conv_in["proj_b"],
        "L3_conv_ln_g": _L3_conv_in["ln_g"],
        "L3_conv_ln_b": _L3_conv_in["ln_b"],
    }

def reference(x, L0_conv_dwh_w, L0_conv_dwh_b, L0_conv_dww_w, L0_conv_dww_b, L0_conv_conv_w, L0_conv_conv_b, L0_conv_bn_g, L0_conv_bn_b, L0_conv_bn_m, L0_conv_bn_v, L0_conv_ln_g, L0_conv_ln_b, L0_conv_in_proj_w, L0_conv_convd_w, L0_conv_convd_b, L0_conv_x_proj_w, L0_conv_dt_proj_w, L0_conv_dt_proj_b, L0_conv_A_log, L0_conv_Dp, L0_conv_out_proj_w, L1_conv_hd_w, L1_conv_hm_in_w, L1_conv_hm_conv_w, L1_conv_hm_conv_b, L1_conv_hm_xproj_w, L1_conv_hm_dproj_w, L1_conv_hm_dproj_b, L1_conv_hm_A_log, L1_conv_hm_D, L1_conv_hm_out_w, L1_conv_hu_w, L1_conv_hn_gamma, L1_conv_hn_beta, L1_conv_hn_mean, L1_conv_hn_var, L1_conv_wd_w, L1_conv_wm_in_w, L1_conv_wm_conv_w, L1_conv_wm_conv_b, L1_conv_wm_xproj_w, L1_conv_wm_dproj_w, L1_conv_wm_dproj_b, L1_conv_wm_A_log, L1_conv_wm_D, L1_conv_wm_out_w, L1_conv_wu_w, L1_conv_wn_gamma, L1_conv_wn_beta, L1_conv_wn_mean, L1_conv_wn_var, L2_conv_w1, L2_conv_b1, L2_conv_w2, L2_conv_b2, L3_conv_in_proj_w, L3_conv_conv_w, L3_conv_conv_b, L3_conv_x_proj_w, L3_conv_dt_proj_w, L3_conv_dt_proj_b, L3_conv_A_log, L3_conv_D, L3_conv_out_proj_w, L3_conv_proj_w, L3_conv_proj_b, L3_conv_ln_g, L3_conv_ln_b):
    import jax
    import jax.numpy as jnp
    def _L0_conv_ref(x, dwh_w, dwh_b, dww_w, dww_b, conv_w, conv_b, bn_g, bn_b, bn_m, bn_v, ln_g, ln_b, in_proj_w, convd_w, convd_b, x_proj_w, dt_proj_w, dt_proj_b, A_log, Dp, out_proj_w):
        import jax, jax.numpy as jnp
        import numpy as np
        from jax import lax
        C = 64
        D_INNER = 128
        D_STATE = 16
        D_CONV = 4
        DT_RANK = 4
        B, H, W = (4, 64, 64)

        def _mamba(h, in_proj_w, convd_w, convd_b, x_proj_w, dt_proj_w, dt_proj_b, A_log, Dp, out_proj_w):
            Bt, L, _ = h.shape
            xz = jnp.einsum('blc,dc->bld', h, in_proj_w)
            xm, z = jnp.split(xz, 2, axis=-1)
            xc = lax.conv_general_dilated(xm.transpose(0, 2, 1), convd_w, (1,), [(D_CONV - 1, 0)], feature_group_count=D_INNER, dimension_numbers=('NCH', 'OIH', 'NCH'))
            xc = jax.nn.silu(xc + convd_b[None, :, None]).transpose(0, 2, 1)
            dbc = jnp.einsum('bld,ed->ble', xc, x_proj_w)
            dt, Bm, Cm = jnp.split(dbc, [DT_RANK, DT_RANK + D_STATE], axis=-1)
            dt = jax.nn.softplus(jnp.einsum('blr,dr->bld', dt, dt_proj_w) + dt_proj_b)
            A = -jnp.exp(A_log)
            dA = jnp.exp(dt[..., None] * A)
            dBx = dt[..., None] * Bm[:, :, None, :] * xc[..., None]

            def step(hc, inp):
                dA_t, dBx_t, C_t = inp
                hc = hc * dA_t + dBx_t
                y = jnp.einsum('bds,bs->bd', hc, C_t)
                return (hc, y)
            h0 = jnp.zeros((Bt, D_INNER, D_STATE), h.dtype)
            _, ys = lax.scan(step, h0, (dA.transpose(1, 0, 2, 3), dBx.transpose(1, 0, 2, 3), Cm.transpose(1, 0, 2)))
            ys = ys.transpose(1, 0, 2)
            ys = (ys + xc * Dp) * jax.nn.silu(z)
            return jnp.einsum('bld,cd->blc', ys, out_proj_w)

        def _forward(x, dwh_w, dwh_b, dww_w, dww_b, conv_w, conv_b, bn_g, bn_b, bn_m, bn_v, ln_g, ln_b, in_proj_w, convd_w, convd_b, x_proj_w, dt_proj_w, dt_proj_b, A_log, Dp, out_proj_w):
            dn = ('NCHW', 'OIHW', 'NCHW')
            xh = lax.conv_general_dilated(x, dwh_w, (1, 1), 'SAME', feature_group_count=C, dimension_numbers=dn)
            xw = lax.conv_general_dilated(x, dww_w, (1, 1), 'SAME', feature_group_count=C, dimension_numbers=dn)
            x = x + xh + dwh_b[None, :, None, None] + xw + dww_b[None, :, None, None]
            x = lax.conv_general_dilated(x, conv_w, (1, 1), 'SAME', dimension_numbers=dn) + conv_b[None, :, None, None]
            x = (x - bn_m[None, :, None, None]) * lax.rsqrt(bn_v + 1e-05)[None, :, None, None] * bn_g[None, :, None, None] + bn_b[None, :, None, None]
            x = jax.nn.relu(x)
            Bt, Cc, Hh, Ww = x.shape
            seq = x.reshape(Bt, Cc, Hh * Ww).transpose(0, 2, 1)
            mu = seq.mean(-1, keepdims=True)
            var = ((seq - mu) ** 2).mean(-1, keepdims=True)
            hn = (seq - mu) * lax.rsqrt(var + 1e-05) * ln_g + ln_b
            y = _mamba(hn, in_proj_w, convd_w, convd_b, x_proj_w, dt_proj_w, dt_proj_b, A_log, Dp, out_proj_w)
            out = (y + seq).transpose(0, 2, 1).reshape(Bt, Cc, Hh, Ww)
            return out
        return _forward(x, dwh_w, dwh_b, dww_w, dww_b, conv_w, conv_b, bn_g, bn_b, bn_m, bn_v, ln_g, ln_b, in_proj_w, convd_w, convd_b, x_proj_w, dt_proj_w, dt_proj_b, A_log, Dp, out_proj_w)

    def _L1_conv_ref(x, hd_w, hm_in_w, hm_conv_w, hm_conv_b, hm_xproj_w, hm_dproj_w, hm_dproj_b, hm_A_log, hm_D, hm_out_w, hu_w, hn_gamma, hn_beta, hn_mean, hn_var, wd_w, wm_in_w, wm_conv_w, wm_conv_b, wm_xproj_w, wm_dproj_w, wm_dproj_b, wm_A_log, wm_D, wm_out_w, wu_w, wn_gamma, wn_beta, wn_mean, wn_var):
        import jax, jax.numpy as jnp
        import numpy as np
        D_IN = 96
        D_INT = 192
        N = 96
        DTR = 6
        K = 4
        BN_EPS = 1e-05

        def selective_scan(u, delta, A, B, C, D):
            A = jnp.clip(A, -5.0, 5.0)
            dA = jnp.einsum('bld,dn->bldn', delta, A)
            dB_u = jnp.einsum('bld,bld,bln->bldn', delta, u, B)
            c = jnp.concatenate([dA[:, 1:], jnp.zeros_like(dA[:, :1])], axis=1)
            c = jnp.flip(c, axis=1)
            c = jnp.cumsum(c, axis=1)
            c = jnp.exp(jnp.minimum(c, 15.0))
            c = jnp.flip(c, axis=1)
            x = jnp.cumsum(dB_u * c, axis=1) / (c + 1e-06)
            y = jnp.einsum('bldn,bln->bld', x, C)
            return y + u * D

        def mamba(x, in_w, conv_w, conv_b, xproj_w, dproj_w, dproj_b, A_log, Dp, out_w):
            x1, res = jnp.split(x @ in_w.T, 2, axis=-1)
            xc = jnp.transpose(x1, (0, 2, 1))
            xc = jnp.pad(xc, ((0, 0), (0, 0), (K - 1, 0)))
            xc = jax.lax.conv_general_dilated(xc, conv_w, (1,), 'VALID', dimension_numbers=('NCH', 'OIH', 'NCH'), feature_group_count=D_INT) + conv_b[None, :, None]
            x1 = jax.nn.silu(jnp.transpose(xc, (0, 2, 1)))
            A = -jnp.exp(jnp.clip(A_log, -5.0, 5.0))
            x_dbl = x1 @ xproj_w.T
            delta = jax.nn.softplus(x_dbl[..., :DTR] @ dproj_w.T + dproj_b)
            B = x_dbl[..., DTR:DTR + N]
            C = x_dbl[..., DTR + N:]
            y = selective_scan(x1, delta, A, B, C, Dp)
            return y * jax.nn.silu(res) @ out_w.T

        def bn_eval(x, gamma, beta, mean, var):
            inv = gamma / jnp.sqrt(var + BN_EPS)
            return x * inv[None, :, None, None] + (beta - mean * inv)[None, :, None, None]

        def _mamba_params(key):
            ks = jax.random.split(key, 5)
            in_w = jax.random.normal(ks[0], (2 * D_INT, D_IN)) * 0.05
            conv_w = jax.random.normal(ks[1], (D_INT, 1, K)) * 0.2
            conv_b = jnp.zeros((D_INT,), jnp.float32)
            xproj_w = jax.random.normal(ks[2], (DTR + 2 * N, D_INT)) * 0.05
            dproj_w = jax.random.normal(ks[3], (D_INT, DTR)) * 0.1
            dproj_b = jnp.zeros((D_INT,), jnp.float32)
            A_vals = jnp.arange(1, N + 1, dtype=jnp.float32) / N * 3.0
            A_log = jnp.log(jnp.broadcast_to(A_vals, (D_INT, N)))
            Dp = jnp.ones((D_INT,), jnp.float32)
            out_w = jax.random.normal(ks[4], (D_IN, D_INT)) * 0.05
            return (in_w, conv_w, conv_b, xproj_w, dproj_w, dproj_b, A_log, Dp, out_w)
        b, c, h, w = x.shape
        hp = jnp.einsum('bchw,dc->bdhw', x, hd_w)
        hs = jnp.transpose(hp, (0, 3, 2, 1)).reshape(b * w, h, D_IN)
        hs = mamba(hs, hm_in_w, hm_conv_w, hm_conv_b, hm_xproj_w, hm_dproj_w, hm_dproj_b, hm_A_log, hm_D, hm_out_w)
        hmx = jnp.transpose(hs.reshape(b, w, h, D_IN), (0, 3, 2, 1))
        h_out = bn_eval(jnp.einsum('bdhw,od->bohw', hmx, hu_w), hn_gamma, hn_beta, hn_mean, hn_var)
        wp = jnp.einsum('bchw,dc->bdhw', x, wd_w)
        ws = jnp.transpose(wp, (0, 2, 3, 1)).reshape(b * h, w, D_IN)
        ws = mamba(ws, wm_in_w, wm_conv_w, wm_conv_b, wm_xproj_w, wm_dproj_w, wm_dproj_b, wm_A_log, wm_D, wm_out_w)
        wmx = jnp.transpose(ws.reshape(b, h, w, D_IN), (0, 3, 1, 2))
        w_out = bn_eval(jnp.einsum('bdhw,od->bohw', wmx, wu_w), wn_gamma, wn_beta, wn_mean, wn_var)
        return h_out + w_out + x

    def _L2_conv_ref(x, w1, b1, w2, b2):
        import jax, jax.numpy as jnp
        import numpy as np
        K = 3
        PAD = K // 2
        CENTER = K * K // 2

        def _conv(x, w, b, pad):
            y = jax.lax.conv_general_dilated(x, w, window_strides=(1, 1), padding=[(pad, pad), (pad, pad)], dimension_numbers=('NCHW', 'OIHW', 'NCHW'))
            return y + b[None, :, None, None]
        B, C, H, W = x.shape
        h = _conv(x, w1, b1, pad=1)
        h = jnp.where(h >= 0, h, 0.2 * h)
        w_lp = jax.nn.softmax(_conv(h, w2, b2, pad=0), axis=1)
        delta = jnp.zeros_like(w_lp).at[:, CENTER].set(1.0)
        w_hp = delta - w_lp
        xp = jnp.pad(x, ((0, 0), (0, 0), (PAD, PAD), (PAD, PAD)))
        high = jnp.zeros_like(x)
        for i in range(K):
            for j in range(K):
                k = i * K + j
                high = high + xp[:, :, i:i + H, j:j + W] * w_hp[:, k:k + 1]
        return x + high

    def _L3_conv_ref(x, in_proj_w, conv_w, conv_b, x_proj_w, dt_proj_w, dt_proj_b, A_log, D, out_proj_w, proj_w, proj_b, ln_g, ln_b):
        import jax, jax.numpy as jnp
        import numpy as np
        D_STATE = 16
        D_CONV = 4
        EXPAND = 2
        LN_EPS = 1e-05

        def _mamba(u, in_proj_w, conv_w, conv_b, x_proj_w, dt_proj_w, dt_proj_b, A_log, D):
            L = u.shape[0]
            d_inner = conv_w.shape[0]
            dt_rank = dt_proj_w.shape[1]
            xz = u @ in_proj_w.T
            xh, z = (xz[:, :d_inner], xz[:, d_inner:])
            xp = jnp.pad(xh, ((D_CONV - 1, 0), (0, 0)))
            conv = conv_b
            for k in range(D_CONV):
                conv = conv + xp[k:k + L] * conv_w[:, k]
            xc = jax.nn.silu(conv)
            dbc = xc @ x_proj_w.T
            dt = dbc[:, :dt_rank]
            Bm = dbc[:, dt_rank:dt_rank + D_STATE]
            Cm = dbc[:, dt_rank + D_STATE:]
            delta = jax.nn.softplus(dt @ dt_proj_w.T + dt_proj_b)
            A = -jnp.exp(A_log)

            def step(h, t):
                d, b, c, xt = t
                h = h * jnp.exp(d[:, None] * A) + (d * xt)[:, None] * b[None, :]
                return (h, h @ c)
            h0 = jnp.zeros((d_inner, D_STATE), dtype=u.dtype)
            _, ys = jax.lax.scan(step, h0, (delta, Bm, Cm, xc))
            y = ys + xc * D
            y = y * jax.nn.silu(z)
            return y @ jnp.swapaxes(in_proj_w, 0, 1)[:0, :0].reshape(0, 0) if False else y
        B, C, H, W = x.shape
        u = jnp.transpose(x, (0, 2, 3, 1)).reshape(-1, C)
        y = _mamba(u, in_proj_w, conv_w, conv_b, x_proj_w, dt_proj_w, dt_proj_b, A_log, D)
        y = y @ out_proj_w.T
        p = y @ proj_w.T + proj_b
        mu = jnp.mean(p, axis=-1, keepdims=True)
        var = jnp.mean(jnp.square(p - mu), axis=-1, keepdims=True)
        p = (p - mu) * jax.lax.rsqrt(var + LN_EPS) * ln_g + ln_b
        p = jax.nn.silu(p)
        out = jnp.transpose(p.reshape(B, H, W, C), (0, 3, 1, 2))
        return out + x

    def _gn(v, G=32, eps=1e-5):
        B_, C_, H_, W_ = v.shape
        g = v.reshape(B_, G, C_ // G, H_, W_)
        m = jnp.mean(g, axis=(2, 3, 4), keepdims=True)
        s = jnp.var(g, axis=(2, 3, 4), keepdims=True)
        return ((g - m) / jnp.sqrt(s + eps)).reshape(v.shape)

    def _ln_c(v, eps=1e-6):
        m = jnp.mean(v, axis=1, keepdims=True)
        s = jnp.var(v, axis=1, keepdims=True)
        return (v - m) / jnp.sqrt(s + eps)

    def _ln_t(v, eps=1e-5):
        m = jnp.mean(v, axis=-1, keepdims=True)
        s = jnp.var(v, axis=-1, keepdims=True)
        return (v - m) / jnp.sqrt(s + eps)

    def _to_tokens(v):
        B_, C_, H_, W_ = v.shape
        return v.reshape(B_, C_, H_ * W_).transpose(0, 2, 1)
    def _from_tokens(t, like):
        B_, C_, H_, W_ = like.shape
        return t.transpose(0, 2, 1).reshape(B_, C_, H_, W_)

    x = _L0_conv_ref(x, L0_conv_dwh_w, L0_conv_dwh_b, L0_conv_dww_w, L0_conv_dww_b, L0_conv_conv_w, L0_conv_conv_b, L0_conv_bn_g, L0_conv_bn_b, L0_conv_bn_m, L0_conv_bn_v, L0_conv_ln_g, L0_conv_ln_b, L0_conv_in_proj_w, L0_conv_convd_w, L0_conv_convd_b, L0_conv_x_proj_w, L0_conv_dt_proj_w, L0_conv_dt_proj_b, L0_conv_A_log, L0_conv_Dp, L0_conv_out_proj_w)
    x = _L1_conv_ref(x, L1_conv_hd_w, L1_conv_hm_in_w, L1_conv_hm_conv_w, L1_conv_hm_conv_b, L1_conv_hm_xproj_w, L1_conv_hm_dproj_w, L1_conv_hm_dproj_b, L1_conv_hm_A_log, L1_conv_hm_D, L1_conv_hm_out_w, L1_conv_hu_w, L1_conv_hn_gamma, L1_conv_hn_beta, L1_conv_hn_mean, L1_conv_hn_var, L1_conv_wd_w, L1_conv_wm_in_w, L1_conv_wm_conv_w, L1_conv_wm_conv_b, L1_conv_wm_xproj_w, L1_conv_wm_dproj_w, L1_conv_wm_dproj_b, L1_conv_wm_A_log, L1_conv_wm_D, L1_conv_wm_out_w, L1_conv_wu_w, L1_conv_wn_gamma, L1_conv_wn_beta, L1_conv_wn_mean, L1_conv_wn_var)
    x = _L2_conv_ref(x, L2_conv_w1, L2_conv_b1, L2_conv_w2, L2_conv_b2)
    x = _L3_conv_ref(x, L3_conv_in_proj_w, L3_conv_conv_w, L3_conv_conv_b, L3_conv_x_proj_w, L3_conv_dt_proj_w, L3_conv_dt_proj_b, L3_conv_A_log, L3_conv_D, L3_conv_out_proj_w, L3_conv_proj_w, L3_conv_proj_b, L3_conv_ln_g, L3_conv_ln_b)
    return x


_drawn_inputs = setup_inputs


def setup_inputs(seed=0):
    import zlib

    import numpy as np

    out = dict(_drawn_inputs(seed))
    spreads = {'L0_conv_bn_g': (1.0, 0.2),
     'L0_conv_bn_b': (0.0, 0.1),
     'L0_conv_ln_g': (1.0, 0.2),
     'L0_conv_ln_b': (0.0, 0.1),
     'L0_conv_Dp': (1.0, 0.2),
     'L1_conv_hm_conv_b': (0.0, 0.1),
     'L1_conv_hm_dproj_b': (0.0, 0.1),
     'L1_conv_hm_D': (1.0, 0.2),
     'L1_conv_hn_gamma': (1.0, 0.2),
     'L1_conv_hn_beta': (0.0, 0.1),
     'L1_conv_hn_mean': (0.0, 0.1),
     'L1_conv_hn_var': (1.0, 0.2),
     'L1_conv_wm_conv_b': (0.0, 0.1),
     'L1_conv_wm_dproj_b': (0.0, 0.1),
     'L1_conv_wm_D': (1.0, 0.2),
     'L1_conv_wn_gamma': (1.0, 0.2),
     'L1_conv_wn_beta': (0.0, 0.1),
     'L1_conv_wn_mean': (0.0, 0.1),
     'L1_conv_wn_var': (1.0, 0.2),
     'L2_conv_b1': (0.0, 0.1),
     'L2_conv_b2': (0.0, 0.1),
     'L3_conv_D': (1.0, 0.2),
     'L3_conv_proj_b': (0.0, 0.1),
     'L3_conv_ln_g': (1.0, 0.2),
     'L3_conv_ln_b': (0.0, 0.1)}
    factors = {}
    for name, (base, spread) in spreads.items():
        noise = np.random.default_rng([zlib.crc32(name.encode()), seed]).standard_normal(out[name].shape)
        drawn = base * np.exp(spread * noise) if base else spread * noise
        out[name] = jnp.asarray(drawn.astype(out[name].dtype))
    for name, factor in factors.items():
        out[name] = (out[name] * factor).astype(out[name].dtype)
    return out
```

```python
from contextlib import ExitStack

import numpy as np
import concourse.bass as bass
from concourse import mybir

F32 = mybir.dt.float32
ALU = mybir.AluOpType
ACT = mybir.ActivationFunctionType
AX_X = mybir.AxisListType.X

B, C, H, W = 4, 64, 64, 64
L = H * W
NT = B * L
TOK = 512
ROWS = TOK // W
TPB = L // TOK
TILES = NT // TOK
HT = TILES // 2
HIST = 3
SLOT = HIST + TOK
PADR = 2 * H + 3
PADW = W + 2

D = 128
NS = 16
RANK = 4

DX = 192
NX = 96
RX = 6
EX = 96
JB = DX // 64
G16 = NX // 16
SEQ = 64
NSEQ = TOK // SEQ
RESET = 1.0e5
HALF_LOG = 0.5 * float(np.log(1.0e6))


def image_row(b2, rb):
    return b2 * (H + 1) + rb * ROWS


def phase_conv_norm(nc, sem, ident_in, w, x, seq_s, hn_s):
    with ExitStack() as ctx:
        def sb(name, shape):
            return ctx.enter_context(nc.sbuf_tensor("a_" + name, shape, F32))

        def ps(name, shape):
            return ctx.enter_context(nc.psum_tensor("a_" + name, shape, F32))

        xp = sb("xp", [128, PADR, PADW])
        cols = sb("cols", [128, 15])
        convT = sb("convT", [128, C])
        taps = sb("taps", [128, 5])
        sumb = sb("sumb", [128, 1])
        tapw = sb("tapw", [128, 5, 128])
        plain = sb("plain", [128, 128])
        center = sb("center", [128, 128])
        mean = sb("mean", [128, 128])
        ident = sb("ident", [128, 128])
        scale = sb("scale", [128, 1])
        shift = sb("shift", [128, 1])
        eps = sb("eps", [128, 1])
        tmp = sb("tmp", [128, 2])
        seq = sb("seq", [128, TOK])
        sq = sb("sq", [128, TOK])
        rstd = sb("rstd", [128, TOK])
        hn0 = sb("hn0", [128, TOK])
        hn = sb("hn", [128, TOK])
        zero = sb("zero", [128, HIST])
        pc = ps("pc", [128, TOK])
        pm = ps("pm", [128, TOK])
        pv = ps("pv", [128, TOK])
        pb = ps("pb", [128, 512])
        DWH_B, DWW_B, CONV_B, BN_G, BN_B, BN_M, BN_V, LN_G, LN_B, TH, TW = 0, 1, 2, 3, 4, 5, 6, 7, 8, 9, 12

        s_in, s_img = sem("a_loaded"), sem("a_image_loaded")
        s_pad, s_dve = sem("a_padded"), sem("a_dve_step")
        s_bias, s_lnv = sem("a_bias"), sem("a_bn_rsqrt")
        s_conv, s_seq, s_mean, s_sq = sem("a_conv"), sem("a_seq"), sem("a_centered"), sem("a_squares")
        s_var, s_rstd, s_hn, s_out = sem("a_var"), sem("a_rstd"), sem("a_hn"), sem("a_stored")
        s_ln = sem("a_act_step")
        PREP = 12

        with nc.Block() as block:
            @block.sync
            def _(sp):
                sp.dma_start(ident[:], ident_in).then_inc(s_in, 16)
                for g in range(2):
                    sp.dma_start(cols[g * C:(g + 1) * C, :], w["L0_cols"]).then_inc(s_in, 16)
                    sp.dma_start(convT[g * C:(g + 1) * C, :], w["L0_convT"]).then_inc(s_in, 16)
                sp.wait_ge(s_pad, 1)
                for g in range(2):
                    for b2 in range(2):
                        r = 1 + b2 * (H + 1)
                        sp.dma_start(xp[g * C:(g + 1) * C, r:r + H, 1:1 + W], x[:, (2 * g + b2) * L:(2 * g + b2 + 1) * L]
                                     .rearrange("c (h w) -> c h w", w=W)).then_inc(s_img, 16)
                sp.wait_ge(s_dve, PREP)
                for t in range(0, TILES, TPB):
                    sp.dma_start(hn_s[:, t, 0:HIST], zero[0:C, :]).then_inc(s_out, 16)
                with sp.Fori(0, 2) as b2:
                    with sp.Fori(0, TPB) as rb:
                        i = b2 * TPB + rb
                        to = [sp.snap((b2 * TPB + rb + g * HT) * TOK) for g in range(2)]
                        sp.wait_ge(s_seq, i + 1)
                        for g in range(2):
                            sp.dma_start(seq_s[:, bass.ds(to[g], TOK)],
                                         seq[g * C:(g + 1) * C, :]).then_inc(s_out, 16)
                        sp.wait_ge(s_hn, i + 1)
                        for g in range(2):
                            sp.dma_start(hn_s[:, bass.ds(b2 * TPB + rb + g * HT, 1), HIST:SLOT],
                                         hn[g * C:(g + 1) * C, :].unsqueeze(1)).then_inc(s_out, 16)
                        for g in range(2):
                            sp.dma_start(hn_s[:, bass.ds(b2 * TPB + rb + g * HT + 1, 1), 0:HIST],
                                         hn[g * C:(g + 1) * C, TOK - HIST:TOK].unsqueeze(1)).then_inc(s_out, 16)
                sp.wait_ge(s_out, 16 * (B + 6 * HT))
                for t in range(0, TILES, TPB):
                    sp.dma_start(hn_s[:, t, 0:HIST], zero[0:C, :]).then_inc(s_out, 16)
                sp.wait_ge(s_out, 16 * (2 * B + 6 * HT))

            @block.vector
            def _(dve):
                k = [0]

                def step(ins):
                    k[0] += 1
                    ins.then_inc(s_dve, 1)
                    dve.wait_ge(s_dve, k[0])
                v = nc.vector
                v.memset(xp[:], 0.0).then_inc(s_pad, 1)
                v.memset(tapw[:], 0.0)
                v.memset(plain[:], 0.0)
                v.memset(mean[:], 0.0)
                v.memset(zero[:], 0.0)
                step(v.memset(eps[:], 1e-5))
                dve.wait_ge(s_in, 16 * 5)
                col = lambda n: cols[:, n:n + 1]
                step(v.tensor_tensor(taps[:, 0:1], col(TH + 1), col(TW + 1), ALU.add))
                step(v.tensor_scalar(taps[:, 0:1], taps[:, 0:1], 1.0, None, ALU.add))
                v.tensor_copy(taps[:, 1:2], col(TH))
                v.tensor_copy(taps[:, 2:3], col(TH + 2))
                v.tensor_copy(taps[:, 3:4], col(TW))
                step(v.tensor_copy(taps[:, 4:5], col(TW + 2)))
                for g in range(2):
                    q = slice(g * C, (g + 1) * C)
                    v.tensor_copy(plain[q, q], convT[q, :])
                    v.memset(mean[q, q], 1.0 / C)
                    for n in range(5):
                        last = v.tensor_scalar(tapw[q, n, q], convT[q, :], taps[q, n:n + 1], None, ALU.mult)
                step(last)
                step(v.tensor_tensor(center[:], ident[:], mean[:], ALU.subtract))
                step(v.tensor_tensor(sumb[:], col(DWH_B), col(DWW_B), ALU.add))
                step(v.tensor_tensor(tmp[:, 0:1], col(CONV_B), col(BN_M), ALU.subtract))
                dve.wait_ge(s_bias, 1)
                dve.wait_ge(s_lnv, 1)
                step(v.tensor_tensor(scale[:], tmp[:, 1:2], col(BN_G), ALU.mult))
                step(v.tensor_tensor(tmp[:, 0:1], tmp[:, 0:1], pb[:, 0:1], ALU.add))
                step(v.tensor_tensor(tmp[:, 0:1], tmp[:, 0:1], scale[:], ALU.mult))
                step(v.tensor_tensor(shift[:], tmp[:, 0:1], col(BN_B), ALU.add))
                assert k[0] == PREP, k[0]
                with dve.Fori(0, HT) as i:
                    dve.wait_ge(s_rstd, i + 1)
                    dve.wait_ge(s_out, i * 96 + 16 * B)
                    v.tensor_tensor(hn0[:], pm[:], rstd[:], ALU.mult).then_inc(s_dve, 1)
                    dve.wait_ge(s_dve, i + PREP + 1)
                    v.tensor_scalar(hn[:], hn0[:], col(LN_G), col(LN_B), ALU.mult, ALU.add).then_inc(s_hn, 1)

            @block.scalar
            def _(act):
                a = nc.scalar
                act.wait_ge(s_in, 16 * 5)
                act.wait_ge(s_dve, 1)
                a.activation(tmp[:, 1:2], cols[:, BN_V:BN_V + 1], ACT.Ln, bias=eps[:]).then_inc(s_ln, 1)
                act.wait_ge(s_ln, 1)
                a.activation(tmp[:, 1:2], tmp[:, 1:2], ACT.Exp, scale=-0.5).then_inc(s_lnv, 1)
                act.wait_ge(s_dve, PREP)
                with act.Fori(0, HT) as i:
                    act.wait_ge(s_conv, i + 1)
                    act.wait_ge(s_out, i * 96 + 16 * B)
                    a.activation(seq[:], pc[:], ACT.Relu, bias=shift[:], scale=scale[:]).then_inc(s_seq, 1)
                    act.wait_ge(s_mean, i + 1)
                    a.activation(sq[:], pm[:], ACT.Square).then_inc(s_sq, 1)
                    act.wait_ge(s_var, i + 1)
                    a.activation(rstd[:], pv[:], ACT.Ln, bias=eps[:]).then_inc(s_ln, 1)
                    act.wait_ge(s_ln, i + 2)
                    a.activation(rstd[:], rstd[:], ACT.Exp, scale=-0.5).then_inc(s_rstd, 1)

            @block.tensor
            def _(pe):
                t = nc.tensor
                pe.wait_ge(s_dve, 7)
                t.matmul(pb[:, 0:1], plain[:], sumb[:], start=True, stop=True).then_inc(s_bias, 1)
                pe.wait_ge(s_img, 16 * B)
                with pe.Fori(0, 2) as b2:
                    with pe.Fori(0, TPB) as rb:
                        i = b2 * TPB + rb
                        r = image_row(b2, rb)
                        pe.wait_ge(s_dve, i + PREP)
                        for n, (dr, dc) in enumerate([(0, 0), (-1, 0), (1, 0), (0, -1), (0, 1)]):
                            mm = t.matmul(pc[:], tapw[:, n, :], xp[:, bass.ds(r + 1 + dr, ROWS), 1 + dc:1 + dc + W],
                                          start=(n == 0), stop=(n == 4))
                        mm.then_inc(s_conv, 1)
                        pe.wait_ge(s_seq, i + 1)
                        t.matmul(pm[:], center[:], seq[:], start=True, stop=True).then_inc(s_mean, 1)
                        pe.wait_ge(s_sq, i + 1)
                        t.matmul(pv[:], mean[:], sq[:], start=True, stop=True).then_inc(s_var, 1)


def phase_mamba(nc, sem, ident_in, tag, w, u_s, res_s, out_s, reset, final):
    with ExitStack() as ctx:
        def sb(name, shape):
            return ctx.enter_context(nc.sbuf_tensor(tag + name, shape, F32))

        def ps(name, shape):
            return ctx.enter_context(nc.psum_tensor(tag + name, shape, F32))

        ident = sb("ident", [128, 128])
        inT = sb("inT", [C, 2 * D])
        cols = sb("cols", [D, 3 + NS])
        CB, DTB, DP, AL = 0, 1, 2, 3
        xpT = sb("xpT", [D, RANK + 2 * NS])
        xpr = sb("xpr", [RANK, D])
        dtT = sb("dtT", [RANK, D])
        outT = sb("outT", [D, C])
        taprow = sb("taprow", [C, 4, D])
        tapw = sb("tapw", [C, 4, D])
        gatew = sb("gatew", [C, D])
        wdt = sb("wdt", [D, D])
        wbc = sb("wbc", [D, 2 * NS, 128])
        diag_d = sb("diag_d", [D, D])
        amat = sb("amat", [D, NS])
        cbh = sb("cbh", [D, 1])
        keep = sb("keep", [D, TILES])
        eps = sb("eps", [128, 1])
        mark = sb("mark", [1, 3])
        ocols = sb("ocols", [C, 3])
        opw = sb("opw", [C, D])
        pw = sb("pw", [C, C])
        center = sb("center", [C, C])
        mean = sb("mean", [C, 128])
        pjc = sb("pjc", [C, C])
        half = sb("half", [C, 3])

        u = sb("u", [C, 2, SLOT])
        res = sb("res", [C, 2, TOK])
        th = sb("th", [D, TOK])
        tg = sb("tg", [D, TOK])
        v0 = sb("v0", [D, TOK])
        xc = sb("xc", [D, TOK])
        gate = sb("gate", [D, TOK])
        sp1 = sb("sp1", [D, TOK])
        sp2 = sb("sp2", [D, TOK])
        sp3 = sb("sp3", [D, TOK])
        dt = sb("dt", [D, TOK])
        dx = sb("dx", [D, TOK])
        av = sb("av", [D, 2, TOK])
        bv = sb("bv", [D, 2, TOK])
        cv = sb("cv", [D, 2, TOK])
        gv = sb("gv", [D, 2, TOK])
        hs = sb("hs", [D, NS, TOK])
        st = sb("st", [D, NS])
        yz = sb("yz", [D, TOK])
        n1 = sb("n1", [C, TOK])
        n2 = sb("n2", [C, TOK])
        n3 = sb("n3", [C, TOK])
        ot = sb("ot", [C, TOK])
        pf = ps("pf", [128, TOK])
        pg = ps("pg", [128, TOK])
        pb = ps("pb", [128, 2, TOK])
        pc = ps("pc", [128, 2, TOK])
        py = ps("py", [128, TOK])
        po = ps("po", [128, TOK])

        s_w, s_prep, s_wps, s_aexp = sem(tag + "weights"), sem(tag + "prep_step"), sem(tag + "weights_made"), sem(tag + "a_exp")
        s_u = [sem(tag + "input0"), sem(tag + "input1")]
        s_done, s_out = sem(tag + "tile_done"), sem(tag + "stored")
        s_xz, s_tanh, s_xc = sem(tag + "in_proj"), sem(tag + "tanh"), sem(tag + "xc")
        s_dtp, s_act, s_sp, s_dt, s_dx = (sem(tag + n) for n in ("dt_pre", "act_step", "softplus", "dt", "dx"))
        s_bb, s_cb, s_a, s_c = (sem(tag + n) for n in ("b_bcast", "c_bcast", "decay", "c_copied"))
        s_b, s_h, s_g, s_y = (sem(tag + n) for n in ("dbx", "states", "c_times_h", "y_added"))
        s_st, s_v, s_yz, s_o = (sem(tag + n) for n in ("state_kept", "conv", "gated", "out_proj"))
        s_sq, s_var, s_rs, s_pn, s_tn = (sem(tag + n) for n in ("squares", "var", "rstd", "normed", "silu_tanh"))
        NW = 8 + (3 if final else 0)

        with nc.Block() as block:
            @block.sync
            def _(sp):
                loads = [(ident, ident_in), (inT, w["inT"]), (cols, w["cols"]), (xpT, w["xpT"]), (xpr, w["xpr"]),
                         (dtT, w["dtT"]), (outT, w["outT"])]
                if final:
                    loads += [(ocols, w["ocols"]), (opw, w["opw"]), (pw, w["pw"])]
                for dst, src in loads:
                    sp.dma_start(dst[:], src).then_inc(s_w, 16)
                sp.dma_start(taprow[:], w["taps"].partition_broadcast(C)).then_inc(s_w, 16)

                def load(i, p):
                    sp.dma_start(u[:, p:p + 1, :], u_s[:, bass.ds(i, 1), :]).then_inc(s_u[p], 16)
                    sp.dma_start(res[:, p, :], res_s[:, bass.ds(i * TOK, TOK)]).then_inc(s_u[p], 16)

                def store(i):
                    sp.dma_start(out_s[:, bass.ds(i * TOK, TOK)], ot[:]).then_inc(s_out, 16)

                load(0, 0)
                with sp.Fori(0, TILES // 2 - 1) as m:
                    for i, p in ((m * 2 + 1, 1), (m * 2 + 2, 0)):
                        sp.wait_ge(s_done, i)
                        load(i, p)
                        sp.wait_ge(s_done, i + 1)
                        store(i - 1)
                sp.wait_ge(s_done, TILES - 1)
                load(TILES - 1, 1)
                sp.wait_ge(s_done, TILES)
                store(TILES - 2)
                sp.wait_ge(s_done, TILES + 1)
                store(TILES - 1)
                sp.wait_ge(s_out, 16 * (TILES + 1))

            @block.vector
            def _(dve):
                v = nc.vector
                k = [0]

                def step(ins):
                    k[0] += 1
                    ins.then_inc(s_prep, 1)
                    dve.wait_ge(s_prep, k[0])
                v.memset(st[:], 0.0)
                v.memset(keep[:], 1.0)
                step(v.memset(mean[:], 1.0 / C))
                if reset:
                    v.memset(keep[:].rearrange("p (b t) -> p b t", t=TPB)[:, :, TPB - 1], 0.0)
                step(v.memset(eps[:], 1e-5))
                dve.wait_ge(s_w, 16 * NW)
                v.tensor_scalar(gatew[:], inT[:, D:2 * D], 0.5, None, ALU.mult)
                step(v.tensor_scalar(taprow[:], taprow[:], 0.5, None, ALU.mult))
                for n in range(4):
                    v.tensor_tensor(tapw[:, n, :], inT[:, 0:D], taprow[:, n, :], ALU.mult)
                v.tensor_scalar(cbh[:], cols[:, CB:CB + 1], 0.5, None, ALU.mult)
                v.tensor_scalar(diag_d[:], ident[:], cols[:, DP:DP + 1], None, ALU.mult)
                for n in range(2 * NS):
                    v.tensor_copy(wbc[:, n, :], xpT[:, RANK + n:RANK + n + 1].broadcast_to([D, 128]))
                dve.wait_ge(s_wps, 1)
                v.tensor_copy(wdt[:], pf[:, 0:D])
                dve.wait_ge(s_aexp, 1)
                step(v.tensor_scalar(amat[:], amat[:], -1.0, None, ALU.mult))
                if final:
                    v.tensor_tensor(center[:], ident[0:C, 0:C], mean[:, 0:C], ALU.subtract).then_inc(s_wps, 1)
                    dve.wait_ge(s_wps, 3)
                    v.tensor_copy(half[:, 0:1], pc[0:C, 0, 0:1])
                    v.tensor_scalar(half[:, 1:3], ocols[:, 1:3], 0.5, None, ALU.mult)
                    v.tensor_copy(pjc[:], pg[0:C, 0:C]).then_inc(s_wps, 1)
                    dve.wait_ge(s_wps, 5)
                    step(v.tensor_copy(outT[:], pb[:, 0, 0:C]))
                step(v.memset(mark[:, 0:1], 0.0))
                v.memset(mark[:, 1:2], 0.0).then_inc(s_out, 16)
                v.memset(mark[:, 2:3], 0.0).then_inc(s_done, 1)

                with dve.Fori(0, TILES // 2) as m:
                    for p in range(2):
                        i = m * 2 + p
                        dve.wait_ge(s_tanh, 2 * i + 1)
                        v.tensor_scalar(v0[:], pf[:], cbh[:, 0:1], None, ALU.add).then_inc(s_v, 1)
                        dve.wait_ge(s_v, i + 1)
                        v.scalar_tensor_tensor(xc[:], th[:], 1.0, v0[:], ALU.add, ALU.mult).then_inc(s_xc, 1)
                        dve.wait_ge(s_tanh, 2 * i + 2)
                        v.scalar_tensor_tensor(gate[:], tg[:], 1.0, pg[:], ALU.add, ALU.mult)
                        dve.wait_ge(s_sp, i + 1)
                        v.tensor_tensor(dt[:], sp2[:], sp3[:], ALU.add).then_inc(s_dt, 1)
                        dve.wait_ge(s_dt, i + 1)
                        v.tensor_tensor(dx[:], dt[:], xc[:], ALU.mult).then_inc(s_dx, 1)
                        dve.wait_ge(s_dx, i + 1)
                        for n in range(NS):
                            un = i * NS + n
                            dve.wait_ge(s_bb, un + 1)
                            v.tensor_tensor(bv[:, n % 2, :], pb[:, n % 2, :], dx[:], ALU.mult).then_inc(s_b, 1)
                            dve.wait_ge(s_b, un + 1)
                            dve.wait_ge(s_a, un + 1)
                            v.tensor_tensor_scan(hs[:, n, :], av[:, n % 2, :], bv[:, n % 2, :], st[:, n:n + 1],
                                                 ALU.mult, ALU.add).then_inc(s_h, 1)
                        dve.wait_ge(s_h, i * NS + NS)
                        v.tensor_scalar(st[:], hs[:, :, TOK - 1], keep[:, bass.ds(i, 1)], None,
                                        ALU.mult).then_inc(s_st, 1)
                        dve.wait_ge(s_st, i + 1)
                        dve.wait_ge(s_y, i * NS + NS)
                        v.tensor_tensor(yz[:], py[:], gate[:], ALU.mult).then_inc(s_yz, 1)
                        if not final:
                            dve.wait_ge(s_o, i + 1)
                            dve.wait_ge(s_out, 16 * i + 16)
                            dve.wait_ge(s_u[p], 32 * m + 32)
                            v.tensor_tensor(ot[:], pf[0:C, :], res[:, p, :], ALU.add).then_inc(s_done, 1)
                        else:
                            dve.wait_ge(s_rs, i + 1)
                            v.tensor_tensor(n3[:], n1[:], n2[:], ALU.mult).then_inc(s_pn, 1)
                            dve.wait_ge(s_pn, 3 * i + 1)
                            v.tensor_scalar(n1[:], n3[:], half[:, 1:2], half[:, 2:3], ALU.mult,
                                            ALU.add).then_inc(s_pn, 1)
                            dve.wait_ge(s_tn, i + 1)
                            v.scalar_tensor_tensor(n3[:], n2[:], 1.0, n1[:], ALU.add, ALU.mult).then_inc(s_pn, 1)
                            dve.wait_ge(s_pn, 3 * i + 3)
                            dve.wait_ge(s_out, 16 * i + 16)
                            v.tensor_tensor(ot[:], n3[:], res[:, p, :], ALU.add).then_inc(s_done, 1)

            @block.scalar
            def _(act):
                a = nc.scalar
                act.wait_ge(s_w, 16 * NW)
                a.activation(amat[:], cols[:, AL:AL + NS], ACT.Exp).then_inc(s_aexp, 1)
                act.wait_ge(s_done, 1)
                with act.Fori(0, TILES // 2) as m:
                    for p in range(2):
                        i = m * 2 + p
                        act.wait_ge(s_xz, i + 1)
                        a.activation(th[:], pf[:], ACT.Tanh, bias=cbh[:, 0:1]).then_inc(s_tanh, 1)
                        a.activation(tg[:], pg[:], ACT.Tanh).then_inc(s_tanh, 1)
                        act.wait_ge(s_dtp, i + 1)
                        a.activation(sp1[:], po[:], ACT.Abs, bias=cols[:, DTB:DTB + 1]).then_inc(s_act, 1)
                        a.activation(sp3[:], po[:], ACT.Relu, bias=cols[:, DTB:DTB + 1])
                        act.wait_ge(s_act, 2 * i + 1)
                        a.activation(sp1[:], sp1[:], ACT.Exp, scale=-1.0).then_inc(s_act, 1)
                        act.wait_ge(s_act, 2 * i + 2)
                        a.activation(sp2[:], sp1[:], ACT.Ln, bias=1.0).then_inc(s_sp, 1)
                        act.wait_ge(s_dt, i + 1)
                        for n in range(NS):
                            un = i * NS + n
                            if n >= 2:
                                act.wait_ge(s_h, un - 1)
                            a.activation(av[:, n % 2, :], dt[:], ACT.Exp, scale=amat[:, n:n + 1]).then_inc(s_a, 1)
                            act.wait_ge(s_cb, un + 1)
                            if n >= 2:
                                act.wait_ge(s_g, un - 1)
                            a.activation(cv[:, n % 2, :], pc[:, n % 2, :], ACT.Copy).then_inc(s_c, 1)
                        if final:
                            act.wait_ge(s_o, i + 1)
                            a.activation(n1[:], pf[0:C, :], ACT.Identity, bias=half[:, 0:1])
                            a.activation(n2[:], pf[0:C, :], ACT.Square, bias=half[:, 0:1]).then_inc(s_sq, 1)
                            act.wait_ge(s_var, i + 1)
                            a.activation(n2[:], pg[0:C, :], ACT.Ln, bias=eps[0:C, :]).then_inc(s_sq, 1)
                            act.wait_ge(s_sq, 2 * i + 2)
                            a.activation(n2[:], n2[:], ACT.Exp, scale=-0.5).then_inc(s_rs, 1)
                            act.wait_ge(s_pn, 3 * i + 2)
                            a.activation(n2[:], n1[:], ACT.Tanh).then_inc(s_tn, 1)

            @block.gpsimd
            def _(pool):
                with pool.Fori(0, TILES // 2) as m:
                    for p in range(2):
                        for n in range(NS):
                            un = (m * 2 + p) * NS + n
                            pool.wait_ge(s_h, un + 1)
                            pool.wait_ge(s_c, un + 1)
                            if n >= 2:
                                pool.wait_ge(s_y, un - 1)
                            nc.gpsimd.tensor_tensor(gv[:, n % 2, :], hs[:, n, :], cv[:, n % 2, :],
                                                    ALU.mult).then_inc(s_g, 1)

            @block.tensor
            def _(pe):
                t = nc.tensor
                pe.wait_ge(s_w, 16 * NW)
                t.matmul(pf[:, 0:D], xpr[:], dtT[:], start=True, stop=True).then_inc(s_wps, 1)
                if final:
                    pe.wait_ge(s_wps, 2)
                    t.matmul(pc[0:C, 0, 0:1], center[:], ocols[:, 0:1], start=True, stop=True)
                    t.matmul(pg[0:C, 0:C], pw[:], center[:], start=True, stop=True).then_inc(s_wps, 1)
                    pe.wait_ge(s_wps, 4)
                    t.matmul(pb[:, 0, 0:C], opw[:], pjc[:], start=True, stop=True).then_inc(s_wps, 1)
                with pe.Fori(0, TILES // 2) as m:
                    for p in range(2):
                        i = m * 2 + p
                        pe.wait_ge(s_done, i + 1)
                        pe.wait_ge(s_u[p], 32 * m + 32)
                        for n in range(4):
                            t.matmul(pf[:], tapw[:, n, :], u[:, p, n:n + TOK], start=(n == 0), stop=(n == 3))
                        t.matmul(pg[:], gatew[:], u[:, p, HIST:SLOT], start=True, stop=True).then_inc(s_xz, 1)
                        pe.wait_ge(s_xc, i + 1)
                        t.matmul(po[:], wdt[:], xc[:], start=True, stop=True).then_inc(s_dtp, 1)
                        t.matmul(py[:], diag_d[:], xc[:], start=True, stop=False, skip_group_check=True)

                        def add(n, i=i):
                            pe.wait_ge(s_g, i * NS + n + 1)
                            t.matmul(py[:], ident[:], gv[:, n % 2, :], start=False, stop=(n == NS - 1),
                                     skip_group_check=True).then_inc(s_y, 1)
                        for n in range(NS):
                            un = i * NS + n
                            if n >= 2:
                                pe.wait_ge(s_b, un - 1)
                            t.matmul(pb[:, n % 2, :], wbc[:, n, :], xc[:], start=True, stop=True).then_inc(s_bb, 1)
                            if n >= 2:
                                pe.wait_ge(s_c, un - 1)
                            t.matmul(pc[:, n % 2, :], wbc[:, NS + n, :], xc[:], start=True, stop=True).then_inc(s_cb, 1)
                            if n >= 1:
                                add(n - 1)
                        add(NS - 1)
                        pe.wait_ge(s_yz, i + 1)
                        t.matmul(pf[0:C, :], outT[:], yz[:], start=True, stop=True).then_inc(s_o, 1)
                        if final:
                            pe.wait_ge(s_sq, 2 * i + 1)
                            t.matmul(pg[:], mean[:], n2[:], start=True, stop=True).then_inc(s_var, 1)


def phase_axis(nc, sem, ident_in, tag, w, x_s, acc, vertical):
    with ExitStack() as ctx:
        def sb(name, shape):
            return ctx.enter_context(nc.sbuf_tensor(tag + name, shape, F32))

        def ps(name, shape):
            return ctx.enter_context(nc.psum_tensor(tag + name, shape, F32))

        JT = JB * TOK
        ident = sb("ident", [128, 128])
        inw = sb("inw", [128, 2 * JB, 128])
        wdt = sb("wdt", [128, JB, JB, 128])
        wbc = sb("wbc", [128, JB, 2 * G16, 2, 16])
        wo = sb("wo", [128, JB, 128])
        diag_d = sb("diag_d", [128, JB, 128])
        sel = sb("sel", [128, 16, 2, 64])
        cols = sb("cols", [128, JB, 7])
        TAP, CB, DTB, DP = 0, 4, 5, 6
        amat = sb("amat", [128, JB, NX])
        amh = sb("amh", [128, JB, NX])
        bn = sb("bn", [128, 4])
        bsc = sb("bsc", [128, 4])
        mask = sb("mask", [128, TOK])
        mark = sb("mark", [1, 10])
        consts = sb("consts", [128, 2])

        xt = sb("xt", [128, 2, TOK])
        xpad = sb("xpad", [128, NSEQ, HIST + SEQ])
        cvb = sb("cvb", [128, TOK])
        th = sb("th", [128, TOK])
        sp1 = sb("sp1", [128, TOK])
        sp3 = sb("sp3", [128, TOK])
        xc = sb("xc", [128, JB, TOK])
        gate = sb("gate", [128, JB, TOK])
        dt = sb("dt", [128, JB, TOK])
        dx = sb("dx", [128, JB, TOK])
        sfx = sb("sfx", [128, JB, TOK])
        tot = sb("tot", [128, JB, NSEQ])
        bc = sb("bc", [128, 2 * G16, TOK])
        av = sb("av", [128, 2, JT])
        bv = sb("bv", [128, 2, JT])
        rv = sb("rv", [128, 4, JT])
        pf = ps("pf", [128, TOK])
        pb = ps("pb", [128, 2, TOK])
        pc = ps("pc", [128, 2, TOK])
        py = ps("py", [128, JB, TOK])

        s_w, s_prep, s_wps, s_aexp = sem(tag + "weights"), sem(tag + "prep_step"), sem(tag + "weight_product"), sem(tag + "a_exp")
        s_x = [sem(tag + "input0"), sem(tag + "input1")]
        s_ff, s_fe = sem(tag + "front_full"), sem(tag + "front_free")
        s_cv, s_v, s_th, s_xc = (sem(tag + n) for n in ("conv_step", "conv", "tanh", "xc"))
        s_act, s_sp, s_dt, s_pf, s_rdy = (sem(tag + n) for n in ("act_step", "softplus", "dt", "prefix", "scan_inputs"))
        s_bb, s_cb, s_a, s_t = (sem(tag + n) for n in ("b_bcast", "c_bcast", "decay", "ratio_tanh"))
        s_b, s_rc, s_h, s_g, s_y = (sem(tag + n) for n in ("dbx", "ratio_c", "states", "product", "y_added"))
        s_yz, s_o, s_ac, s_done = (sem(tag + n) for n in ("gated", "out", "consts", "tile_done"))
        NF = 3 * JB + 2 * G16 + 1
        F_X, F_Z, F_DT, F_BC, F_O = 0, JB, 2 * JB, 3 * JB, NF - 1
        AT = HT

        def tiles(eng):
            with eng.Fori(0, 2) as b2:
                with eng.Fori(0, AT // 4) as rb:
                    for p in range(2):
                        yield b2, rb, p, b2 * (AT // 2) + rb * 2 + p

        raw = av[:, :, :].rearrange("p a n -> p (a n)")
        raw2 = bv[:, :, :].rearrange("p a n -> p (a n)")
        down2 = raw[0:EX, 0:128]
        inT = raw[0:EX, 128:128 + 2 * DX]
        outw2 = raw[0:EX, 512:512 + 2 * DX].rearrange("e (j g d) -> e j g d", j=JB, g=2)
        upT = raw[0:EX, 1024:1024 + C]
        xpr2 = raw[0:RX, 1280:1280 + 2 * DX].rearrange("r (j g d) -> r j g d", j=JB, g=2)
        dtT = raw[0:RX, 1792:1792 + DX]
        xpT = raw2[:, 0:JB * 2 * NX].rearrange("p (j n) -> p j n", j=JB)
        NW = 1 + 2 + 1 + 2 + 1 + 2 + 1 + 2 * (1 + 1 + 1 + 1)

        with nc.Block() as block:
            @block.sync
            def _(sp):
                def ld(dst, src):
                    sp.dma_start(dst, src).then_inc(s_w, 16)
                ld(ident[:], ident_in)
                ld(inT, w["inT"])
                ld(upT, w["upT"])
                ld(dtT, w["dtT"])
                for g in range(2):
                    q = slice(64 * g, 64 * g + 64)
                    ld(down2[:, q], w["down"])
                    ld(outw2[:, :, g, :], w["outw"].rearrange("e (j d) -> e j d", j=JB))
                    ld(xpr2[:, :, g, :], w["xpr"].rearrange("r (j d) -> r j d", j=JB))
                    ld(xpT[q], w["xpT"].rearrange("(j d) n -> d j n", j=JB))
                    ld(cols[q], w["cols"].rearrange("(j d) n -> d j n", j=JB))
                    ld(amat[q], w["alog"].rearrange("(j d) n -> d j n", j=JB))
                    ld(bn[q], w["bn"])
                with sp.Fori(0, 2) as b2:
                    with sp.Fori(0, AT // 4) as rb:
                        for p in range(2):
                            i = b2 * (AT // 2) + rb * 2 + p
                            sp.wait_ge(s_done, i + 1)
                            for g in range(2):
                                src = x_s[:, g * HT * TOK:(g + 1) * HT * TOK]
                                dst = xt[64 * g:64 * g + 64, p, :]
                                if vertical:
                                    src = src.rearrange("c (b h w) -> c b h w", b=2, w=W)
                                    src = src[:, bass.ds(b2, 1), :, bass.ds((rb * 2 + p) * NSEQ, NSEQ)].squeeze(1)
                                    dst = dst.rearrange("c (h w) -> c h w", w=NSEQ)
                                else:
                                    src = src[:, bass.ds(b2 * L + (rb * 2 + p) * TOK, TOK)]
                                sp.dma_start(dst, src).then_inc(s_x[p], 16)

            @block.vector
            def _(dve):
                v = nc.vector
                k = [0]

                def step(ins):
                    k[0] += 1
                    ins.then_inc(s_prep, 1)
                    dve.wait_ge(s_prep, k[0])
                for big in (inw, wdt, wbc, wo, mask, xpad, sel, bc):
                    v.memset(big[:], 1.0 if big is mask else 0.0)
                v.memset(consts[:, 0:1], HALF_LOG)
                step(v.memset(consts[:, 1:2], 1e-5))
                v.memset(mask[:].rearrange("p (s l) -> p s l", l=SEQ)[:, :, 0], 0.0)
                dve.wait_ge(s_w, 16 * NW)
                v.tensor_copy(sel[0:32], ident[0:32, 0:32].rearrange("p (g n) -> p n g", g=2).unsqueeze(3)
                              .broadcast_to([32, 16, 2, 64]))
                step(v.tensor_scalar(cols[:, :, TAP:CB + 1], cols[:, :, TAP:CB + 1], 0.5, None, ALU.mult))
                for j in range(JB):
                    v.tensor_scalar(diag_d[:, j, :], ident[:], cols[:, j, DP:DP + 1], None, ALU.mult)
                for g in range(2):
                    q = slice(64 * g, 64 * g + 64)
                    v.tensor_copy(wbc[q, :, :, g, :], xpT[q].rearrange("p j (m n) -> p j m n", n=16))
                dve.wait_ge(s_wps, 1)
                for g in range(2):
                    q = slice(64 * g, 64 * g + 64)
                    v.tensor_copy(inw[q, 0:JB, q], pf[q, 0:DX].rearrange("p (j d) -> p j d", j=JB))
                    last = v.tensor_scalar(inw[q, JB:2 * JB, q], pf[q, DX:2 * DX].rearrange("p (j d) -> p j d", j=JB),
                                           0.5, None, ALU.mult)
                step(last)
                dve.wait_ge(s_wps, 1 + JB)
                for kk in range(JB):
                    for g in range(2):
                        q = slice(64 * g, 64 * g + 64)
                        v.tensor_copy(wdt[q, kk, :, q], py[q, kk, 0:DX].rearrange("p (j d) -> p j d", j=JB))
                dve.wait_ge(s_wps, 4 + JB)
                for j in range(JB):
                    for g in range(2):
                        q = slice(64 * g, 64 * g + 64)
                        v.tensor_copy(wo[q, j, q], pb[q, j % 2, (j // 2) * 64:(j // 2) * 64 + 64])
                dve.wait_ge(s_aexp, 1)
                step(v.tensor_tensor(bsc[:, 0:1], bsc[:, 3:4], bn[:, 0:1], ALU.mult))
                step(v.tensor_tensor(bsc[:, 2:3], bn[:, 2:3], bsc[:, 0:1], ALU.mult))
                step(v.tensor_tensor(bsc[:, 1:2], bn[:, 1:2], bsc[:, 2:3], ALU.subtract))
                v.tensor_scalar(amat[:], amat[:], -5.0, 5.0, ALU.max, ALU.min).then_inc(s_aexp, 1)
                dve.wait_ge(s_aexp, 3)
                step(v.tensor_scalar(amat[:], amat[:], -1.0, -5.0, ALU.mult, ALU.max))
                step(v.tensor_scalar(amh[:], amat[:], -0.5, None, ALU.mult))
                for m, (s, n) in enumerate([(s_b, 2), (s_rc, 2), (s_h, 2), (s_g, 2), (s_y, 4), (s_fe, 1), (s_done, 2)]):
                    v.memset(mark[:, m:m + 1], 0.0).then_inc(s, n)

                for b2, rb, p, i in tiles(dve):
                    seqs = lambda ap: ap.rearrange("p (s l) -> p s l", l=SEQ)
                    for j in range(JB):
                        if j > 0:
                            dve.wait_ge(s_xc, i * JB + j)
                        dve.wait_ge(s_fe, i * NF + F_X + j + 2)
                        for n in range(4):
                            src = xpad[:, :, n:n + SEQ]
                            tap = cols[:, j, TAP + n:TAP + n + 1]
                            if n == 0:
                                ins = v.tensor_scalar(seqs(cvb[:]), src, tap, cols[:, j, CB:CB + 1], ALU.mult, ALU.add)
                            else:
                                dve.wait_ge(s_cv, (i * JB + j) * 3 + n)
                                ins = v.scalar_tensor_tensor(seqs(cvb[:]), src, tap, seqs(cvb[:]), ALU.mult, ALU.add)
                            ins.then_inc(s_cv if n < 3 else s_v, 1)
                        dve.wait_ge(s_v, i * JB + j + 1)
                        dve.wait_ge(s_th, i * 2 * JB + j + 1)
                        v.scalar_tensor_tensor(xc[:, j, :], th[:], 1.0, cvb[:], ALU.add, ALU.mult).then_inc(s_xc, 1)
                    for j in range(JB):
                        dve.wait_ge(s_th, i * 2 * JB + JB + j + 1)
                        v.scalar_tensor_tensor(gate[:, j, :], th[:], 1.0, pf[:], ALU.add, ALU.mult).then_inc(s_fe, 1)
                    for j in range(JB):
                        dve.wait_ge(s_sp, i * JB + j + 1)
                        v.tensor_tensor(dt[:, j, :], sp1[:], sp3[:], ALU.add).then_inc(s_dt, 1)
                    dve.wait_ge(s_dt, i * JB + JB)
                    v.tensor_tensor(dx[:], dt[:], xc[:], ALU.mult)
                    for j in range(JB):
                        last = v.tensor_tensor_scan(sfx[:, j, :], mask[:], dt[:, j, :], 0.0, ALU.mult, ALU.add)
                    last.then_inc(s_pf, 1)
                    dve.wait_ge(s_pf, 3 * i + 1)
                    v.memset(dt[:].rearrange("p j (s l) -> p j s l", l=SEQ)[:, :, :, 0], RESET)
                    s4 = sfx[:].rearrange("p j (s l) -> p j s l", l=SEQ)
                    v.tensor_copy(tot[:], s4[:, :, :, SEQ - 1]).then_inc(s_pf, 1)
                    dve.wait_ge(s_pf, 3 * i + 2)
                    for j in range(JB):
                        last = v.tensor_tensor(s4[:, j], s4[:, j], tot[:, j, :].unsqueeze(2).broadcast_to([128, NSEQ, SEQ]),
                                               ALU.subtract)
                    last.then_inc(s_pf, 1)
                    dve.wait_ge(s_pf, 3 * i + 3)
                    v.memset(mark[:, 7:8], 0.0).then_inc(s_rdy, 1)

                    with dve.Fori(0, G16) as q:
                        for n in range(16):
                            un = i * NX + q * 16 + n
                            b3 = bv[:, n % 2, :].rearrange("p (j t) -> p j t", j=JB)
                            r3 = rv[:, n % 4, :].rearrange("p (j t) -> p j t", j=JB)
                            dve.wait_ge(s_bb, un + 1)
                            dve.wait_ge(s_g, un + 1)
                            v.tensor_tensor(b3, dx[:], pb[:, n % 2, :].unsqueeze(1).broadcast_to([128, JB, TOK]),
                                            ALU.mult).then_inc(s_b, 1)
                            dve.wait_ge(s_t, un + 1)
                            dve.wait_ge(s_cb, un + 1)
                            v.scalar_tensor_tensor(r3, r3, 1.0, pc[:, n % 2, :].unsqueeze(1).broadcast_to([128, JB, TOK]),
                                                   ALU.add, ALU.mult).then_inc(s_rc, 1)
                            dve.wait_ge(s_a, un + 1)
                            dve.wait_ge(s_b, un + 3)
                            v.tensor_tensor_scan(bv[:, n % 2, :], av[:, n % 2, :], bv[:, n % 2, :], 0.0,
                                                 ALU.mult, ALU.add).then_inc(s_h, 1)
                    dve.wait_ge(s_y, (i + 1) * NX + 4)
                    v.tensor_tensor(gate[:], gate[:], py[:], ALU.mult).then_inc(s_yz, 1)
                    dve.wait_ge(s_o, i + 1)
                    if vertical:
                        v.memset(mark[:, 8:9], 0.0).then_inc(s_done, 1)
                    else:
                        v.tensor_tensor(th[:], th[:], xt[:, p, :], ALU.add).then_inc(s_ac, 1)
                        dve.wait_ge(s_ac, i + 1)
                        image = acc[:, bass.ds(1 + b2 * (H + 1) + (rb * 2 + p) * ROWS, ROWS), 1:1 + W]
                        v.tensor_tensor(image, image, th[:].rearrange("p (r c) -> p r c", c=W),
                                        ALU.add).then_inc(s_done, 1)

            @block.scalar
            def _(act):
                a = nc.scalar
                act.wait_ge(s_prep, 1)
                act.wait_ge(s_w, 16 * NW)
                a.activation(bsc[:, 3:4], bn[:, 3:4], ACT.Ln, bias=consts[:, 1:2]).then_inc(s_act, 1)
                act.wait_ge(s_act, 1)
                a.activation(bsc[:, 3:4], bsc[:, 3:4], ACT.Exp, scale=-0.5).then_inc(s_aexp, 1)
                act.wait_ge(s_aexp, 2)
                a.activation(amat[:], amat[:], ACT.Exp).then_inc(s_aexp, 1)
                act.wait_ge(s_done, 2)

                for b2, rb, p, i in tiles(act):
                    for j in range(JB):
                        act.wait_ge(s_ff, i * NF + F_X + j + 1)
                        if j > 0:
                            act.wait_ge(s_v, i * JB + j)
                        a.activation(xpad[:, :, HIST:HIST + SEQ], pf[:].rearrange("p (s l) -> p s l", l=SEQ),
                                     ACT.Copy).then_inc(s_fe, 1)
                        act.wait_ge(s_v, i * JB + j + 1)
                        a.activation(th[:], cvb[:], ACT.Tanh).then_inc(s_th, 1)
                    act.wait_ge(s_xc, i * JB + JB)
                    for j in range(JB):
                        act.wait_ge(s_ff, i * NF + F_Z + j + 1)
                        a.activation(th[:], pf[:], ACT.Tanh).then_inc(s_th, 1)
                    for j in range(JB):
                        act.wait_ge(s_ff, i * NF + F_DT + j + 1)
                        if j > 0:
                            act.wait_ge(s_dt, i * JB + j)
                        a.activation(sp1[:], pf[:], ACT.Abs, bias=cols[:, j, DTB:DTB + 1]).then_inc(s_act, 1)
                        a.activation(sp3[:], pf[:], ACT.Relu, bias=cols[:, j, DTB:DTB + 1]).then_inc(s_fe, 1)
                        act.wait_ge(s_act, (i * JB + j) * 2 + 2)
                        a.activation(sp1[:], sp1[:], ACT.Exp, scale=-1.0).then_inc(s_act, 1)
                        act.wait_ge(s_act, (i * JB + j) * 2 + 3)
                        a.activation(sp1[:], sp1[:], ACT.Ln, bias=1.0).then_inc(s_sp, 1)
                    for grp in range(2 * G16):
                        act.wait_ge(s_ff, i * NF + F_BC + grp + 1)
                        a.activation(bc[0:32, grp, :], pf[0:32, :], ACT.Copy,
                                     scale=1.0 if grp < G16 else 0.5).then_inc(s_fe, 1)
                    act.wait_ge(s_rdy, i + 1)
                    with act.Fori(0, G16) as q:
                        for n in range(16):
                            un = i * NX + q * 16 + n
                            at = q * 16 + n
                            act.wait_ge(s_h, un + 1)
                            for j in range(JB):
                                ins = a.activation(av[:, n % 2, j * TOK:(j + 1) * TOK], dt[:, j, :], ACT.Exp,
                                                   scale=amat[:, j, bass.ds(at, 1)])
                            ins.then_inc(s_a, 1)
                            act.wait_ge(s_y, un + 1)
                            for j in range(JB):
                                ins = a.activation(rv[:, n % 4, j * TOK:(j + 1) * TOK], sfx[:, j, :], ACT.Tanh,
                                                   bias=consts[:, 0:1], scale=amh[:, j, bass.ds(at, 1)])
                            ins.then_inc(s_t, 1)
                    act.wait_ge(s_ff, i * NF + F_O + 1)
                    if vertical:
                        rows = acc[:, bass.ds(1 + b2 * (H + 1), H), bass.ds(1 + (rb * 2 + p) * NSEQ, NSEQ)]
                        a.activation(rows.rearrange("p h w -> p w h"), pf[:].rearrange("p (w h) -> p w h", h=H),
                                     ACT.Identity, bias=bsc[:, 1:2], scale=bsc[:, 0:1]).then_inc(s_o, 1)
                    else:
                        a.activation(th[:], pf[:], ACT.Identity, bias=bsc[:, 1:2], scale=bsc[:, 0:1]).then_inc(s_o, 1)
                    act.wait_ge(s_o, i + 1)
                    a.activation(sp1[:, 0:1], consts[:, 0:1], ACT.Copy).then_inc(s_fe, 1)

            @block.gpsimd
            def _(pool):
                for b2, rb, p, i in tiles(pool):
                    with pool.Fori(0, G16) as q:
                        for n in range(16):
                            un = i * NX + q * 16 + n
                            pool.wait_ge(s_rc, un + 3)
                            pool.wait_ge(s_h, un + 3)
                            nc.gpsimd.tensor_tensor(rv[:, n % 4, :], rv[:, n % 4, :], bv[:, n % 2, :],
                                                    ALU.mult).then_inc(s_g, 1)

            @block.tensor
            def _(pe):
                t = nc.tensor
                pe.wait_ge(s_w, 16 * NW)
                t.matmul(pf[:, 0:2 * DX], down2, inT, start=True, stop=True).then_inc(s_wps, 1)
                for kk in range(JB):
                    t.matmul(py[:, kk, 0:DX], xpr2[:, kk].rearrange("r g d -> r (g d)"), dtT, start=True,
                             stop=True).then_inc(s_wps, 1)
                for j in range(JB):
                    t.matmul(pb[:, j % 2, (j // 2) * 64:(j // 2) * 64 + 64], outw2[:, j].rearrange("e g d -> e (g d)"),
                             upT, start=True, stop=True).then_inc(s_wps, 1)

                for b2, rb, p, i in tiles(pe):
                    pe.wait_ge(s_x[p], 32 * (b2 * (AT // 4) + rb) + 32)
                    pe.wait_ge(s_done, i + 2)
                    xin = xt[:, p, :]
                    if vertical:
                        xin = xin.rearrange("p (h w) -> p w h", w=NSEQ)
                    for j in range(2 * JB):
                        pe.wait_ge(s_fe, i * NF + F_X + j + 1)
                        t.matmul(pf[:].rearrange("p (a b) -> p a b", b=SEQ) if vertical else pf[:], inw[:, j, :], xin,
                                 start=True, stop=True).then_inc(s_ff, 1)
                    pe.wait_ge(s_xc, i * JB + JB)
                    for j in range(JB):
                        pe.wait_ge(s_fe, i * NF + F_DT + j + 1)
                        for kk in range(JB):
                            mm = t.matmul(pf[:], wdt[:, kk, j, :], xc[:, kk, :], start=(kk == 0), stop=(kk == JB - 1))
                        mm.then_inc(s_ff, 1)
                    for grp in range(2 * G16):
                        pe.wait_ge(s_fe, i * NF + F_BC + grp + 1)
                        for kk in range(JB):
                            mm = t.matmul(pf[0:32, :], wbc[:, kk, grp].rearrange("p g n -> p (g n)"), xc[:, kk, :],
                                          start=(kk == 0), stop=(kk == JB - 1))
                        mm.then_inc(s_ff, 1)
                    for j in range(JB):
                        t.matmul(py[:, j, :], diag_d[:, j, :], xc[:, j, :], start=True, stop=False, skip_group_check=True)
                    pe.wait_ge(s_fe, i * NF + F_BC + 2 * G16 + 1)

                    def spread(q, n):
                        un = i * NX + q * 16 + n
                        lhsT = sel[:, n % 16].rearrange("p g d -> p (g d)")
                        pe.wait_ge(s_b, un + 1)
                        t.matmul(pb[:, n % 2, :], lhsT, bc[:, bass.ds(q + n // 16, 1), :].squeeze(1),
                                 start=True, stop=True).then_inc(s_bb, 1)
                        pe.wait_ge(s_rc, un + 1)
                        t.matmul(pc[:, n % 2, :], lhsT, bc[:, bass.ds(q + (G16 + n // 16), 1), :].squeeze(1),
                                 start=True, stop=True).then_inc(s_cb, 1)

                    def add(q, n):
                        pe.wait_ge(s_g, i * NX + q * 16 + n + 3)
                        for j in range(JB):
                            mm = t.matmul(py[:, j, :], ident[:], rv[:, n % 4, j * TOK:(j + 1) * TOK], start=False,
                                          stop=True, skip_group_check=True)
                        mm.then_inc(s_y, 1)
                    spread(0, 0)
                    with pe.Fori(0, G16 - 1) as q:
                        for n in range(16):
                            spread(q, n + 1)
                            add(q, n)
                    for n in range(16):
                        if n < 15:
                            spread(G16 - 1, n + 1)
                        add(G16 - 1, n)
                    pe.wait_ge(s_yz, i + 1)
                    pe.wait_ge(s_fe, i * NF + F_O + 1)
                    for j in range(JB):
                        mm = t.matmul(pf[:], wo[:, j, :], gate[:, j, :], start=(j == 0), stop=(j == JB - 1))
                    mm.then_inc(s_ff, 1)


def phase_filter(nc, sem, ident_in, w, acc, x_s, slots_s):
    with ExitStack() as ctx:
        def sb(name, shape):
            return ctx.enter_context(nc.sbuf_tensor("f_" + name, shape, F32))

        def ps(name, shape):
            return ctx.enter_context(nc.psum_tensor("f_" + name, shape, F32))

        MID, K9, BLK = C // 2, 9, TOK // 128
        ident = sb("ident", [128, 128])
        w1T = sb("w1T", [128, K9, MID])
        w1 = sb("w1", [128, K9, 2, MID])
        w2T = sb("w2T", [2 * MID, K9])
        w2 = sb("w2", [2 * MID, 2, K9])
        b1 = sb("b1", [2 * MID, 1])
        b2r = sb("b2r", [128, K9])
        sel = sb("sel", [2 * K9, K9, 2, C])
        zero = sb("zero", [C, HIST])
        h1 = sb("h1", [2 * MID, TOK])
        h2 = sb("h2", [2 * MID, TOK])
        lg = sb("lg", [128, BLK * 2, K9])
        ex = sb("ex", [128, BLK * 2, K9])
        mx = sb("mx", [128, BLK * 2])
        sm = sb("sm", [128, BLK * 2])
        wt = sb("wt", [2 * K9, TOK])
        pr = sb("pr", [128, 2, TOK])
        ot = sb("ot", [128, TOK])
        ph = ps("ph", [128, TOK])
        pl = ps("pl", [128, 512])
        pt = ps("pt", [128, TOK])
        pw = ps("pw", [128, 2, TOK])
        py = ps("py", [128, TOK])

        s_w, s_prep, s_done, s_out = sem("f_weights"), sem("f_prep_step"), sem("f_tile_done"), sem("f_stored")
        s_h, s_h1, s_h2, s_l, s_d = sem("f_conv1"), sem("f_biased"), sem("f_leaky"), sem("f_logits"), sem("f_dve_step")
        s_lx, s_ex, s_p, s_t, s_wt = sem("f_shifted"), sem("f_exp"), sem("f_softmax"), sem("f_transposed"), sem("f_weights_t")
        s_wb, s_pr, s_y = sem("f_weight_bcast"), sem("f_product"), sem("f_summed")
        NW = 1 + 2 * 3 + 1
        OUTS = 6

        with nc.Block() as block:
            @block.sync
            def _(sp):
                sp.dma_start(ident[:], ident_in).then_inc(s_w, 16)
                for g in range(2):
                    sp.dma_start(w1T[g * C:(g + 1) * C], w["w1T"]).then_inc(s_w, 16)
                    sp.dma_start(w2T[g * MID:(g + 1) * MID], w["w2T"]).then_inc(s_w, 16)
                    sp.dma_start(b1[g * MID:(g + 1) * MID], w["b1"]).then_inc(s_w, 16)
                sp.dma_start(b2r[:], w["b2"].partition_broadcast(128)).then_inc(s_w, 16)
                with sp.Fori(0, 2) as b2:
                    with sp.Fori(0, TPB) as rb:
                        i = b2 * TPB + rb
                        sp.wait_ge(s_done, i + 2)
                        for g in range(2):
                            q = slice(g * C, (g + 1) * C)
                            t = b2 * TPB + rb + g * HT
                            sp.dma_start(x_s[:, bass.ds(t * TOK, TOK)], ot[q, :]).then_inc(s_out, 16)
                            sp.dma_start(slots_s[:, bass.ds(t, 1), HIST:SLOT], ot[q, :].unsqueeze(1)).then_inc(s_out, 16)
                            sp.dma_start(slots_s[:, bass.ds(t + 1, 1), 0:HIST],
                                         ot[q, TOK - HIST:TOK].unsqueeze(1)).then_inc(s_out, 16)
                sp.dma_start(slots_s[:, 0, 0:HIST], zero[:]).then_inc(s_out, 16)
                sp.wait_ge(s_out, 16 * OUTS * (HT + 1) + 16)

            @block.vector
            def _(dve):
                v = nc.vector
                k = [0]

                def step(ins):
                    k[0] += 1
                    ins.then_inc(s_prep, 1)
                    dve.wait_ge(s_prep, k[0])
                v.memset(w1[:], 0.0)
                v.memset(zero[:], 0.0)
                step(v.memset(w2[:], 0.0))
                dve.wait_ge(s_w, 16 * NW)
                for g in range(2):
                    v.tensor_copy(w1[g * C:(g + 1) * C, :, g, :], w1T[g * C:(g + 1) * C])
                    v.tensor_copy(w2[g * MID:(g + 1) * MID, g, :], w2T[g * MID:(g + 1) * MID])
                v.tensor_copy(sel[:], ident[0:2 * K9, 0:2 * K9].rearrange("p (g n) -> p n g", g=2).unsqueeze(3)
                              .broadcast_to([2 * K9, K9, 2, C]))
                v.memset(mx[:], 0.0).then_inc(s_out, 16 * OUTS)
                v.memset(sm[:], 0.0).then_inc(s_done, 1)
                dve.wait_ge(s_done, 1)
                STEPS = 4
                with dve.Fori(0, 2) as b2:
                    with dve.Fori(0, TPB) as rb:
                        i = b2 * TPB + rb
                        r = image_row(b2, rb)
                        dve.wait_ge(s_h1, i + 1)
                        v.scalar_tensor_tensor(h2[:], h1[:], 0.2, h1[:], ALU.mult, ALU.max).then_inc(s_h2, 1)
                        dve.wait_ge(s_l, i + 1)
                        v.tensor_tensor(lg[:], pl[:, 0:BLK * 2 * K9].rearrange("p (m n) -> p m n", n=K9),
                                        b2r[:].unsqueeze(1).broadcast_to([128, BLK * 2, K9]), ALU.add).then_inc(s_d, 1)
                        dve.wait_ge(s_d, i * STEPS + 1)
                        v.tensor_reduce(mx[:], lg[:], AX_X, ALU.max).then_inc(s_d, 1)
                        dve.wait_ge(s_d, i * STEPS + 2)
                        v.tensor_tensor(lg[:], lg[:], mx[:].unsqueeze(2).broadcast_to([128, BLK * 2, K9]),
                                        ALU.subtract).then_inc(s_lx, 1)
                        dve.wait_ge(s_ex, i + 1)
                        v.tensor_reduce(sm[:], ex[:], AX_X, ALU.add).then_inc(s_d, 1)
                        dve.wait_ge(s_d, i * STEPS + 3)
                        v.reciprocal(mx[:], sm[:]).then_inc(s_d, 1)
                        dve.wait_ge(s_d, i * STEPS + 4)
                        v.tensor_tensor(lg[:], ex[:], mx[:].unsqueeze(2).broadcast_to([128, BLK * 2, K9]),
                                        ALU.mult).then_inc(s_p, 1)
                        for n in range(K9):
                            dve.wait_ge(s_wb, i * K9 + n + 1)
                            if n >= 2:
                                dve.wait_ge(s_y, i * K9 + n - 1)
                            v.tensor_tensor(pr[:, n % 2, :].rearrange("p (r c) -> p r c", c=W),
                                            pw[:, n % 2, :].rearrange("p (r c) -> p r c", c=W),
                                            acc[:, bass.ds(r + n // 3, ROWS), n % 3:n % 3 + W],
                                            ALU.mult).then_inc(s_pr, 1)
                        dve.wait_ge(s_y, i * K9 + K9)
                        dve.wait_ge(s_out, 16 * OUTS * (i + 1))
                        v.scalar_tensor_tensor(ot[:].rearrange("p (r c) -> p r c", c=W),
                                               acc[:, bass.ds(r + 1, ROWS), 1:1 + W], 2.0,
                                               py[:].rearrange("p (r c) -> p r c", c=W),
                                               ALU.mult, ALU.subtract).then_inc(s_done, 1)

            @block.scalar
            def _(act):
                a = nc.scalar
                act.wait_ge(s_w, 16 * NW)
                with act.Fori(0, HT) as i:
                    act.wait_ge(s_h, i + 1)
                    a.activation(h1[:], ph[0:2 * MID, :], ACT.Identity, bias=b1[:]).then_inc(s_h1, 1)
                    act.wait_ge(s_lx, i + 1)
                    a.activation(ex[:], lg[:], ACT.Exp).then_inc(s_ex, 1)
                    act.wait_ge(s_t, i + 1)
                    a.activation(wt[:], pt[0:2 * K9, :], ACT.Copy).then_inc(s_wt, 1)

            @block.tensor
            def _(pe):
                t = nc.tensor
                with pe.Fori(0, 2) as b2:
                    with pe.Fori(0, TPB) as rb:
                        i = b2 * TPB + rb
                        r = image_row(b2, rb)
                        pe.wait_ge(s_done, i + 1)
                        for n in range(K9):
                            mm = t.matmul(ph[0:2 * MID, :], w1[:, n].rearrange("p g m -> p (g m)"),
                                          acc[:, bass.ds(r + n // 3, ROWS), n % 3:n % 3 + W],
                                          start=(n == 0), stop=(n == K9 - 1))
                        mm.then_inc(s_h, 1)
                        pe.wait_ge(s_h2, i + 1)
                        for m in range(BLK):
                            mm = t.matmul(pl[:, m * 2 * K9:(m + 1) * 2 * K9], h2[:, m * 128:(m + 1) * 128],
                                          w2[:].rearrange("p g n -> p (g n)"), start=True, stop=True)
                        mm.then_inc(s_l, 1)
                        pe.wait_ge(s_p, i + 1)
                        for m in range(BLK):
                            mm = t.matmul(pt[0:2 * K9, m * 128:(m + 1) * 128],
                                          lg[:, 2 * m:2 * m + 2, :].rearrange("p g n -> p (g n)"), ident[:],
                                          start=True, stop=True)
                        mm.then_inc(s_t, 1)
                        pe.wait_ge(s_wt, i + 1)

                        def add(n, i=i):
                            pe.wait_ge(s_pr, i * K9 + n + 1)
                            t.matmul(py[:], ident[:], pr[:, n % 2, :], start=(n == 0), stop=(n == K9 - 1)).then_inc(s_y, 1)
                        for n in range(K9):
                            if n >= 2:
                                pe.wait_ge(s_pr, i * K9 + n - 1)
                            t.matmul(pw[:, n % 2, :], sel[:, n].rearrange("p g c -> p (g c)"), wt[:], start=True,
                                     stop=True).then_inc(s_wb, 1)
                            if n >= 1:
                                add(n - 1)
                        add(K9 - 1)


def phase_clear(nc, sem, acc):
    s_clear = sem("acc_cleared")
    with nc.Block() as block:
        @block.vector
        def _(dve):
            nc.vector.memset(acc[:], 0.0).then_inc(s_clear, 1)
            dve.wait_ge(s_clear, 1)


def build(nc, ins, out):
    seq_s = nc.dram_tensor("seq_s", [C, NT], F32).ap()
    hn_s = nc.dram_tensor("hn_s", [C, TILES + 1, SLOT], F32).ap()
    first_s = nc.dram_tensor("first_s", [C, NT], F32).ap()
    filt_s = nc.dram_tensor("filt_s", [C, NT], F32).ap()
    slots_s = nc.dram_tensor("slots_s", [C, TILES + 1, SLOT], F32).ap()
    ident = ins["ident"]

    def part(prefix):
        return {k[len(prefix):]: v for k, v in ins.items() if k.startswith(prefix)}

    def run(phase, *args, **kw):
        with nc.cleanup_on_exit():
            phase(nc, lambda name: nc.alloc_semaphore(name=name), *args, **kw)

    run(phase_conv_norm, ident, ins, ins["x"], seq_s, hn_s)
    run(phase_mamba, ident, "m0_", part("M0_"), hn_s, seq_s, first_s, reset=True, final=False)
    with nc.sbuf_tensor("acc", [128, PADR, PADW], F32) as acc:
        run(phase_clear, acc)
        run(phase_axis, ident, "h_", part("H_"), first_s, acc, vertical=True)
        run(phase_axis, ident, "w_", part("W_"), first_s, acc, vertical=False)
        run(phase_filter, ident, part("F_"), acc, filt_s, slots_s)
    run(phase_mamba, ident, "m3_", part("M3_"), slots_s, filt_s, out, reset=False, final=True)


def layouts(inputs):
    a = {k: np.asarray(v) for k, v in inputs.items()}

    def cc(*xs):
        return np.ascontiguousarray(np.concatenate([x.reshape(x.shape[0], -1) for x in xs], axis=1))

    t = np.ascontiguousarray
    out = {"x": t(a["x"].transpose(1, 0, 2, 3).reshape(C, NT)), "ident": np.eye(128, dtype=np.float32)}
    p = "L0_conv_"
    out["L0_cols"] = cc(*[a[p + n] for n in ("dwh_b", "dww_b", "conv_b", "bn_g", "bn_b", "bn_m", "bn_v", "ln_g", "ln_b",
                                             "dwh_w", "dww_w")])
    out["L0_convT"] = t(a[p + "conv_w"].reshape(C, C).T)

    def mamba(tag, p, taps, convb, dp):
        out[tag + "inT"] = t(a[p + "in_proj_w"].T)
        out[tag + "cols"] = cc(a[p + convb], a[p + "dt_proj_b"], a[p + dp], a[p + "A_log"])
        out[tag + "xpT"] = t(a[p + "x_proj_w"].T)
        out[tag + "xpr"] = t(a[p + "x_proj_w"][0:RANK])
        out[tag + "dtT"] = t(a[p + "dt_proj_w"].T)
        out[tag + "outT"] = t(a[p + "out_proj_w"].T)
        out[tag + "taps"] = t(a[p + taps].reshape(D, 4).T)

    mamba("M0_", "L0_conv_", "convd_w", "convd_b", "Dp")
    mamba("M3_", "L3_conv_", "conv_w", "conv_b", "D")
    p = "L3_conv_"
    out["M3_ocols"] = cc(a[p + "proj_b"], a[p + "ln_g"], a[p + "ln_b"])
    out["M3_opw"] = a[p + "out_proj_w"]
    out["M3_pw"] = a[p + "proj_w"]
    for tag, m, d, u, n in (("H_", "hm_", "hd_w", "hu_w", "hn_"), ("W_", "wm_", "wd_w", "wu_w", "wn_")):
        p = "L1_conv_"
        out[tag + "inT"] = t(a[p + m + "in_w"].T)
        out[tag + "down"] = a[p + d]
        out[tag + "outw"] = a[p + m + "out_w"]
        out[tag + "upT"] = t(a[p + u].T)
        out[tag + "xpr"] = t(a[p + m + "xproj_w"][0:RX])
        out[tag + "dtT"] = t(a[p + m + "dproj_w"].T)
        out[tag + "xpT"] = t(a[p + m + "xproj_w"][RX:].T)
        out[tag + "cols"] = cc(a[p + m + "conv_w"], a[p + m + "conv_b"], a[p + m + "dproj_b"], a[p + m + "D"])
        out[tag + "alog"] = a[p + m + "A_log"]
        out[tag + "bn"] = cc(*[a[p + n + k] for k in ("gamma", "beta", "mean", "var")])
    p = "L2_conv_"
    out["F_w1T"] = t(a[p + "w1"].reshape(C // 2, C, 9).transpose(1, 2, 0))
    out["F_w2T"] = t(a[p + "w2"].reshape(9, C // 2).T)
    out["F_b1"] = a[p + "b1"].reshape(C // 2, 1)
    out["F_b2"] = a[p + "b2"]
    return out


def kernel(**inputs):
    import concourse.bacc as _bacc
    from concourse.bass_utils import run_bass_kernel_spmd as _run

    nc = _bacc.Bacc("TRN2", target_bir_lowering=False, num_devices=1)
    arrays, ins = {}, {}
    for name, a in layouts(inputs).items():
        arrays[f"in_{name}"] = a
        ins[name] = nc.dram_tensor(f"in_{name}", a.shape, mybir.dt.from_np(a.dtype), kind="ExternalInput").ap()
    out = nc.dram_tensor("out_0", (C, NT), F32, kind="ExternalOutput").ap()
    build(nc, ins, out)
    r = _run(nc, [arrays], core_ids=[0])
    got = r.results[0]["out_0"]
    return np.ascontiguousarray(np.asarray(got).reshape(C, B, H, W).transpose(1, 0, 2, 3))
```

```python
from contextlib import ExitStack

import numpy as np
import concourse.bass as bass
from concourse import mybir

F32 = mybir.dt.float32
ALU = mybir.AluOpType
ACT = mybir.ActivationFunctionType
AX_X = mybir.AxisListType.X

B, C, H, W = 4, 64, 64, 64
L = H * W
NT = B * L
TOK = 512
ROWS = TOK // W
TPB = L // TOK
TILES = NT // TOK
HT = TILES // 2
HIST = 3
SLOT = HIST + TOK
PADR = 2 * H + 3
PADW = W + 2

D = 128
NS = 16
RANK = 4

DX = 192
NX = 96
RX = 6
EX = 96
JB = DX // 64
G16 = NX // 16
SEQ = 64
NSEQ = TOK // SEQ
RESET = 1.0e5
HALF_LOG = 0.5 * float(np.log(1.0e6))


def image_row(b2, rb):
    return b2 * (H + 1) + rb * ROWS


def phase_conv_norm(nc, sem, ident_in, w, x, seq_s, hn_s):
    with ExitStack() as ctx:
        def sb(name, shape):
            return ctx.enter_context(nc.sbuf_tensor("a_" + name, shape, F32))

        def ps(name, shape):
            return ctx.enter_context(nc.psum_tensor("a_" + name, shape, F32))

        xp = sb("xp", [128, PADR, PADW])
        cols = sb("cols", [128, 15])
        convT = sb("convT", [128, C])
        taps = sb("taps", [128, 5])
        sumb = sb("sumb", [128, 1])
        tapw = sb("tapw", [128, 5, 128])
        plain = sb("plain", [128, 128])
        center = sb("center", [128, 128])
        mean = sb("mean", [128, 128])
        ident = sb("ident", [128, 128])
        scale = sb("scale", [128, 1])
        shift = sb("shift", [128, 1])
        eps = sb("eps", [128, 1])
        tmp = sb("tmp", [128, 2])
        seq = sb("seq", [128, TOK])
        sq = sb("sq", [128, TOK])
        rstd = sb("rstd", [128, TOK])
        hn0 = sb("hn0", [128, TOK])
        hn = sb("hn", [128, TOK])
        zero = sb("zero", [128, HIST])
        pc = ps("pc", [128, TOK])
        pm = ps("pm", [128, TOK])
        pv = ps("pv", [128, TOK])
        pb = ps("pb", [128, 512])
        DWH_B, DWW_B, CONV_B, BN_G, BN_B, BN_M, BN_V, LN_G, LN_B, TH, TW = 0, 1, 2, 3, 4, 5, 6, 7, 8, 9, 12

        s_in, s_img = sem("a_loaded"), sem("a_image_loaded")
        s_pad, s_dve = sem("a_padded"), sem("a_dve_step")
        s_bias, s_lnv = sem("a_bias"), sem("a_bn_rsqrt")
        s_conv, s_seq, s_mean, s_sq = sem("a_conv"), sem("a_seq"), sem("a_centered"), sem("a_squares")
        s_var, s_rstd, s_hn, s_out = sem("a_var"), sem("a_rstd"), sem("a_hn"), sem("a_stored")
        s_ln = sem("a_act_step")
        PREP = 12

        with nc.Block() as block:
            @block.sync
            def _(sp):
                sp.dma_start(ident[:], ident_in).then_inc(s_in, 16)
                for g in range(2):
                    sp.dma_start(cols[g * C:(g + 1) * C, :], w["L0_cols"]).then_inc(s_in, 16)
                    sp.dma_start(convT[g * C:(g + 1) * C, :], w["L0_convT"]).then_inc(s_in, 16)
                sp.wait_ge(s_pad, 1)
                for g in range(2):
                    for b2 in range(2):
                        r = 1 + b2 * (H + 1)
                        sp.dma_start(xp[g * C:(g + 1) * C, r:r + H, 1:1 + W], x[:, (2 * g + b2) * L:(2 * g + b2 + 1) * L]
                                     .rearrange("c (h w) -> c h w", w=W)).then_inc(s_img, 16)
                sp.wait_ge(s_dve, PREP)
                for t in range(0, TILES, TPB):
                    sp.dma_start(hn_s[:, t, 0:HIST], zero[0:C, :]).then_inc(s_out, 16)
                with sp.Fori(0, 2) as b2:
                    with sp.Fori(0, TPB) as rb:
                        i = b2 * TPB + rb
                        to = [sp.snap((b2 * TPB + rb + g * HT) * TOK) for g in range(2)]
                        sp.wait_ge(s_seq, i + 1)
                        for g in range(2):
                            sp.dma_start(seq_s[:, bass.ds(to[g], TOK)],
                                         seq[g * C:(g + 1) * C, :]).then_inc(s_out, 16)
                        sp.wait_ge(s_hn, i + 1)
                        for g in range(2):
                            sp.dma_start(hn_s[:, bass.ds(b2 * TPB + rb + g * HT, 1), HIST:SLOT],
                                         hn[g * C:(g + 1) * C, :].unsqueeze(1)).then_inc(s_out, 16)
                        for g in range(2):
                            sp.dma_start(hn_s[:, bass.ds(b2 * TPB + rb + g * HT + 1, 1), 0:HIST],
                                         hn[g * C:(g + 1) * C, TOK - HIST:TOK].unsqueeze(1)).then_inc(s_out, 16)
                sp.wait_ge(s_out, 16 * (B + 6 * HT))
                for t in range(0, TILES, TPB):
                    sp.dma_start(hn_s[:, t, 0:HIST], zero[0:C, :]).then_inc(s_out, 16)
                sp.wait_ge(s_out, 16 * (2 * B + 6 * HT))

            @block.vector
            def _(dve):
                k = [0]

                def step(ins):
                    k[0] += 1
                    ins.then_inc(s_dve, 1)
                    dve.wait_ge(s_dve, k[0])
                v = nc.vector
                v.memset(xp[:], 0.0).then_inc(s_pad, 1)
                v.memset(tapw[:], 0.0)
                v.memset(plain[:], 0.0)
                v.memset(mean[:], 0.0)
                v.memset(zero[:], 0.0)
                step(v.memset(eps[:], 1e-5))
                dve.wait_ge(s_in, 16 * 5)
                col = lambda n: cols[:, n:n + 1]
                step(v.tensor_tensor(taps[:, 0:1], col(TH + 1), col(TW + 1), ALU.add))
                step(v.tensor_scalar(taps[:, 0:1], taps[:, 0:1], 1.0, None, ALU.add))
                v.tensor_copy(taps[:, 1:2], col(TH))
                v.tensor_copy(taps[:, 2:3], col(TH + 2))
                v.tensor_copy(taps[:, 3:4], col(TW))
                step(v.tensor_copy(taps[:, 4:5], col(TW + 2)))
                for g in range(2):
                    q = slice(g * C, (g + 1) * C)
                    v.tensor_copy(plain[q, q], convT[q, :])
                    v.memset(mean[q, q], 1.0 / C)
                    for n in range(5):
                        last = v.tensor_scalar(tapw[q, n, q], convT[q, :], taps[q, n:n + 1], None, ALU.mult)
                step(last)
                step(v.tensor_tensor(center[:], ident[:], mean[:], ALU.subtract))
                step(v.tensor_tensor(sumb[:], col(DWH_B), col(DWW_B), ALU.add))
                step(v.tensor_tensor(tmp[:, 0:1], col(CONV_B), col(BN_M), ALU.subtract))
                dve.wait_ge(s_bias, 1)
                dve.wait_ge(s_lnv, 1)
                step(v.tensor_tensor(scale[:], tmp[:, 1:2], col(BN_G), ALU.mult))
                step(v.tensor_tensor(tmp[:, 0:1], tmp[:, 0:1], pb[:, 0:1], ALU.add))
                step(v.tensor_tensor(tmp[:, 0:1], tmp[:, 0:1], scale[:], ALU.mult))
                step(v.tensor_tensor(shift[:], tmp[:, 0:1], col(BN_B), ALU.add))
                assert k[0] == PREP, k[0]
                with dve.Fori(0, HT) as i:
                    dve.wait_ge(s_rstd, i + 1)
                    dve.wait_ge(s_out, i * 96 + 16 * B)
                    v.tensor_tensor(hn0[:], pm[:], rstd[:], ALU.mult).then_inc(s_dve, 1)
                    dve.wait_ge(s_dve, i + PREP + 1)
                    v.tensor_scalar(hn[:], hn0[:], col(LN_G), col(LN_B), ALU.mult, ALU.add).then_inc(s_hn, 1)

            @block.scalar
            def _(act):
                a = nc.scalar
                act.wait_ge(s_in, 16 * 5)
                act.wait_ge(s_dve, 1)
                a.activation(tmp[:, 1:2], cols[:, BN_V:BN_V + 1], ACT.Ln, bias=eps[:]).then_inc(s_ln, 1)
                act.wait_ge(s_ln, 1)
                a.activation(tmp[:, 1:2], tmp[:, 1:2], ACT.Exp, scale=-0.5).then_inc(s_lnv, 1)
                act.wait_ge(s_dve, PREP)
                with act.Fori(0, HT) as i:
                    act.wait_ge(s_conv, i + 1)
                    act.wait_ge(s_out, i * 96 + 16 * B)
                    a.activation(seq[:], pc[:], ACT.Relu, bias=shift[:], scale=scale[:]).then_inc(s_seq, 1)
                    act.wait_ge(s_mean, i + 1)
                    a.activation(sq[:], pm[:], ACT.Square).then_inc(s_sq, 1)
                    act.wait_ge(s_var, i + 1)
                    a.activation(rstd[:], pv[:], ACT.Ln, bias=eps[:]).then_inc(s_ln, 1)
                    act.wait_ge(s_ln, i + 2)
                    a.activation(rstd[:], rstd[:], ACT.Exp, scale=-0.5).then_inc(s_rstd, 1)

            @block.tensor
            def _(pe):
                t = nc.tensor
                pe.wait_ge(s_dve, 7)
                t.matmul(pb[:, 0:1], plain[:], sumb[:], start=True, stop=True).then_inc(s_bias, 1)
                pe.wait_ge(s_img, 16 * B)
                with pe.Fori(0, 2) as b2:
                    with pe.Fori(0, TPB) as rb:
                        i = b2 * TPB + rb
                        r = image_row(b2, rb)
                        pe.wait_ge(s_dve, i + PREP)
                        for n, (dr, dc) in enumerate([(0, 0), (-1, 0), (1, 0), (0, -1), (0, 1)]):
                            mm = t.matmul(pc[:], tapw[:, n, :], xp[:, bass.ds(r + 1 + dr, ROWS), 1 + dc:1 + dc + W],
                                          start=(n == 0), stop=(n == 4))
                        mm.then_inc(s_conv, 1)
                        pe.wait_ge(s_seq, i + 1)
                        t.matmul(pm[:], center[:], seq[:], start=True, stop=True).then_inc(s_mean, 1)
                        pe.wait_ge(s_sq, i + 1)
                        t.matmul(pv[:], mean[:], sq[:], start=True, stop=True).then_inc(s_var, 1)


def phase_mamba(nc, sem, ident_in, tag, w, u_s, res_s, out_s, reset, final):
    with ExitStack() as ctx:
        def sb(name, shape):
            return ctx.enter_context(nc.sbuf_tensor(tag + name, shape, F32))

        def ps(name, shape):
            return ctx.enter_context(nc.psum_tensor(tag + name, shape, F32))

        ident = sb("ident", [128, 128])
        inT = sb("inT", [C, 2 * D])
        cols = sb("cols", [D, 3 + NS])
        CB, DTB, DP, AL = 0, 1, 2, 3
        xpT = sb("xpT", [D, RANK + 2 * NS])
        xpr = sb("xpr", [RANK, D])
        dtT = sb("dtT", [RANK, D])
        outT = sb("outT", [D, C])
        taprow = sb("taprow", [C, 4, D])
        tapw = sb("tapw", [C, 4, D])
        gatew = sb("gatew", [C, D])
        wdt = sb("wdt", [D, D])
        wbc = sb("wbc", [D, 2 * NS, 128])
        diag_d = sb("diag_d", [D, D])
        amat = sb("amat", [D, NS])
        cbh = sb("cbh", [D, 1])
        keep = sb("keep", [D, TILES])
        eps = sb("eps", [128, 1])
        mark = sb("mark", [1, 3])
        ocols = sb("ocols", [C, 3])
        opw = sb("opw", [C, D])
        pw = sb("pw", [C, C])
        center = sb("center", [C, C])
        mean = sb("mean", [C, 128])
        pjc = sb("pjc", [C, C])
        half = sb("half", [C, 3])

        u = sb("u", [C, 2, SLOT])
        res = sb("res", [C, 2, TOK])
        th = sb("th", [D, TOK])
        tg = sb("tg", [D, TOK])
        v0 = sb("v0", [D, TOK])
        xc = sb("xc", [D, TOK])
        gate = sb("gate", [D, TOK])
        sp1 = sb("sp1", [D, TOK])
        sp2 = sb("sp2", [D, TOK])
        sp3 = sb("sp3", [D, TOK])
        dt = sb("dt", [D, TOK])
        dx = sb("dx", [D, TOK])
        av = sb("av", [D, 2, TOK])
        bv = sb("bv", [D, 2, TOK])
        cv = sb("cv", [D, 2, TOK])
        gv = sb("gv", [D, 2, TOK])
        hs = sb("hs", [D, NS, TOK])
        st = sb("st", [D, NS])
        yz = sb("yz", [D, TOK])
        n1 = sb("n1", [C, TOK])
        n2 = sb("n2", [C, TOK])
        n3 = sb("n3", [C, TOK])
        ot = sb("ot", [C, TOK])
        pf = ps("pf", [128, TOK])
        pg = ps("pg", [128, TOK])
        pb = ps("pb", [128, 2, TOK])
        pc = ps("pc", [128, 2, TOK])
        py = ps("py", [128, TOK])
        po = ps("po", [128, TOK])

        s_w, s_prep, s_wps, s_aexp = sem(tag + "weights"), sem(tag + "prep_step"), sem(tag + "weights_made"), sem(tag + "a_exp")
        s_u = [sem(tag + "input0"), sem(tag + "input1")]
        s_done, s_out = sem(tag + "tile_done"), sem(tag + "stored")
        s_xz, s_tanh, s_xc = sem(tag + "in_proj"), sem(tag + "tanh"), sem(tag + "xc")
        s_dtp, s_act, s_sp, s_dt, s_dx = (sem(tag + n) for n in ("dt_pre", "act_step", "softplus", "dt", "dx"))
        s_bb, s_cb, s_a, s_c = (sem(tag + n) for n in ("b_bcast", "c_bcast", "decay", "c_copied"))
        s_b, s_h, s_g, s_y = (sem(tag + n) for n in ("dbx", "states", "c_times_h", "y_added"))
        s_st, s_v, s_yz, s_o = (sem(tag + n) for n in ("state_kept", "conv", "gated", "out_proj"))
        s_sq, s_var, s_rs, s_pn, s_tn = (sem(tag + n) for n in ("squares", "var", "rstd", "normed", "silu_tanh"))
        NW = 8 + (3 if final else 0)

        with nc.Block() as block:
            @block.sync
            def _(sp):
                loads = [(ident, ident_in), (inT, w["inT"]), (cols, w["cols"]), (xpT, w["xpT"]), (xpr, w["xpr"]),
                         (dtT, w["dtT"]), (outT, w["outT"])]
                if final:
                    loads += [(ocols, w["ocols"]), (opw, w["opw"]), (pw, w["pw"])]
                for dst, src in loads:
                    sp.dma_start(dst[:], src).then_inc(s_w, 16)
                sp.dma_start(taprow[:], w["taps"].partition_broadcast(C)).then_inc(s_w, 16)

                def load(i, p):
                    sp.dma_start(u[:, p:p + 1, :], u_s[:, bass.ds(i, 1), :]).then_inc(s_u[p], 16)
                    sp.dma_start(res[:, p, :], res_s[:, bass.ds(i * TOK, TOK)]).then_inc(s_u[p], 16)

                def store(i):
                    sp.dma_start(out_s[:, bass.ds(i * TOK, TOK)], ot[:]).then_inc(s_out, 16)

                load(0, 0)
                with sp.Fori(0, TILES // 2 - 1) as m:
                    for i, p in ((m * 2 + 1, 1), (m * 2 + 2, 0)):
                        sp.wait_ge(s_done, i)
                        load(i, p)
                        sp.wait_ge(s_done, i + 1)
                        store(i - 1)
                sp.wait_ge(s_done, TILES - 1)
                load(TILES - 1, 1)
                sp.wait_ge(s_done, TILES)
                store(TILES - 2)
                sp.wait_ge(s_done, TILES + 1)
                store(TILES - 1)
                sp.wait_ge(s_out, 16 * (TILES + 1))

            @block.vector
            def _(dve):
                v = nc.vector
                k = [0]

                def step(ins):
                    k[0] += 1
                    ins.then_inc(s_prep, 1)
                    dve.wait_ge(s_prep, k[0])
                v.memset(st[:], 0.0)
                v.memset(keep[:], 1.0)
                step(v.memset(mean[:], 1.0 / C))
                if reset:
                    v.memset(keep[:].rearrange("p (b t) -> p b t", t=TPB)[:, :, TPB - 1], 0.0)
                step(v.memset(eps[:], 1e-5))
                dve.wait_ge(s_w, 16 * NW)
                v.tensor_scalar(gatew[:], inT[:, D:2 * D], 0.5, None, ALU.mult)
                step(v.tensor_scalar(taprow[:], taprow[:], 0.5, None, ALU.mult))
                for n in range(4):
                    v.tensor_tensor(tapw[:, n, :], inT[:, 0:D], taprow[:, n, :], ALU.mult)
                v.tensor_scalar(cbh[:], cols[:, CB:CB + 1], 0.5, None, ALU.mult)
                v.tensor_scalar(diag_d[:], ident[:], cols[:, DP:DP + 1], None, ALU.mult)
                for n in range(2 * NS):
                    v.tensor_copy(wbc[:, n, :], xpT[:, RANK + n:RANK + n + 1].broadcast_to([D, 128]))
                dve.wait_ge(s_wps, 1)
                v.tensor_copy(wdt[:], pf[:, 0:D])
                dve.wait_ge(s_aexp, 1)
                step(v.tensor_scalar(amat[:], amat[:], -1.0, None, ALU.mult))
                if final:
                    v.tensor_tensor(center[:], ident[0:C, 0:C], mean[:, 0:C], ALU.subtract).then_inc(s_wps, 1)
                    dve.wait_ge(s_wps, 3)
                    v.tensor_copy(half[:, 0:1], pc[0:C, 0, 0:1])
                    v.tensor_scalar(half[:, 1:3], ocols[:, 1:3], 0.5, None, ALU.mult)
                    v.tensor_copy(pjc[:], pg[0:C, 0:C]).then_inc(s_wps, 1)
                    dve.wait_ge(s_wps, 5)
                    step(v.tensor_copy(outT[:], pb[:, 0, 0:C]))
                step(v.memset(mark[:, 0:1], 0.0))
                v.memset(mark[:, 1:2], 0.0).then_inc(s_out, 16)
                v.memset(mark[:, 2:3], 0.0).then_inc(s_done, 1)

                with dve.Fori(0, TILES // 2) as m:
                    for p in range(2):
                        i = m * 2 + p
                        dve.wait_ge(s_tanh, 2 * i + 1)
                        v.tensor_scalar(v0[:], pf[:], cbh[:, 0:1], None, ALU.add).then_inc(s_v, 1)
                        dve.wait_ge(s_v, i + 1)
                        v.scalar_tensor_tensor(xc[:], th[:], 1.0, v0[:], ALU.add, ALU.mult).then_inc(s_xc, 1)
                        dve.wait_ge(s_tanh, 2 * i + 2)
                        v.scalar_tensor_tensor(gate[:], tg[:], 1.0, pg[:], ALU.add, ALU.mult)
                        dve.wait_ge(s_sp, i + 1)
                        v.tensor_tensor(dt[:], sp2[:], sp3[:], ALU.add).then_inc(s_dt, 1)
                        dve.wait_ge(s_dt, i + 1)
                        v.tensor_tensor(dx[:], dt[:], xc[:], ALU.mult).then_inc(s_dx, 1)
                        dve.wait_ge(s_dx, i + 1)
                        for n in range(NS):
                            un = i * NS + n
                            dve.wait_ge(s_bb, un + 1)
                            v.tensor_tensor(bv[:, n % 2, :], pb[:, n % 2, :], dx[:], ALU.mult).then_inc(s_b, 1)
                            dve.wait_ge(s_b, un + 1)
                            dve.wait_ge(s_a, un + 1)
                            v.tensor_tensor_scan(hs[:, n, :], av[:, n % 2, :], bv[:, n % 2, :], st[:, n:n + 1],
                                                 ALU.mult, ALU.add).then_inc(s_h, 1)
                        dve.wait_ge(s_h, i * NS + NS)
                        v.tensor_scalar(st[:], hs[:, :, TOK - 1], keep[:, bass.ds(i, 1)], None,
                                        ALU.mult).then_inc(s_st, 1)
                        dve.wait_ge(s_st, i + 1)
                        dve.wait_ge(s_y, i * NS + NS)
                        v.tensor_tensor(yz[:], py[:], gate[:], ALU.mult).then_inc(s_yz, 1)
                        if not final:
                            dve.wait_ge(s_o, i + 1)
                            dve.wait_ge(s_out, 16 * i + 16)
                            dve.wait_ge(s_u[p], 32 * m + 32)
                            v.tensor_tensor(ot[:], pf[0:C, :], res[:, p, :], ALU.add).then_inc(s_done, 1)
                        else:
                            dve.wait_ge(s_rs, i + 1)
                            v.tensor_tensor(n3[:], n1[:], n2[:], ALU.mult).then_inc(s_pn, 1)
                            dve.wait_ge(s_pn, 3 * i + 1)
                            v.tensor_scalar(n1[:], n3[:], half[:, 1:2], half[:, 2:3], ALU.mult,
                                            ALU.add).then_inc(s_pn, 1)
                            dve.wait_ge(s_tn, i + 1)
                            v.scalar_tensor_tensor(n3[:], n2[:], 1.0, n1[:], ALU.add, ALU.mult).then_inc(s_pn, 1)
                            dve.wait_ge(s_pn, 3 * i + 3)
                            dve.wait_ge(s_out, 16 * i + 16)
                            v.tensor_tensor(ot[:], n3[:], res[:, p, :], ALU.add).then_inc(s_done, 1)

            @block.scalar
            def _(act):
                a = nc.scalar
                act.wait_ge(s_w, 16 * NW)
                a.activation(amat[:], cols[:, AL:AL + NS], ACT.Exp).then_inc(s_aexp, 1)
                act.wait_ge(s_done, 1)
                with act.Fori(0, TILES // 2) as m:
                    for p in range(2):
                        i = m * 2 + p
                        act.wait_ge(s_xz, i + 1)
                        a.activation(th[:], pf[:], ACT.Tanh, bias=cbh[:, 0:1]).then_inc(s_tanh, 1)
                        a.activation(tg[:], pg[:], ACT.Tanh).then_inc(s_tanh, 1)
                        act.wait_ge(s_dtp, i + 1)
                        a.activation(sp1[:], po[:], ACT.Abs, bias=cols[:, DTB:DTB + 1]).then_inc(s_act, 1)
                        a.activation(sp3[:], po[:], ACT.Relu, bias=cols[:, DTB:DTB + 1])
                        act.wait_ge(s_act, 2 * i + 1)
                        a.activation(sp1[:], sp1[:], ACT.Exp, scale=-1.0).then_inc(s_act, 1)
                        act.wait_ge(s_act, 2 * i + 2)
                        a.activation(sp2[:], sp1[:], ACT.Ln, bias=1.0).then_inc(s_sp, 1)
                        act.wait_ge(s_dt, i + 1)
                        for n in range(NS):
                            un = i * NS + n
                            if n >= 2:
                                act.wait_ge(s_h, un - 1)
                            a.activation(av[:, n % 2, :], dt[:], ACT.Exp, scale=amat[:, n:n + 1]).then_inc(s_a, 1)
                            act.wait_ge(s_cb, un + 1)
                            if n >= 2:
                                act.wait_ge(s_g, un - 1)
                            a.activation(cv[:, n % 2, :], pc[:, n % 2, :], ACT.Copy).then_inc(s_c, 1)
                        if final:
                            act.wait_ge(s_o, i + 1)
                            a.activation(n1[:], pf[0:C, :], ACT.Identity, bias=half[:, 0:1])
                            a.activation(n2[:], pf[0:C, :], ACT.Square, bias=half[:, 0:1]).then_inc(s_sq, 1)
                            act.wait_ge(s_var, i + 1)
                            a.activation(n2[:], pg[0:C, :], ACT.Ln, bias=eps[0:C, :]).then_inc(s_sq, 1)
                            act.wait_ge(s_sq, 2 * i + 2)
                            a.activation(n2[:], n2[:], ACT.Exp, scale=-0.5).then_inc(s_rs, 1)
                            act.wait_ge(s_pn, 3 * i + 2)
                            a.activation(n2[:], n1[:], ACT.Tanh).then_inc(s_tn, 1)

            @block.gpsimd
            def _(pool):
                with pool.Fori(0, TILES // 2) as m:
                    for p in range(2):
                        for n in range(NS):
                            un = (m * 2 + p) * NS + n
                            pool.wait_ge(s_h, un + 1)
                            pool.wait_ge(s_c, un + 1)
                            if n >= 2:
                                pool.wait_ge(s_y, un - 1)
                            nc.gpsimd.tensor_tensor(gv[:, n % 2, :], hs[:, n, :], cv[:, n % 2, :],
                                                    ALU.mult).then_inc(s_g, 1)

            @block.tensor
            def _(pe):
                t = nc.tensor
                pe.wait_ge(s_w, 16 * NW)
                t.matmul(pf[:, 0:D], xpr[:], dtT[:], start=True, stop=True).then_inc(s_wps, 1)
                if final:
                    pe.wait_ge(s_wps, 2)
                    t.matmul(pc[0:C, 0, 0:1], center[:], ocols[:, 0:1], start=True, stop=True)
                    t.matmul(pg[0:C, 0:C], pw[:], center[:], start=True, stop=True).then_inc(s_wps, 1)
                    pe.wait_ge(s_wps, 4)
                    t.matmul(pb[:, 0, 0:C], opw[:], pjc[:], start=True, stop=True).then_inc(s_wps, 1)
                with pe.Fori(0, TILES // 2) as m:
                    for p in range(2):
                        i = m * 2 + p
                        pe.wait_ge(s_done, i + 1)
                        pe.wait_ge(s_u[p], 32 * m + 32)
                        for n in range(4):
                            t.matmul(pf[:], tapw[:, n, :], u[:, p, n:n + TOK], start=(n == 0), stop=(n == 3))
                        t.matmul(pg[:], gatew[:], u[:, p, HIST:SLOT], start=True, stop=True).then_inc(s_xz, 1)
                        pe.wait_ge(s_xc, i + 1)
                        t.matmul(po[:], wdt[:], xc[:], start=True, stop=True).then_inc(s_dtp, 1)
                        t.matmul(py[:], diag_d[:], xc[:], start=True, stop=False, skip_group_check=True)

                        def add(n, i=i):
                            pe.wait_ge(s_g, i * NS + n + 1)
                            t.matmul(py[:], ident[:], gv[:, n % 2, :], start=False, stop=(n == NS - 1),
                                     skip_group_check=True).then_inc(s_y, 1)
                        for n in range(NS):
                            un = i * NS + n
                            if n >= 2:
                                pe.wait_ge(s_b, un - 1)
                            t.matmul(pb[:, n % 2, :], wbc[:, n, :], xc[:], start=True, stop=True).then_inc(s_bb, 1)
                            if n >= 2:
                                pe.wait_ge(s_c, un - 1)
                            t.matmul(pc[:, n % 2, :], wbc[:, NS + n, :], xc[:], start=True, stop=True).then_inc(s_cb, 1)
                            if n >= 1:
                                add(n - 1)
                        add(NS - 1)
                        pe.wait_ge(s_yz, i + 1)
                        t.matmul(pf[0:C, :], outT[:], yz[:], start=True, stop=True).then_inc(s_o, 1)
                        if final:
                            pe.wait_ge(s_sq, 2 * i + 1)
                            t.matmul(pg[:], mean[:], n2[:], start=True, stop=True).then_inc(s_var, 1)


def phase_axis(nc, sem, ident_in, tag, w, x_s, acc, vertical):
    with ExitStack() as ctx:
        def sb(name, shape):
            return ctx.enter_context(nc.sbuf_tensor(tag + name, shape, F32))

        def ps(name, shape):
            return ctx.enter_context(nc.psum_tensor(tag + name, shape, F32))

        JT = JB * TOK
        ident = sb("ident", [128, 128])
        inw = sb("inw", [128, 2 * JB, 128])
        wdt = sb("wdt", [128, JB, JB, 128])
        wbc = sb("wbc", [128, JB, 2 * G16, 2, 16])
        wo = sb("wo", [128, JB, 128])
        diag_d = sb("diag_d", [128, JB, 128])
        sel = sb("sel", [128, 16, 2, 64])
        cols = sb("cols", [128, JB, 7])
        TAP, CB, DTB, DP = 0, 4, 5, 6
        amat = sb("amat", [128, JB, NX])
        amh = sb("amh", [128, JB, NX])
        bn = sb("bn", [128, 4])
        bsc = sb("bsc", [128, 4])
        mask = sb("mask", [128, TOK])
        mark = sb("mark", [1, 10])
        consts = sb("consts", [128, 2])

        xt = sb("xt", [128, 2, TOK])
        xpad = sb("xpad", [128, NSEQ, HIST + SEQ])
        cvb = sb("cvb", [128, TOK])
        th = sb("th", [128, TOK])
        tz = sb("tz", [128, TOK])
        xc = sb("xc", [128, JB, TOK])
        gate = sb("gate", [128, 2, JB, TOK])
        dt = sb("dt", [128, 2, JB, TOK])
        dx = sb("dx", [128, 2, JB, TOK])
        sfx = sb("sfx", [128, 2, JB, TOK])
        tot = sb("tot", [128, JB, NSEQ])
        bc = sb("bc", [128, 2 * G16, TOK])
        av = sb("av", [128, 2, JT])
        bv = sb("bv", [128, 2, JT])
        rv = sb("rv", [128, 4, JT])
        pf = ps("pf", [128, TOK])
        pb = ps("pb", [128, 2, TOK])
        pc = ps("pc", [128, 2, TOK])
        py = ps("py", [128, JB, TOK])

        s_w, s_prep, s_wps, s_aexp = sem(tag + "weights"), sem(tag + "prep_step"), sem(tag + "weight_product"), sem(tag + "a_exp")
        s_x = [sem(tag + "input0"), sem(tag + "input1")]
        s_ff, s_fe = sem(tag + "front_full"), sem(tag + "front_free")
        s_cv, s_v, s_th, s_xc, s_tz = (sem(tag + n) for n in ("conv_step", "conv", "tanh", "xc", "gate_tanh"))
        s_act, s_sp, s_dt, s_pf, s_rdy = (sem(tag + n) for n in ("act_step", "softplus", "dt", "prefix", "scan_inputs"))
        s_bb, s_cb, s_a, s_t = (sem(tag + n) for n in ("b_bcast", "c_bcast", "decay", "ratio_tanh"))
        s_b, s_rc, s_h, s_g, s_y = (sem(tag + n) for n in ("dbx", "ratio_c", "states", "product", "y_added"))
        s_yz, s_o, s_ac, s_done = (sem(tag + n) for n in ("gated", "out", "consts", "tile_done"))
        BC_FILLS = [[(0, g) for g in range(4)], [(1, g) for g in range(4)], [(0, 4), (1, 4)], [(0, 5), (1, 5)]]
        F_X, F_DT, F_Z, F_BC = 0, JB, 2 * JB, 3 * JB
        FRONT = F_O = F_BC + len(BC_FILLS)
        NF = FRONT + 1
        AT = HT

        def tiles(eng):
            with eng.Fori(0, 2) as b2:
                with eng.Fori(0, AT // 4) as rb:
                    for p in range(2):
                        yield b2, rb, p, b2 * (AT // 2) + rb * 2 + p

        raw = av[:, :, :].rearrange("p a n -> p (a n)")
        raw2 = bv[:, :, :].rearrange("p a n -> p (a n)")
        down2 = raw[0:EX, 0:128]
        inT = raw[0:EX, 128:128 + 2 * DX]
        outw2 = raw[0:EX, 512:512 + 2 * DX].rearrange("e (j g d) -> e j g d", j=JB, g=2)
        upT = raw[0:EX, 1024:1024 + C]
        xpr2 = raw[0:RX, 1280:1280 + 2 * DX].rearrange("r (j g d) -> r j g d", j=JB, g=2)
        dtT = raw[0:RX, 1792:1792 + DX]
        xpT = raw2[:, 0:JB * 2 * NX].rearrange("p (j n) -> p j n", j=JB)
        NW = 1 + 2 + 1 + 2 + 1 + 2 + 1 + 2 * (1 + 1 + 1 + 1)

        with nc.Block() as block:
            @block.sync
            def _(sp):
                def ld(dst, src):
                    sp.dma_start(dst, src).then_inc(s_w, 16)
                ld(ident[:], ident_in)
                ld(inT, w["inT"])
                ld(upT, w["upT"])
                ld(dtT, w["dtT"])
                for g in range(2):
                    q = slice(64 * g, 64 * g + 64)
                    ld(down2[:, q], w["down"])
                    ld(outw2[:, :, g, :], w["outw"].rearrange("e (j d) -> e j d", j=JB))
                    ld(xpr2[:, :, g, :], w["xpr"].rearrange("r (j d) -> r j d", j=JB))
                    ld(xpT[q], w["xpT"].rearrange("(j d) n -> d j n", j=JB))
                    ld(cols[q], w["cols"].rearrange("(j d) n -> d j n", j=JB))
                    ld(amat[q], w["alog"].rearrange("(j d) n -> d j n", j=JB))
                    ld(bn[q], w["bn"])
                with sp.Fori(0, 2) as b2:
                    with sp.Fori(0, AT // 4) as rb:
                        for p in range(2):
                            i = b2 * (AT // 2) + rb * 2 + p
                            sp.wait_ge(s_done, i + 1)
                            for g in range(2):
                                src = x_s[:, g * HT * TOK:(g + 1) * HT * TOK]
                                dst = xt[64 * g:64 * g + 64, p, :]
                                if vertical:
                                    src = src.rearrange("c (b h w) -> c b h w", b=2, w=W)
                                    src = src[:, bass.ds(b2, 1), :, bass.ds((rb * 2 + p) * NSEQ, NSEQ)].squeeze(1)
                                    dst = dst.rearrange("c (h w) -> c h w", w=NSEQ)
                                else:
                                    src = src[:, bass.ds(b2 * L + (rb * 2 + p) * TOK, TOK)]
                                sp.dma_start(dst, src).then_inc(s_x[p], 16)
                sp.wait_ge(s_done, AT + 1)
                for g in range(2):
                    sp.dma_start(xt[64 * g:64 * g + 64, 0, :], x_s[:, 0:TOK]).then_inc(s_x[0], 16)

            @block.vector
            def _(dve):
                v = nc.vector
                k = [0]

                def step(ins):
                    k[0] += 1
                    ins.then_inc(s_prep, 1)
                    dve.wait_ge(s_prep, k[0])
                for big in (inw, wdt, wbc, wo, mask, xpad, sel, bc):
                    v.memset(big[:], 1.0 if big is mask else 0.0)
                v.memset(consts[:, 0:1], HALF_LOG)
                step(v.memset(consts[:, 1:2], 1e-5))
                v.memset(mask[:].rearrange("p (s l) -> p s l", l=SEQ)[:, :, 0], 0.0)
                dve.wait_ge(s_w, 16 * NW)
                v.tensor_copy(sel[0:32], ident[0:32, 0:32].rearrange("p (g n) -> p n g", g=2).unsqueeze(3)
                              .broadcast_to([32, 16, 2, 64]))
                step(v.tensor_scalar(cols[:, :, TAP:CB + 1], cols[:, :, TAP:CB + 1], 0.5, None, ALU.mult))
                for j in range(JB):
                    v.tensor_scalar(diag_d[:, j, :], ident[:], cols[:, j, DP:DP + 1], None, ALU.mult)
                for g in range(2):
                    q = slice(64 * g, 64 * g + 64)
                    for slot, (kind, m) in enumerate(f for fill in BC_FILLS for f in fill):
                        v.tensor_copy(wbc[q, :, slot, g, :], xpT[q, :, kind * NX + m * 16:kind * NX + m * 16 + 16])
                dve.wait_ge(s_wps, 1)
                for g in range(2):
                    q = slice(64 * g, 64 * g + 64)
                    v.tensor_copy(inw[q, 0:JB, q], pf[q, 0:DX].rearrange("p (j d) -> p j d", j=JB))
                    last = v.tensor_scalar(inw[q, JB:2 * JB, q], pf[q, DX:2 * DX].rearrange("p (j d) -> p j d", j=JB),
                                           0.5, None, ALU.mult)
                step(last)
                dve.wait_ge(s_wps, 1 + JB)
                for kk in range(JB):
                    for g in range(2):
                        q = slice(64 * g, 64 * g + 64)
                        v.tensor_copy(wdt[q, kk, :, q], py[q, kk, 0:DX].rearrange("p (j d) -> p j d", j=JB))
                dve.wait_ge(s_wps, 4 + JB)
                for j in range(JB):
                    for g in range(2):
                        q = slice(64 * g, 64 * g + 64)
                        v.tensor_copy(wo[q, j, q], pb[q, j % 2, (j // 2) * 64:(j // 2) * 64 + 64])
                dve.wait_ge(s_aexp, 1)
                step(v.tensor_tensor(bsc[:, 0:1], bsc[:, 3:4], bn[:, 0:1], ALU.mult))
                step(v.tensor_tensor(bsc[:, 2:3], bn[:, 2:3], bsc[:, 0:1], ALU.mult))
                step(v.tensor_tensor(bsc[:, 1:2], bn[:, 1:2], bsc[:, 2:3], ALU.subtract))
                v.tensor_scalar(amat[:], amat[:], -5.0, 5.0, ALU.max, ALU.min).then_inc(s_aexp, 1)
                dve.wait_ge(s_aexp, 3)
                step(v.tensor_scalar(amat[:], amat[:], -1.0, -5.0, ALU.mult, ALU.max))
                step(v.tensor_scalar(amh[:], amat[:], -0.5, None, ALU.mult))
                for m, (s, n) in enumerate([(s_b, 2), (s_rc, 2), (s_h, 2), (s_g, 2), (s_y, 4), (s_fe, 1), (s_done, 2)]):
                    v.memset(mark[:, m:m + 1], 0.0).then_inc(s, n)

                seqs = lambda ap: ap.rearrange("p (s l) -> p s l", l=SEQ)

                def conv(T, base, first, j):
                    if j > 0 or not first:
                        dve.wait_ge(s_xc, T * JB + j)
                    dve.wait_ge(s_fe, base + F_X + j + 2)
                    for n in range(4):
                        src = xpad[:, :, n:n + SEQ]
                        tap = cols[:, j, TAP + n:TAP + n + 1]
                        if n == 0:
                            ins = v.tensor_scalar(seqs(cvb[:]), src, tap, cols[:, j, CB:CB + 1], ALU.mult, ALU.add)
                        else:
                            dve.wait_ge(s_cv, (T * JB + j) * 3 + n)
                            ins = v.scalar_tensor_tensor(seqs(cvb[:]), src, tap, seqs(cvb[:]), ALU.mult, ALU.add)
                        ins.then_inc(s_cv if n < 3 else s_v, 1)

                def silu(T, j):
                    dve.wait_ge(s_v, T * JB + j + 1)
                    dve.wait_ge(s_th, T * JB + j + 1)
                    v.scalar_tensor_tensor(xc[:, j, :], th[:], 1.0, cvb[:], ALU.add, ALU.mult).then_inc(s_xc, 1)

                def gates(T, tp, j):
                    dve.wait_ge(s_tz, T * JB + j + 1)
                    v.scalar_tensor_tensor(gate[:, tp, j, :], tz[:], 1.0, pf[:], ALU.add, ALU.mult).then_inc(s_fe, 1)

                def steps(T, tp):
                    dtt, sf = dt[:, tp], sfx[:, tp]
                    dve.wait_ge(s_sp, T + 1)
                    v.tensor_tensor(dtt, dtt, sf, ALU.add).then_inc(s_dt, 1)
                    dve.wait_ge(s_dt, T + 1)
                    v.tensor_tensor(dx[:, tp], dtt, xc[:], ALU.mult)
                    for j in range(JB):
                        last = v.tensor_tensor_scan(sf[:, j, :], mask[:], dtt[:, j, :], 0.0, ALU.mult, ALU.add)
                    last.then_inc(s_pf, 1)
                    dve.wait_ge(s_pf, 3 * T + 1)
                    v.memset(dtt.rearrange("p j (s l) -> p j s l", l=SEQ)[:, :, :, 0], RESET)
                    s4 = sf.rearrange("p j (s l) -> p j s l", l=SEQ)
                    v.tensor_copy(tot[:], s4[:, :, :, SEQ - 1]).then_inc(s_pf, 1)
                    dve.wait_ge(s_pf, 3 * T + 2)
                    for j in range(JB):
                        last = v.tensor_tensor(s4[:, j], s4[:, j], tot[:, j, :].unsqueeze(2).broadcast_to([128, NSEQ, SEQ]),
                                               ALU.subtract)
                    last.then_inc(s_pf, 1)
                    dve.wait_ge(s_pf, 3 * T + 3)
                    v.memset(mark[:, 7:8], 0.0).then_inc(s_rdy, 1)

                def unit(i, p, q, n):
                    un = i * NX + q * 16 + n
                    b3 = bv[:, n % 2, :].rearrange("p (j t) -> p j t", j=JB)
                    r3 = rv[:, n % 4, :].rearrange("p (j t) -> p j t", j=JB)
                    dve.wait_ge(s_bb, un + 1)
                    dve.wait_ge(s_g, un + 1)
                    v.tensor_tensor(b3, dx[:, p], pb[:, n % 2, :].unsqueeze(1).broadcast_to([128, JB, TOK]),
                                    ALU.mult).then_inc(s_b, 1)
                    dve.wait_ge(s_t, un + 1)
                    dve.wait_ge(s_cb, un + 1)
                    v.scalar_tensor_tensor(r3, r3, 1.0, pc[:, n % 2, :].unsqueeze(1).broadcast_to([128, JB, TOK]),
                                           ALU.add, ALU.mult).then_inc(s_rc, 1)
                    dve.wait_ge(s_a, un + 1)
                    dve.wait_ge(s_b, un + 3)
                    v.tensor_tensor_scan(bv[:, n % 2, :], av[:, n % 2, :], bv[:, n % 2, :], 0.0,
                                         ALU.mult, ALU.add).then_inc(s_h, 1)

                for j in range(JB):
                    conv(0, 0, True, j)
                    silu(0, j)
                steps(0, 0)
                for j in range(JB):
                    gates(0, 0, j)
                for b2, rb, p, i in tiles(dve):
                    for n in range(16):
                        unit(i, p, 0, n)
                        for j in range(JB):
                            if n == 6 + 2 * j:
                                silu(i + 1, j)
                            if n == 4 + 2 * j:
                                conv(i + 1, FRONT + NF * i, False, j)
                    steps(i + 1, 1 - p)
                    with dve.Fori(1, G16 - 1) as q:
                        for n in range(16):
                            unit(i, p, q, n)
                    for n in range(16):
                        unit(i, p, G16 - 1, n)
                        for j in range(JB):
                            if n == 2 + 2 * j:
                                gates(i + 1, 1 - p, j)
                    dve.wait_ge(s_y, (i + 1) * NX + 4)
                    v.tensor_tensor(gate[:, p], gate[:, p], py[:], ALU.mult).then_inc(s_yz, 1)
                    dve.wait_ge(s_o, i + 1)
                    v.memset(mark[:, 9:10], 0.0).then_inc(s_fe, 1)
                    if vertical:
                        v.memset(mark[:, 8:9], 0.0).then_inc(s_done, 1)
                    else:
                        v.tensor_tensor(tz[:], tz[:], xt[:, p, :], ALU.add).then_inc(s_ac, 1)
                        dve.wait_ge(s_ac, i + 1)
                        image = acc[:, bass.ds(1 + b2 * (H + 1) + (rb * 2 + p) * ROWS, ROWS), 1:1 + W]
                        v.tensor_tensor(image, image, tz[:].rearrange("p (r c) -> p r c", c=W),
                                        ALU.add).then_inc(s_done, 1)

            @block.scalar
            def _(act):
                a = nc.scalar
                act.wait_ge(s_prep, 1)
                act.wait_ge(s_w, 16 * NW)
                a.activation(bsc[:, 3:4], bn[:, 3:4], ACT.Ln, bias=consts[:, 1:2]).then_inc(s_act, 1)
                act.wait_ge(s_act, 1)
                a.activation(bsc[:, 3:4], bsc[:, 3:4], ACT.Exp, scale=-0.5).then_inc(s_aexp, 1)
                act.wait_ge(s_aexp, 2)
                a.activation(amat[:], amat[:], ACT.Exp).then_inc(s_aexp, 1)
                act.wait_ge(s_done, 2)

                def copy(T, base, first, j):
                    act.wait_ge(s_ff, base + F_X + j + 1)
                    if j > 0 or not first:
                        act.wait_ge(s_v, T * JB + j)
                    a.activation(xpad[:, :, HIST:HIST + SEQ], pf[:].rearrange("p (s l) -> p s l", l=SEQ),
                                 ACT.Copy).then_inc(s_fe, 1)

                def tanh_x(T, first, j):
                    if j > 0 or not first:
                        act.wait_ge(s_xc, T * JB + j)
                    act.wait_ge(s_v, T * JB + j + 1)
                    a.activation(th[:], cvb[:], ACT.Tanh).then_inc(s_th, 1)

                def tanh_z(T, base, j):
                    act.wait_ge(s_ff, base + F_Z + j + 1)
                    act.wait_ge(s_done, T + 1)
                    a.activation(tz[:], pf[:], ACT.Tanh).then_inc(s_tz, 1)

                def softplus(T, base, tp, j):
                    act.wait_ge(s_ff, base + F_DT + j + 1)
                    a.activation(sfx[:, tp, j, :], pf[:], ACT.Abs, bias=cols[:, j, DTB:DTB + 1]).then_inc(s_act, 1)
                    a.activation(dt[:, tp, j, :], pf[:], ACT.Relu, bias=cols[:, j, DTB:DTB + 1]).then_inc(s_fe, 1)
                    act.wait_ge(s_act, 2 * JB * T + 2 * j + 2)
                    a.activation(sfx[:, tp, j, :], sfx[:, tp, j, :], ACT.Exp, scale=-1.0).then_inc(s_act, 1)

                def log(T, tp):
                    act.wait_ge(s_act, 2 * JB * T + 2 * JB + 1)
                    a.activation(sfx[:, tp], sfx[:, tp], ACT.Ln, bias=1.0).then_inc(s_sp, 1)

                def keep_bc(base, m):
                    act.wait_ge(s_ff, base + F_BC + m + 1)
                    for k, (kind, g) in enumerate(BC_FILLS[m]):
                        last = a.activation(bc[0:32, kind * G16 + g, :], pf[32 * k:32 * k + 32, :], ACT.Copy,
                                            scale=0.5 if kind else 1.0)
                    last.then_inc(s_fe, 1)

                def unit(i, p, q, n):
                    un = i * NX + q * 16 + n
                    at = q * 16 + n
                    act.wait_ge(s_y, un + 1)
                    for j in range(JB):
                        ins = a.activation(rv[:, n % 4, j * TOK:(j + 1) * TOK], sfx[:, p, j, :], ACT.Tanh,
                                           bias=consts[:, 0:1], scale=amh[:, j, bass.ds(at, 1)])
                    ins.then_inc(s_t, 1)
                    act.wait_ge(s_h, un + 1)
                    for j in range(JB):
                        ins = a.activation(av[:, n % 2, j * TOK:(j + 1) * TOK], dt[:, p, j, :], ACT.Exp,
                                           scale=amat[:, j, bass.ds(at, 1)])
                    ins.then_inc(s_a, 1)

                for j in range(JB):
                    copy(0, 0, True, j)
                    tanh_x(0, True, j)
                for j in range(JB):
                    softplus(0, 0, 0, j)
                log(0, 0)
                for j in range(JB):
                    tanh_z(0, 0, j)
                for m in range(len(BC_FILLS)):
                    keep_bc(0, m)
                for b2, rb, p, i in tiles(act):
                    base = FRONT + NF * i
                    act.wait_ge(s_rdy, i + 1)
                    for n in range(16):
                        unit(i, p, 0, n)
                        for j in range(JB):
                            if n == 5 + 2 * j:
                                tanh_x(i + 1, False, j)
                            if n == 4 + 2 * j:
                                copy(i + 1, base, False, j)
                            if n == 12 + j:
                                softplus(i + 1, base, 1 - p, j)
                    log(i + 1, 1 - p)
                    with act.Fori(1, G16 - 1) as q:
                        for n in range(16):
                            unit(i, p, q, n)
                    for n in range(16):
                        unit(i, p, G16 - 1, n)
                        for j in range(JB):
                            if n == 2 + 2 * j:
                                tanh_z(i + 1, base, j)
                            if n == 8 + 2 * j:
                                keep_bc(base, j)
                    keep_bc(base, 3)
                    act.wait_ge(s_ff, base + NF)
                    if vertical:
                        rows = acc[:, bass.ds(1 + b2 * (H + 1), H), bass.ds(1 + (rb * 2 + p) * NSEQ, NSEQ)]
                        a.activation(rows.rearrange("p h w -> p w h"), pf[:].rearrange("p (w h) -> p w h", h=H),
                                     ACT.Identity, bias=bsc[:, 1:2], scale=bsc[:, 0:1]).then_inc(s_o, 1)
                    else:
                        a.activation(tz[:], pf[:], ACT.Identity, bias=bsc[:, 1:2], scale=bsc[:, 0:1]).then_inc(s_o, 1)

            @block.gpsimd
            def _(pool):
                for b2, rb, p, i in tiles(pool):
                    with pool.Fori(0, G16) as q:
                        for n in range(16):
                            un = i * NX + q * 16 + n
                            pool.wait_ge(s_rc, un + 3)
                            pool.wait_ge(s_h, un + 3)
                            nc.gpsimd.tensor_tensor(rv[:, n % 4, :], rv[:, n % 4, :], bv[:, n % 2, :],
                                                    ALU.mult).then_inc(s_g, 1)

            @block.tensor
            def _(pe):
                t = nc.tensor
                pe.wait_ge(s_w, 16 * NW)
                t.matmul(pf[:, 0:2 * DX], down2, inT, start=True, stop=True).then_inc(s_wps, 1)
                for kk in range(JB):
                    t.matmul(py[:, kk, 0:DX], xpr2[:, kk].rearrange("r g d -> r (g d)"), dtT, start=True,
                             stop=True).then_inc(s_wps, 1)
                for j in range(JB):
                    t.matmul(pb[:, j % 2, (j // 2) * 64:(j // 2) * 64 + 64], outw2[:, j].rearrange("e g d -> e (g d)"),
                             upT, start=True, stop=True).then_inc(s_wps, 1)

                def front_free(base, f):
                    pe.wait_ge(s_fe, base + f + 1)

                def in_proj(base, tp, j):
                    front_free(base, F_X + j if j < JB else F_Z + j - JB)
                    xin = xt[:, tp, :]
                    if vertical:
                        xin = xin.rearrange("p (h w) -> p w h", w=NSEQ)
                    t.matmul(pf[:].rearrange("p (a b) -> p a b", b=SEQ) if vertical else pf[:], inw[:, j, :], xin,
                             start=True, stop=True).then_inc(s_ff, 1)

                def dt_proj(T, base, j):
                    if j == 0:
                        pe.wait_ge(s_xc, T * JB + JB)
                    front_free(base, F_DT + j)
                    for kk in range(JB):
                        mm = t.matmul(pf[:], wdt[:, kk, j, :], xc[:, kk, :], start=(kk == 0), stop=(kk == JB - 1))
                    mm.then_inc(s_ff, 1)

                def bc_proj(base, m):
                    front_free(base, F_BC + m)
                    at, rows = 4 * m if m < 3 else 10, 32 * len(BC_FILLS[m])
                    for kk in range(JB):
                        mm = t.matmul(pf[0:rows, :], wbc[:, kk, at:at + rows // 32].rearrange("p s g n -> p (s g n)"),
                                      xc[:, kk, :], start=(kk == 0), stop=(kk == JB - 1))
                    mm.then_inc(s_ff, 1)

                def spread(i, q, n):
                    un = i * NX + q * 16 + n
                    lhsT = sel[:, n % 16].rearrange("p g d -> p (g d)")
                    pe.wait_ge(s_b, un + 1)
                    t.matmul(pb[:, n % 2, :], lhsT, bc[:, bass.ds(q + n // 16, 1), :].squeeze(1),
                             start=True, stop=True).then_inc(s_bb, 1)
                    pe.wait_ge(s_rc, un + 1)
                    t.matmul(pc[:, n % 2, :], lhsT, bc[:, bass.ds(q + (G16 + n // 16), 1), :].squeeze(1),
                             start=True, stop=True).then_inc(s_cb, 1)

                def add(i, q, n):
                    pe.wait_ge(s_g, i * NX + q * 16 + n + 3)
                    for j in range(JB):
                        mm = t.matmul(py[:, j, :], ident[:], rv[:, n % 4, j * TOK:(j + 1) * TOK], start=False,
                                      stop=True, skip_group_check=True)
                    mm.then_inc(s_y, 1)

                def open_tile(i):
                    for j in range(JB):
                        t.matmul(py[:, j, :], diag_d[:, j, :], xc[:, j, :], start=True, stop=False, skip_group_check=True)

                pe.wait_ge(s_x[0], 32)
                pe.wait_ge(s_done, 2)
                for j in range(JB):
                    in_proj(0, 0, j)
                for j in range(JB):
                    dt_proj(0, 0, j)
                for j in range(JB):
                    in_proj(0, 0, JB + j)
                for m in range(len(BC_FILLS)):
                    bc_proj(0, m)
                open_tile(0)
                pe.wait_ge(s_fe, FRONT + 1)
                spread(0, 0, 0)
                for b2, rb, p, i in tiles(pe):
                    base = FRONT + NF * i
                    for n in range(16):
                        spread(i, 0, n + 1)
                        if n > 0:
                            add(i, 0, n - 1)
                        for j in range(JB):
                            if n == 3 and j == 0:
                                pe.wait_ge(s_x[1 - p], 32 * (b2 * (AT // 4) + rb) + 32 * (p + 1))
                            if n == 3 + 2 * j:
                                in_proj(base, 1 - p, j)
                            if n == 11 + j:
                                dt_proj(i + 1, base, j)
                    with pe.Fori(1, G16 - 1) as q:
                        for n in range(16):
                            spread(i, q, n + 1)
                            add(i, q, n - 1)
                    for n in range(16):
                        if n < 15:
                            spread(i, G16 - 1, n + 1)
                        add(i, G16 - 1, n - 1)
                        for j in range(JB):
                            if n == 1 + 2 * j:
                                in_proj(base, 1 - p, JB + j)
                            if n == 7 + 2 * j:
                                bc_proj(base, j)
                    bc_proj(base, 3)
                    add(i, G16 - 1, 15)
                    pe.wait_ge(s_yz, i + 1)
                    front_free(base, F_O)
                    for j in range(JB):
                        mm = t.matmul(pf[:], wo[:, j, :], gate[:, p, j, :], start=(j == 0), stop=(j == JB - 1))
                    mm.then_inc(s_ff, 1)
                    spread(i + 1, 0, 0)
                    open_tile(i + 1)


def phase_filter(nc, sem, ident_in, w, acc, x_s, slots_s):
    with ExitStack() as ctx:
        def sb(name, shape):
            return ctx.enter_context(nc.sbuf_tensor("f_" + name, shape, F32))

        def ps(name, shape):
            return ctx.enter_context(nc.psum_tensor("f_" + name, shape, F32))

        MID, K9, BLK = C // 2, 9, TOK // 128
        ident = sb("ident", [128, 128])
        w1T = sb("w1T", [128, K9, MID])
        w1 = sb("w1", [128, K9, 2, MID])
        w2T = sb("w2T", [2 * MID, K9])
        w2 = sb("w2", [2 * MID, 2, K9])
        b1 = sb("b1", [2 * MID, 1])
        b2r = sb("b2r", [128, K9])
        sel = sb("sel", [2 * K9, K9, 2, C])
        zero = sb("zero", [C, HIST])
        h1 = sb("h1", [2 * MID, TOK])
        h2 = sb("h2", [2 * MID, TOK])
        lg = sb("lg", [128, BLK * 2, K9])
        ex = sb("ex", [128, BLK * 2, K9])
        mx = sb("mx", [128, BLK * 2])
        sm = sb("sm", [128, BLK * 2])
        wt = sb("wt", [2 * K9, TOK])
        pr = sb("pr", [128, 2, TOK])
        ot = sb("ot", [128, TOK])
        ph = ps("ph", [128, TOK])
        pl = ps("pl", [128, 512])
        pt = ps("pt", [128, TOK])
        pw = ps("pw", [128, 2, TOK])
        py = ps("py", [128, TOK])

        s_w, s_prep, s_done, s_out = sem("f_weights"), sem("f_prep_step"), sem("f_tile_done"), sem("f_stored")
        s_h, s_h1, s_h2, s_l, s_d = sem("f_conv1"), sem("f_biased"), sem("f_leaky"), sem("f_logits"), sem("f_dve_step")
        s_lx, s_ex, s_p, s_t, s_wt = sem("f_shifted"), sem("f_exp"), sem("f_softmax"), sem("f_transposed"), sem("f_weights_t")
        s_wb, s_pr, s_y = sem("f_weight_bcast"), sem("f_product"), sem("f_summed")
        NW = 1 + 2 * 3 + 1
        OUTS = 6

        with nc.Block() as block:
            @block.sync
            def _(sp):
                sp.dma_start(ident[:], ident_in).then_inc(s_w, 16)
                for g in range(2):
                    sp.dma_start(w1T[g * C:(g + 1) * C], w["w1T"]).then_inc(s_w, 16)
                    sp.dma_start(w2T[g * MID:(g + 1) * MID], w["w2T"]).then_inc(s_w, 16)
                    sp.dma_start(b1[g * MID:(g + 1) * MID], w["b1"]).then_inc(s_w, 16)
                sp.dma_start(b2r[:], w["b2"].partition_broadcast(128)).then_inc(s_w, 16)
                with sp.Fori(0, 2) as b2:
                    with sp.Fori(0, TPB) as rb:
                        i = b2 * TPB + rb
                        sp.wait_ge(s_done, i + 2)
                        for g in range(2):
                            q = slice(g * C, (g + 1) * C)
                            t = b2 * TPB + rb + g * HT
                            sp.dma_start(x_s[:, bass.ds(t * TOK, TOK)], ot[q, :]).then_inc(s_out, 16)
                            sp.dma_start(slots_s[:, bass.ds(t, 1), HIST:SLOT], ot[q, :].unsqueeze(1)).then_inc(s_out, 16)
                            sp.dma_start(slots_s[:, bass.ds(t + 1, 1), 0:HIST],
                                         ot[q, TOK - HIST:TOK].unsqueeze(1)).then_inc(s_out, 16)
                sp.dma_start(slots_s[:, 0, 0:HIST], zero[:]).then_inc(s_out, 16)
                sp.wait_ge(s_out, 16 * OUTS * (HT + 1) + 16)

            @block.vector
            def _(dve):
                v = nc.vector
                k = [0]

                def step(ins):
                    k[0] += 1
                    ins.then_inc(s_prep, 1)
                    dve.wait_ge(s_prep, k[0])
                v.memset(w1[:], 0.0)
                v.memset(zero[:], 0.0)
                step(v.memset(w2[:], 0.0))
                dve.wait_ge(s_w, 16 * NW)
                for g in range(2):
                    v.tensor_copy(w1[g * C:(g + 1) * C, :, g, :], w1T[g * C:(g + 1) * C])
                    v.tensor_copy(w2[g * MID:(g + 1) * MID, g, :], w2T[g * MID:(g + 1) * MID])
                v.tensor_copy(sel[:], ident[0:2 * K9, 0:2 * K9].rearrange("p (g n) -> p n g", g=2).unsqueeze(3)
                              .broadcast_to([2 * K9, K9, 2, C]))
                v.memset(mx[:], 0.0).then_inc(s_out, 16 * OUTS)
                v.memset(sm[:], 0.0).then_inc(s_done, 1)
                dve.wait_ge(s_done, 1)
                STEPS = 4
                with dve.Fori(0, 2) as b2:
                    with dve.Fori(0, TPB) as rb:
                        i = b2 * TPB + rb
                        r = image_row(b2, rb)
                        dve.wait_ge(s_h1, i + 1)
                        v.scalar_tensor_tensor(h2[:], h1[:], 0.2, h1[:], ALU.mult, ALU.max).then_inc(s_h2, 1)
                        dve.wait_ge(s_l, i + 1)
                        v.tensor_tensor(lg[:], pl[:, 0:BLK * 2 * K9].rearrange("p (m n) -> p m n", n=K9),
                                        b2r[:].unsqueeze(1).broadcast_to([128, BLK * 2, K9]), ALU.add).then_inc(s_d, 1)
                        dve.wait_ge(s_d, i * STEPS + 1)
                        v.tensor_reduce(mx[:], lg[:], AX_X, ALU.max).then_inc(s_d, 1)
                        dve.wait_ge(s_d, i * STEPS + 2)
                        v.tensor_tensor(lg[:], lg[:], mx[:].unsqueeze(2).broadcast_to([128, BLK * 2, K9]),
                                        ALU.subtract).then_inc(s_lx, 1)
                        dve.wait_ge(s_ex, i + 1)
                        v.tensor_reduce(sm[:], ex[:], AX_X, ALU.add).then_inc(s_d, 1)
                        dve.wait_ge(s_d, i * STEPS + 3)
                        v.reciprocal(mx[:], sm[:]).then_inc(s_d, 1)
                        dve.wait_ge(s_d, i * STEPS + 4)
                        v.tensor_tensor(lg[:], ex[:], mx[:].unsqueeze(2).broadcast_to([128, BLK * 2, K9]),
                                        ALU.mult).then_inc(s_p, 1)
                        for n in range(K9):
                            dve.wait_ge(s_wb, i * K9 + n + 1)
                            if n >= 2:
                                dve.wait_ge(s_y, i * K9 + n - 1)
                            v.tensor_tensor(pr[:, n % 2, :].rearrange("p (r c) -> p r c", c=W),
                                            pw[:, n % 2, :].rearrange("p (r c) -> p r c", c=W),
                                            acc[:, bass.ds(r + n // 3, ROWS), n % 3:n % 3 + W],
                                            ALU.mult).then_inc(s_pr, 1)
                        dve.wait_ge(s_y, i * K9 + K9)
                        dve.wait_ge(s_out, 16 * OUTS * (i + 1))
                        v.scalar_tensor_tensor(ot[:].rearrange("p (r c) -> p r c", c=W),
                                               acc[:, bass.ds(r + 1, ROWS), 1:1 + W], 2.0,
                                               py[:].rearrange("p (r c) -> p r c", c=W),
                                               ALU.mult, ALU.subtract).then_inc(s_done, 1)

            @block.scalar
            def _(act):
                a = nc.scalar
                act.wait_ge(s_w, 16 * NW)
                with act.Fori(0, HT) as i:
                    act.wait_ge(s_h, i + 1)
                    a.activation(h1[:], ph[0:2 * MID, :], ACT.Identity, bias=b1[:]).then_inc(s_h1, 1)
                    act.wait_ge(s_lx, i + 1)
                    a.activation(ex[:], lg[:], ACT.Exp).then_inc(s_ex, 1)
                    act.wait_ge(s_t, i + 1)
                    a.activation(wt[:], pt[0:2 * K9, :], ACT.Copy).then_inc(s_wt, 1)

            @block.tensor
            def _(pe):
                t = nc.tensor
                with pe.Fori(0, 2) as b2:
                    with pe.Fori(0, TPB) as rb:
                        i = b2 * TPB + rb
                        r = image_row(b2, rb)
                        pe.wait_ge(s_done, i + 1)
                        for n in range(K9):
                            mm = t.matmul(ph[0:2 * MID, :], w1[:, n].rearrange("p g m -> p (g m)"),
                                          acc[:, bass.ds(r + n // 3, ROWS), n % 3:n % 3 + W],
                                          start=(n == 0), stop=(n == K9 - 1))
                        mm.then_inc(s_h, 1)
                        pe.wait_ge(s_h2, i + 1)
                        for m in range(BLK):
                            mm = t.matmul(pl[:, m * 2 * K9:(m + 1) * 2 * K9], h2[:, m * 128:(m + 1) * 128],
                                          w2[:].rearrange("p g n -> p (g n)"), start=True, stop=True)
                        mm.then_inc(s_l, 1)
                        pe.wait_ge(s_p, i + 1)
                        for m in range(BLK):
                            mm = t.matmul(pt[0:2 * K9, m * 128:(m + 1) * 128],
                                          lg[:, 2 * m:2 * m + 2, :].rearrange("p g n -> p (g n)"), ident[:],
                                          start=True, stop=True)
                        mm.then_inc(s_t, 1)
                        pe.wait_ge(s_wt, i + 1)

                        def add(n, i=i):
                            pe.wait_ge(s_pr, i * K9 + n + 1)
                            t.matmul(py[:], ident[:], pr[:, n % 2, :], start=(n == 0), stop=(n == K9 - 1)).then_inc(s_y, 1)
                        for n in range(K9):
                            if n >= 2:
                                pe.wait_ge(s_pr, i * K9 + n - 1)
                            t.matmul(pw[:, n % 2, :], sel[:, n].rearrange("p g c -> p (g c)"), wt[:], start=True,
                                     stop=True).then_inc(s_wb, 1)
                            if n >= 1:
                                add(n - 1)
                        add(K9 - 1)


def phase_clear(nc, sem, acc):
    s_clear = sem("acc_cleared")
    with nc.Block() as block:
        @block.vector
        def _(dve):
            nc.vector.memset(acc[:], 0.0).then_inc(s_clear, 1)
            dve.wait_ge(s_clear, 1)


def build(nc, ins, out):
    seq_s = nc.dram_tensor("seq_s", [C, NT], F32).ap()
    hn_s = nc.dram_tensor("hn_s", [C, TILES + 1, SLOT], F32).ap()
    first_s = nc.dram_tensor("first_s", [C, NT], F32).ap()
    filt_s = nc.dram_tensor("filt_s", [C, NT], F32).ap()
    slots_s = nc.dram_tensor("slots_s", [C, TILES + 1, SLOT], F32).ap()
    ident = ins["ident"]

    def part(prefix):
        return {k[len(prefix):]: v for k, v in ins.items() if k.startswith(prefix)}

    def run(phase, *args, **kw):
        with nc.cleanup_on_exit():
            phase(nc, lambda name: nc.alloc_semaphore(name=name), *args, **kw)

    run(phase_conv_norm, ident, ins, ins["x"], seq_s, hn_s)
    run(phase_mamba, ident, "m0_", part("M0_"), hn_s, seq_s, first_s, reset=True, final=False)
    with nc.sbuf_tensor("acc", [128, PADR, PADW], F32) as acc:
        run(phase_clear, acc)
        run(phase_axis, ident, "h_", part("H_"), first_s, acc, vertical=True)
        run(phase_axis, ident, "w_", part("W_"), first_s, acc, vertical=False)
        run(phase_filter, ident, part("F_"), acc, filt_s, slots_s)
    run(phase_mamba, ident, "m3_", part("M3_"), slots_s, filt_s, out, reset=False, final=True)


def layouts(inputs):
    a = {k: np.asarray(v) for k, v in inputs.items()}

    def cc(*xs):
        return np.ascontiguousarray(np.concatenate([x.reshape(x.shape[0], -1) for x in xs], axis=1))

    t = np.ascontiguousarray
    out = {"x": t(a["x"].transpose(1, 0, 2, 3).reshape(C, NT)), "ident": np.eye(128, dtype=np.float32)}
    p = "L0_conv_"
    out["L0_cols"] = cc(*[a[p + n] for n in ("dwh_b", "dww_b", "conv_b", "bn_g", "bn_b", "bn_m", "bn_v", "ln_g", "ln_b",
                                             "dwh_w", "dww_w")])
    out["L0_convT"] = t(a[p + "conv_w"].reshape(C, C).T)

    def mamba(tag, p, taps, convb, dp):
        out[tag + "inT"] = t(a[p + "in_proj_w"].T)
        out[tag + "cols"] = cc(a[p + convb], a[p + "dt_proj_b"], a[p + dp], a[p + "A_log"])
        out[tag + "xpT"] = t(a[p + "x_proj_w"].T)
        out[tag + "xpr"] = t(a[p + "x_proj_w"][0:RANK])
        out[tag + "dtT"] = t(a[p + "dt_proj_w"].T)
        out[tag + "outT"] = t(a[p + "out_proj_w"].T)
        out[tag + "taps"] = t(a[p + taps].reshape(D, 4).T)

    mamba("M0_", "L0_conv_", "convd_w", "convd_b", "Dp")
    mamba("M3_", "L3_conv_", "conv_w", "conv_b", "D")
    p = "L3_conv_"
    out["M3_ocols"] = cc(a[p + "proj_b"], a[p + "ln_g"], a[p + "ln_b"])
    out["M3_opw"] = a[p + "out_proj_w"]
    out["M3_pw"] = a[p + "proj_w"]
    for tag, m, d, u, n in (("H_", "hm_", "hd_w", "hu_w", "hn_"), ("W_", "wm_", "wd_w", "wu_w", "wn_")):
        p = "L1_conv_"
        out[tag + "inT"] = t(a[p + m + "in_w"].T)
        out[tag + "down"] = a[p + d]
        out[tag + "outw"] = a[p + m + "out_w"]
        out[tag + "upT"] = t(a[p + u].T)
        out[tag + "xpr"] = t(a[p + m + "xproj_w"][0:RX])
        out[tag + "dtT"] = t(a[p + m + "dproj_w"].T)
        out[tag + "xpT"] = t(a[p + m + "xproj_w"][RX:].T)
        out[tag + "cols"] = cc(a[p + m + "conv_w"], a[p + m + "conv_b"], a[p + m + "dproj_b"], a[p + m + "D"])
        out[tag + "alog"] = a[p + m + "A_log"]
        out[tag + "bn"] = cc(*[a[p + n + k] for k in ("gamma", "beta", "mean", "var")])
    p = "L2_conv_"
    out["F_w1T"] = t(a[p + "w1"].reshape(C // 2, C, 9).transpose(1, 2, 0))
    out["F_w2T"] = t(a[p + "w2"].reshape(9, C // 2).T)
    out["F_b1"] = a[p + "b1"].reshape(C // 2, 1)
    out["F_b2"] = a[p + "b2"]
    return out


def kernel(**inputs):
    import concourse.bacc as _bacc
    from concourse.bass_utils import run_bass_kernel_spmd as _run

    nc = _bacc.Bacc("TRN2", target_bir_lowering=False, num_devices=1)
    arrays, ins = {}, {}
    for name, a in layouts(inputs).items():
        arrays[f"in_{name}"] = a
        ins[name] = nc.dram_tensor(f"in_{name}", a.shape, mybir.dt.from_np(a.dtype), kind="ExternalInput").ap()
    out = nc.dram_tensor("out_0", (C, NT), F32, kind="ExternalOutput").ap()
    build(nc, ins, out)
    r = _run(nc, [arrays], core_ids=[0])
    got = r.results[0]["out_0"]
    return np.ascontiguousarray(np.asarray(got).reshape(C, B, H, W).transpose(1, 0, 2, 3))
```

```python
from contextlib import ExitStack

import numpy as np
import concourse.bass as bass
from concourse import mybir

F32 = mybir.dt.float32
BF16 = mybir.dt.bfloat16
ALU = mybir.AluOpType
ACT = mybir.ActivationFunctionType
AX_X = mybir.AxisListType.X

B, C, H, W = 4, 64, 64, 64
L = H * W
NT = B * L
TOK = 512
ROWS = TOK // W
TPB = L // TOK
TILES = NT // TOK
HT = TILES // 2
HIST = 3
SLOT = HIST + TOK
PADR = 2 * H + 3
PADW = W + 2

D = 128
NS = 16
RANK = 4

DX = 192
NX = 96
RX = 6
EX = 96
JB = DX // 64
G16 = NX // 16
SEQ = 64
NSEQ = TOK // SEQ
RESET = 1.0e5
HALF_LOG = 0.5 * float(np.log(1.0e6))


def image_row(b2, rb):
    return b2 * (H + 1) + rb * ROWS


def phase_conv_norm(nc, sem, ident_in, w, x, seq_s, hn_s):
    with ExitStack() as ctx:
        def sb(name, shape):
            return ctx.enter_context(nc.sbuf_tensor("a_" + name, shape, F32))

        def ps(name, shape):
            return ctx.enter_context(nc.psum_tensor("a_" + name, shape, F32))

        xp = sb("xp", [128, PADR, PADW])
        cols = sb("cols", [128, 15])
        convT = sb("convT", [128, C])
        taps = sb("taps", [128, 5])
        sumb = sb("sumb", [128, 1])
        tapw = sb("tapw", [128, 5, 128])
        plain = sb("plain", [128, 128])
        center = sb("center", [128, 128])
        mean = sb("mean", [128, 128])
        ident = sb("ident", [128, 128])
        scale = sb("scale", [128, 1])
        shift = sb("shift", [128, 1])
        eps = sb("eps", [128, 1])
        tmp = sb("tmp", [128, 2])
        seq = sb("seq", [128, TOK])
        sq = sb("sq", [128, TOK])
        rstd = sb("rstd", [128, TOK])
        hn0 = sb("hn0", [128, TOK])
        hn = sb("hn", [128, TOK])
        zero = sb("zero", [128, HIST])
        pc = ps("pc", [128, TOK])
        pm = ps("pm", [128, TOK])
        pv = ps("pv", [128, TOK])
        pb = ps("pb", [128, 512])
        DWH_B, DWW_B, CONV_B, BN_G, BN_B, BN_M, BN_V, LN_G, LN_B, TH, TW = 0, 1, 2, 3, 4, 5, 6, 7, 8, 9, 12

        s_in, s_img = sem("a_loaded"), sem("a_image_loaded")
        s_pad, s_dve = sem("a_padded"), sem("a_dve_step")
        s_bias, s_lnv = sem("a_bias"), sem("a_bn_rsqrt")
        s_conv, s_seq, s_mean, s_sq = sem("a_conv"), sem("a_seq"), sem("a_centered"), sem("a_squares")
        s_var, s_rstd, s_hn, s_out = sem("a_var"), sem("a_rstd"), sem("a_hn"), sem("a_stored")
        s_ln = sem("a_act_step")
        PREP = 12

        with nc.Block() as block:
            @block.sync
            def _(sp):
                sp.dma_start(ident[:], ident_in).then_inc(s_in, 16)
                for g in range(2):
                    sp.dma_start(cols[g * C:(g + 1) * C, :], w["L0_cols"]).then_inc(s_in, 16)
                    sp.dma_start(convT[g * C:(g + 1) * C, :], w["L0_convT"]).then_inc(s_in, 16)
                sp.wait_ge(s_pad, 1)
                for g in range(2):
                    for b2 in range(2):
                        r = 1 + b2 * (H + 1)
                        sp.dma_start(xp[g * C:(g + 1) * C, r:r + H, 1:1 + W], x[:, (2 * g + b2) * L:(2 * g + b2 + 1) * L]
                                     .rearrange("c (h w) -> c h w", w=W)).then_inc(s_img, 16)
                sp.wait_ge(s_dve, PREP)
                for t in range(0, TILES, TPB):
                    sp.dma_start(hn_s[:, t, 0:HIST], zero[0:C, :]).then_inc(s_out, 16)
                with sp.Fori(0, 2) as b2:
                    with sp.Fori(0, TPB) as rb:
                        i = b2 * TPB + rb
                        to = [sp.snap((b2 * TPB + rb + g * HT) * TOK) for g in range(2)]
                        sp.wait_ge(s_seq, i + 1)
                        for g in range(2):
                            sp.dma_start(seq_s[:, bass.ds(to[g], TOK)],
                                         seq[g * C:(g + 1) * C, :]).then_inc(s_out, 16)
                        sp.wait_ge(s_hn, i + 1)
                        for g in range(2):
                            sp.dma_start(hn_s[:, bass.ds(b2 * TPB + rb + g * HT, 1), HIST:SLOT],
                                         hn[g * C:(g + 1) * C, :].unsqueeze(1)).then_inc(s_out, 16)
                        for g in range(2):
                            sp.dma_start(hn_s[:, bass.ds(b2 * TPB + rb + g * HT + 1, 1), 0:HIST],
                                         hn[g * C:(g + 1) * C, TOK - HIST:TOK].unsqueeze(1)).then_inc(s_out, 16)
                sp.wait_ge(s_out, 16 * (B + 6 * HT))
                for t in range(0, TILES, TPB):
                    sp.dma_start(hn_s[:, t, 0:HIST], zero[0:C, :]).then_inc(s_out, 16)
                sp.wait_ge(s_out, 16 * (2 * B + 6 * HT))

            @block.vector
            def _(dve):
                k = [0]

                def step(ins):
                    k[0] += 1
                    ins.then_inc(s_dve, 1)
                    dve.wait_ge(s_dve, k[0])
                v = nc.vector
                v.memset(xp[:], 0.0).then_inc(s_pad, 1)
                v.memset(tapw[:], 0.0)
                v.memset(plain[:], 0.0)
                v.memset(mean[:], 0.0)
                v.memset(zero[:], 0.0)
                step(v.memset(eps[:], 1e-5))
                dve.wait_ge(s_in, 16 * 5)
                col = lambda n: cols[:, n:n + 1]
                step(v.tensor_tensor(taps[:, 0:1], col(TH + 1), col(TW + 1), ALU.add))
                step(v.tensor_scalar(taps[:, 0:1], taps[:, 0:1], 1.0, None, ALU.add))
                v.tensor_copy(taps[:, 1:2], col(TH))
                v.tensor_copy(taps[:, 2:3], col(TH + 2))
                v.tensor_copy(taps[:, 3:4], col(TW))
                step(v.tensor_copy(taps[:, 4:5], col(TW + 2)))
                for g in range(2):
                    q = slice(g * C, (g + 1) * C)
                    v.tensor_copy(plain[q, q], convT[q, :])
                    v.memset(mean[q, q], 1.0 / C)
                    for n in range(5):
                        last = v.tensor_scalar(tapw[q, n, q], convT[q, :], taps[q, n:n + 1], None, ALU.mult)
                step(last)
                step(v.tensor_tensor(center[:], ident[:], mean[:], ALU.subtract))
                step(v.tensor_tensor(sumb[:], col(DWH_B), col(DWW_B), ALU.add))
                step(v.tensor_tensor(tmp[:, 0:1], col(CONV_B), col(BN_M), ALU.subtract))
                dve.wait_ge(s_bias, 1)
                dve.wait_ge(s_lnv, 1)
                step(v.tensor_tensor(scale[:], tmp[:, 1:2], col(BN_G), ALU.mult))
                step(v.tensor_tensor(tmp[:, 0:1], tmp[:, 0:1], pb[:, 0:1], ALU.add))
                step(v.tensor_tensor(tmp[:, 0:1], tmp[:, 0:1], scale[:], ALU.mult))
                step(v.tensor_tensor(shift[:], tmp[:, 0:1], col(BN_B), ALU.add))
                assert k[0] == PREP, k[0]
                with dve.Fori(0, HT) as i:
                    dve.wait_ge(s_rstd, i + 1)
                    dve.wait_ge(s_out, i * 96 + 16 * B)
                    v.tensor_tensor(hn0[:], pm[:], rstd[:], ALU.mult).then_inc(s_dve, 1)
                    dve.wait_ge(s_dve, i + PREP + 1)
                    v.tensor_scalar(hn[:], hn0[:], col(LN_G), col(LN_B), ALU.mult, ALU.add).then_inc(s_hn, 1)

            @block.scalar
            def _(act):
                a = nc.scalar
                act.wait_ge(s_in, 16 * 5)
                act.wait_ge(s_dve, 1)
                a.activation(tmp[:, 1:2], cols[:, BN_V:BN_V + 1], ACT.Ln, bias=eps[:]).then_inc(s_ln, 1)
                act.wait_ge(s_ln, 1)
                a.activation(tmp[:, 1:2], tmp[:, 1:2], ACT.Exp, scale=-0.5).then_inc(s_lnv, 1)
                act.wait_ge(s_dve, PREP)
                with act.Fori(0, HT) as i:
                    act.wait_ge(s_conv, i + 1)
                    act.wait_ge(s_out, i * 96 + 16 * B)
                    a.activation(seq[:], pc[:], ACT.Relu, bias=shift[:], scale=scale[:]).then_inc(s_seq, 1)
                    act.wait_ge(s_mean, i + 1)
                    a.activation(sq[:], pm[:], ACT.Square).then_inc(s_sq, 1)
                    act.wait_ge(s_var, i + 1)
                    a.activation(rstd[:], pv[:], ACT.Ln, bias=eps[:]).then_inc(s_ln, 1)
                    act.wait_ge(s_ln, i + 2)
                    a.activation(rstd[:], rstd[:], ACT.Exp, scale=-0.5).then_inc(s_rstd, 1)

            @block.tensor
            def _(pe):
                t = nc.tensor
                pe.wait_ge(s_dve, 7)
                t.matmul(pb[:, 0:1], plain[:], sumb[:], start=True, stop=True).then_inc(s_bias, 1)
                pe.wait_ge(s_img, 16 * B)
                with pe.Fori(0, 2) as b2:
                    with pe.Fori(0, TPB) as rb:
                        i = b2 * TPB + rb
                        r = image_row(b2, rb)
                        pe.wait_ge(s_dve, i + PREP)
                        for n, (dr, dc) in enumerate([(0, 0), (-1, 0), (1, 0), (0, -1), (0, 1)]):
                            mm = t.matmul(pc[:], tapw[:, n, :], xp[:, bass.ds(r + 1 + dr, ROWS), 1 + dc:1 + dc + W],
                                          start=(n == 0), stop=(n == 4))
                        mm.then_inc(s_conv, 1)
                        pe.wait_ge(s_seq, i + 1)
                        t.matmul(pm[:], center[:], seq[:], start=True, stop=True).then_inc(s_mean, 1)
                        pe.wait_ge(s_sq, i + 1)
                        t.matmul(pv[:], mean[:], sq[:], start=True, stop=True).then_inc(s_var, 1)


def phase_mamba(nc, sem, ident_in, tag, w, u_s, res_s, out_s, reset, final):
    with ExitStack() as ctx:
        def sb(name, shape, dtype=F32):
            return ctx.enter_context(nc.sbuf_tensor(tag + name, shape, dtype))

        def ps(name, shape):
            return ctx.enter_context(nc.psum_tensor(tag + name, shape, F32))

        GV, LAG = 8, 4
        UB = 4
        ident = sb("ident", [128, 128])
        inT = sb("inT", [128, 2 * D])
        cols = sb("cols", [D, 3 + NS])
        CB, DTB, DP, AL = 0, 1, 2, 3
        xpT = sb("xpT", [D, RANK + 2 * NS])
        xpr = sb("xpr", [RANK, D])
        dtT = sb("dtT", [RANK, D])
        outT = sb("outT", [D, C])
        taprow = sb("taprow", [128, 2, D])
        tapw = sb("tapw", [128, 2, D])
        gatew = sb("gatew", [C, D])
        wdt = sb("wdt", [D, D])
        wbc = sb("wbc", [D, 4, 2 * NS])
        sel = sb("sel", [128, 2 * NS, 128], BF16)
        diag_d = sb("diag_d", [D, D])
        amat = sb("amat", [D, NS])
        cbh = sb("cbh", [D, 1])
        keep = sb("keep", [D, TILES])
        eps = sb("eps", [128, 1])
        mark = sb("mark", [1, 8])
        ocols = sb("ocols", [C, 3])
        opw = sb("opw", [C, D])
        pw = sb("pw", [C, C])
        center = sb("center", [C, C])
        mean = sb("mean", [C, 128])
        pjc = sb("pjc", [C, C])
        half = sb("half", [C, 3])

        u = sb("u", [128, 2, SLOT])
        res = sb("res", [C, 2, TOK])
        th = sb("th", [D, TOK])
        tg = sb("tg", [D, TOK])
        v0 = sb("v0", [D, TOK])
        xc = sb("xc", [D, TOK])
        sp = sb("softplus", [D, TOK])
        rest = sb("rest", [128, TOK])
        bc = sb("bc", [128, 2, TOK], BF16)
        gate = sb("gate", [D, 2, TOK])
        dt = sb("dt", [D, 2, TOK])
        dx = sb("dx", [D, 2, TOK])
        av = sb("av", [D, UB, TOK])
        bv = sb("bv", [D, UB, TOK])
        cv = sb("cv", [D, UB, TOK])
        gv = sb("gv", [D, GV, TOK])
        hs = sb("hs", [D, NS, TOK])
        st = sb("st", [D, NS])
        yz = sb("yz", [D, TOK])
        n1 = sb("n1", [C, TOK])
        n2 = sb("n2", [C, TOK])
        n3 = sb("n3", [C, TOK])
        ot = sb("ot", [C, TOK])
        pf = ps("pf", [128, TOK])
        pg = ps("pg", [128, TOK])
        pb = ps("pb", [128, 2, TOK])
        pc = ps("pc", [128, 2, TOK])
        py = ps("py", [128, 2, TOK])

        s_w, s_prep, s_wps, s_aexp = sem(tag + "weights"), sem(tag + "prep_step"), sem(tag + "weights_made"), sem(tag + "a_exp")
        s_u = [sem(tag + "input0"), sem(tag + "input1")]
        s_res = [sem(tag + "residual0"), sem(tag + "residual1")]
        s_ready, s_done, s_out = sem(tag + "ready"), sem(tag + "tile_done"), sem(tag + "stored")
        s_xz, s_tanh, s_v, s_xc, s_gate = (sem(tag + n) for n in ("in_proj", "tanh", "conv", "xc", "gate"))
        s_rows, s_dtp, s_hi, s_rest, s_mid, s_bc = (sem(tag + n) for n in ("bc_rows", "dt_pre", "bc_high", "bc_rest",
                                                                          "bc_middle", "bc_split"))
        s_act, s_sp, s_dt, s_dx = (sem(tag + n) for n in ("act_step", "softplus", "dt", "dx"))
        s_bb, s_cb, s_a, s_c = (sem(tag + n) for n in ("b_bcast", "c_bcast", "decay", "c_copied"))
        s_b, s_h, s_g, s_y = (sem(tag + n) for n in ("dbx", "states", "c_times_h", "y_added"))
        s_st, s_yz, s_o = (sem(tag + n) for n in ("state_kept", "gated", "out_proj"))
        s_sq, s_var, s_rs, s_pn, s_tn = (sem(tag + n) for n in ("squares", "var", "rstd", "normed", "silu_tanh"))
        NW = 10 + (3 if final else 0)

        def tiles(eng):
            yield 0, 0, False, True
            with eng.Fori(0, TILES // 2 - 1) as m:
                for k in (1, 2):
                    yield m * 2 + k, k % 2, True, True
            yield TILES - 1, 1, True, False

        with nc.Block() as block:
            @block.sync
            def _(sync):
                loads = [(ident[:], ident_in), (cols[:], w["cols"]), (xpT[:], w["xpT"]), (xpr[:], w["xpr"]),
                         (dtT[:], w["dtT"]), (outT[:], w["outT"])]
                taps = w["taps"].rearrange("(m g) d -> g m d", g=2)
                for g in range(2):
                    q = slice(g * C, (g + 1) * C)
                    loads += [(inT[q], w["inT"]), (taprow[q], taps[g].partition_broadcast(C))]
                if final:
                    loads += [(ocols[:], w["ocols"]), (opw[:], w["opw"]), (pw[:], w["pw"])]
                for dst, src in loads:
                    sync.dma_start(dst, src).then_inc(s_w, 16)

                def load_input(i, p):
                    sync.dma_start(u[0:C, p:p + 1, :], u_s[:, bass.ds(i, 1), :]).then_inc(s_u[p], 16)
                    sync.dma_start(u[C:128, p:p + 1, 0:SLOT - 1], u_s[:, bass.ds(i, 1), 1:SLOT]).then_inc(s_u[p], 16)

                def load_residual(i, p):
                    sync.dma_start(res[:, p, :], res_s[:, bass.ds(i * TOK, TOK)]).then_inc(s_res[p], 16)

                def store(i):
                    sync.dma_start(out_s[:, bass.ds(i * TOK, TOK)], ot[:]).then_inc(s_out, 16)

                for p in range(2):
                    load_input(p, p)
                    load_residual(p, p)
                with sync.Fori(0, TILES // 2 - 1) as m:
                    for p in range(2):
                        i = m * 2 + p
                        sync.wait_ge(s_xz, i + 1)
                        load_input(i + 2, p)
                        sync.wait_ge(s_done, i + 1)
                        store(i)
                        load_residual(i + 2, p)
                for i in (TILES - 2, TILES - 1):
                    sync.wait_ge(s_done, i + 1)
                    store(i)
                sync.wait_ge(s_out, 16 * (TILES + 1))

            @block.vector
            def _(dve):
                v = nc.vector
                k = [0]

                def step(ins):
                    k[0] += 1
                    ins.then_inc(s_prep, 1)
                    dve.wait_ge(s_prep, k[0])
                v.memset(st[:], 0.0)
                v.memset(keep[:], 1.0)
                v.memset(sel[:], 0.0)
                v.memset(wbc[:], 0.0)
                step(v.memset(mean[:], 1.0 / C))
                if reset:
                    v.memset(keep[:].rearrange("p (b t) -> p b t", t=TPB)[:, :, TPB - 1], 0.0)
                step(v.memset(eps[:], 1e-5))
                dve.wait_ge(s_w, 16 * NW)
                v.tensor_scalar(gatew[:], inT[0:C, D:2 * D], 0.5, None, ALU.mult)
                step(v.tensor_scalar(taprow[:], taprow[:], 0.5, None, ALU.mult))
                for n in range(2):
                    v.tensor_tensor(tapw[:, n, :], inT[:, 0:D], taprow[:, n, :], ALU.mult)
                v.tensor_scalar(cbh[:], cols[:, CB:CB + 1], 0.5, None, ALU.mult)
                v.tensor_scalar(diag_d[:], ident[:], cols[:, DP:DP + 1], None, ALU.mult)
                for n in range(3):
                    v.tensor_copy(wbc[:, n, :], xpT[:, RANK:RANK + 2 * NS])
                    r = slice(2 * NS * n, 2 * NS * (n + 1))
                    v.tensor_copy(sel[r], ident[r, r].unsqueeze(2).broadcast_to([2 * NS, 2 * NS, 128]))
                dve.wait_ge(s_wps, 1)
                v.tensor_copy(wdt[:], pf[:, 0:D])
                dve.wait_ge(s_aexp, 1)
                step(v.tensor_scalar(amat[:], amat[:], -1.0, None, ALU.mult))
                if final:
                    v.tensor_tensor(center[:], ident[0:C, 0:C], mean[:, 0:C], ALU.subtract).then_inc(s_wps, 1)
                    dve.wait_ge(s_wps, 3)
                    v.tensor_copy(half[:, 0:1], pc[0:C, 0, 0:1])
                    v.tensor_scalar(half[:, 1:3], ocols[:, 1:3], 0.5, None, ALU.mult)
                    v.tensor_copy(pjc[:], pg[0:C, 0:C]).then_inc(s_wps, 1)
                    dve.wait_ge(s_wps, 5)
                    step(v.tensor_copy(outT[:], pb[:, 0, 0:C]))
                for m, (s, n) in enumerate([(s_b, 2), (s_c, 2), (s_h, UB), (s_g, UB), (s_y, GV), (s_out, 16), (s_ready, 1)]):
                    v.memset(mark[:, m:m + 1], 0.0).then_inc(s, n)

                def silu(T):
                    dve.wait_ge(s_tanh, 2 * T + 1)
                    v.tensor_scalar(v0[:], pf[:], cbh[:, 0:1], None, ALU.add).then_inc(s_v, 1)
                    dve.wait_ge(s_v, T + 1)
                    v.scalar_tensor_tensor(xc[:], th[:], 1.0, v0[:], ALU.add, ALU.mult).then_inc(s_xc, 1)

                def gates(T, tp):
                    dve.wait_ge(s_tanh, 2 * T + 2)
                    v.scalar_tensor_tensor(gate[:, tp], tg[:], 1.0, pg[:], ALU.add, ALU.mult).then_inc(s_gate, 1)

                def remainder(T, tp):
                    dve.wait_ge(s_hi, T + 1)
                    v.tensor_tensor(rest[:], pf[:], bc[:, tp], ALU.subtract).then_inc(s_rest, 1)

                def low(T, tp):
                    dve.wait_ge(s_mid, T + 1)
                    v.tensor_tensor(bc[32:64, tp], rest[32:64], bc[32:64, tp], ALU.subtract).then_inc(s_bc, 1)

                def steps(T, tp):
                    dve.wait_ge(s_sp, T + 1)
                    v.tensor_tensor(dt[:, tp], dt[:, tp], sp[:], ALU.add).then_inc(s_dt, 1)
                    dve.wait_ge(s_dt, T + 1)
                    v.tensor_tensor(dx[:, tp], dt[:, tp], xc[:], ALU.mult).then_inc(s_dx, 1)

                def gated(T, tp):
                    dve.wait_ge(s_y, (T + 1) * NS + GV)
                    v.tensor_tensor(yz[:], py[:, tp], gate[:, tp], ALU.mult).then_inc(s_yz, 1)

                def residual_ready(T, tp):
                    dve.wait_ge(s_res[tp], T * 8 + (16 if tp == 0 else 8))

                def out_plain(T, tp):
                    dve.wait_ge(s_o, T + 1)
                    dve.wait_ge(s_out, 16 * T + 16)
                    residual_ready(T, tp)
                    v.tensor_tensor(ot[:], py[0:C, tp], res[:, tp], ALU.add).then_inc(s_done, 1)

                def norm(T):
                    dve.wait_ge(s_rs, T + 1)
                    v.tensor_tensor(n3[:], n1[:], n2[:], ALU.mult).then_inc(s_pn, 1)
                    dve.wait_ge(s_pn, 3 * T + 1)
                    v.tensor_scalar(n1[:], n3[:], half[:, 1:2], half[:, 2:3], ALU.mult, ALU.add).then_inc(s_pn, 1)

                def out_silu(T, tp):
                    dve.wait_ge(s_tn, T + 1)
                    v.scalar_tensor_tensor(n3[:], n2[:], 1.0, n1[:], ALU.add, ALU.mult).then_inc(s_pn, 1)
                    dve.wait_ge(s_pn, 3 * T + 3)
                    dve.wait_ge(s_out, 16 * T + 16)
                    residual_ready(T, tp)
                    v.tensor_tensor(ot[:], n3[:], res[:, tp], ALU.add).then_inc(s_done, 1)

                def product(i, p, n):
                    un = i * NS + n
                    dve.wait_ge(s_bb, un + 1)
                    dve.wait_ge(s_h, un + 1)
                    v.tensor_tensor(bv[:, n % UB, :], pb[:, n % 2, :], dx[:, p], ALU.mult).then_inc(s_b, 1)

                def scan(i, n):
                    un = i * NS + n
                    dve.wait_ge(s_b, un + 3)
                    dve.wait_ge(s_a, un + 1)
                    v.tensor_tensor_scan(hs[:, n, :], av[:, n % UB, :], bv[:, n % UB, :], st[:, n:n + 1],
                                         ALU.mult, ALU.add).then_inc(s_h, 1)

                silu(0)
                gates(0, 0)
                remainder(0, 0)
                low(0, 0)
                steps(0, 0)
                for i, p, before, behind in tiles(dve):
                    dve.wait_ge(s_dx, i + 1)
                    for n in range(NS):
                        product(i, p, n)
                        if n > 0:
                            scan(i, n - 1)
                        if before and n == 4:
                            gated(i - 1, 1 - p)
                        if before and n == 8 and not final:
                            out_plain(i - 1, 1 - p)
                        if behind and n == 6:
                            silu(i + 1)
                        if behind and n == 7:
                            gates(i + 1, 1 - p)
                        if behind and n == 11:
                            remainder(i + 1, 1 - p)
                        if behind and n == 13:
                            low(i + 1, 1 - p)
                        if behind and n == 14:
                            steps(i + 1, 1 - p)
                        if before and n == 13 and final:
                            norm(i - 1)
                    scan(i, NS - 1)
                    dve.wait_ge(s_h, i * NS + NS + UB)
                    v.tensor_scalar(st[:], hs[:, :, TOK - 1], keep[:, bass.ds(i, 1)], None, ALU.mult).then_inc(s_st, 1)
                    dve.wait_ge(s_st, i + 1)
                    if before and final:
                        out_silu(i - 1, 1 - p)
                gated(TILES - 1, 1)
                if final:
                    norm(TILES - 1)
                    out_silu(TILES - 1, 1)
                else:
                    out_plain(TILES - 1, 1)

            @block.scalar
            def _(act):
                a = nc.scalar
                act.wait_ge(s_w, 16 * NW)
                a.activation(amat[:], cols[:, AL:AL + NS], ACT.Exp).then_inc(s_aexp, 1)
                act.wait_ge(s_ready, 1)

                def tanhs(T):
                    act.wait_ge(s_xz, T + 1)
                    a.activation(th[:], pf[:], ACT.Tanh, bias=cbh[:, 0:1]).then_inc(s_tanh, 1)
                    a.activation(tg[:], pg[:], ACT.Tanh).then_inc(s_tanh, 1)

                def high(T, tp):
                    act.wait_ge(s_rows, T + 1)
                    a.activation(bc[:, tp], pf[:], ACT.Copy).then_inc(s_hi, 1)

                def softplus(T, tp):
                    act.wait_ge(s_dtp, T + 1)
                    a.activation(sp[:], pg[:], ACT.Abs, bias=cols[:, DTB:DTB + 1]).then_inc(s_act, 1)
                    a.activation(dt[:, tp], pg[:], ACT.Relu, bias=cols[:, DTB:DTB + 1])
                    act.wait_ge(s_act, 2 * T + 1)
                    a.activation(sp[:], sp[:], ACT.Exp, scale=-1.0).then_inc(s_act, 1)

                def middle(T, tp):
                    act.wait_ge(s_rest, T + 1)
                    a.activation(bc[0:64, tp], rest[0:64], ACT.Copy).then_inc(s_mid, 1)

                def log(T):
                    act.wait_ge(s_act, 2 * T + 2)
                    a.activation(sp[:], sp[:], ACT.Ln, bias=1.0).then_inc(s_sp, 1)

                def squares(T, tp):
                    act.wait_ge(s_o, T + 1)
                    a.activation(n1[:], py[0:C, tp], ACT.Identity, bias=half[:, 0:1])
                    a.activation(n2[:], py[0:C, tp], ACT.Square, bias=half[:, 0:1]).then_inc(s_sq, 1)

                def rsqrt(T, tp):
                    act.wait_ge(s_var, T + 1)
                    a.activation(n2[:], py[0:C, tp], ACT.Ln, bias=eps[0:C, :]).then_inc(s_sq, 1)
                    act.wait_ge(s_sq, 2 * T + 2)
                    a.activation(n2[:], n2[:], ACT.Exp, scale=-0.5).then_inc(s_rs, 1)

                def tanh_out(T):
                    act.wait_ge(s_pn, 3 * T + 2)
                    a.activation(n2[:], n1[:], ACT.Tanh).then_inc(s_tn, 1)

                tanhs(0)
                high(0, 0)
                softplus(0, 0)
                middle(0, 0)
                log(0)
                for i, p, before, behind in tiles(act):
                    act.wait_ge(s_dt, i + 1)
                    for n in range(NS):
                        un = i * NS + n
                        act.wait_ge(s_h, un + 1)
                        a.activation(av[:, n % UB, :], dt[:, p], ACT.Exp, scale=amat[:, n:n + 1]).then_inc(s_a, 1)
                        act.wait_ge(s_cb, un + 1)
                        act.wait_ge(s_g, un + 1)
                        a.activation(cv[:, n % UB, :], pc[:, n % 2, :], ACT.Copy).then_inc(s_c, 1)
                        if before and n == 6 and final:
                            squares(i - 1, 1 - p)
                        if behind and n == 4:
                            tanhs(i + 1)
                        if behind and n == 9:
                            high(i + 1, 1 - p)
                        if behind and n == 10:
                            softplus(i + 1, 1 - p)
                        if behind and n == 12:
                            middle(i + 1, 1 - p)
                        if behind and n == 12:
                            log(i + 1)
                        if before and n == 12 and final:
                            rsqrt(i - 1, 1 - p)
                        if before and n == 14 and final:
                            tanh_out(i - 1)
                if final:
                    squares(TILES - 1, 1)
                    rsqrt(TILES - 1, 1)
                    tanh_out(TILES - 1)

            @block.gpsimd
            def _(pool):
                g = nc.gpsimd
                for i, p, before, behind in tiles(pool):
                    for n in range(NS):
                        un = i * NS + n
                        pool.wait_ge(s_h, un + 1 + UB)
                        pool.wait_ge(s_c, un + 3)
                        pool.wait_ge(s_y, un + 1)
                        g.tensor_tensor(gv[:, n % GV, :], hs[:, n, :], cv[:, n % UB, :], ALU.mult).then_inc(s_g, 1)

            @block.tensor
            def _(pe):
                t = nc.tensor
                pe.wait_ge(s_w, 16 * NW)
                t.matmul(pf[:, 0:D], xpr[:], dtT[:], start=True, stop=True).then_inc(s_wps, 1)
                if final:
                    pe.wait_ge(s_wps, 2)
                    t.matmul(pc[0:C, 0, 0:1], center[:], ocols[:, 0:1], start=True, stop=True)
                    t.matmul(pg[0:C, 0:C], pw[:], center[:], start=True, stop=True).then_inc(s_wps, 1)
                    pe.wait_ge(s_wps, 4)
                    t.matmul(pb[:, 0, 0:C], opw[:], pjc[:], start=True, stop=True).then_inc(s_wps, 1)
                pe.wait_ge(s_ready, 1)

                def in_proj(T, tp, first):
                    pe.wait_ge(s_u[tp], T * 16 + (32 if tp == 0 else 16))
                    if not first:
                        pe.wait_ge(s_rest, T)
                    for m in range(2):
                        t.matmul(pf[:], tapw[:, m, :], u[:, tp, 2 * m:2 * m + TOK], start=(m == 0), stop=(m == 1))

                def gate_proj(T, tp, first):
                    if not first:
                        pe.wait_ge(s_act, 2 * T)
                    t.matmul(pg[:], gatew[:], u[0:C, tp, HIST:SLOT], start=True, stop=True).then_inc(s_xz, 1)

                def x_proj(T):
                    pe.wait_ge(s_xc, T + 1)
                    t.matmul(pf[:], wbc[:].rearrange("p a n -> p (a n)"), xc[:], start=True, stop=True).then_inc(s_rows, 1)

                def dt_proj(T):
                    pe.wait_ge(s_gate, T + 1)
                    t.matmul(pg[:], wdt[:], xc[:], start=True, stop=True).then_inc(s_dtp, 1)

                def out_proj(T, tp):
                    pe.wait_ge(s_yz, T + 1)
                    t.matmul(py[0:C, tp], outT[:], yz[:], start=True, stop=True).then_inc(s_o, 1)

                def variance(T, tp):
                    pe.wait_ge(s_sq, 2 * T + 1)
                    t.matmul(py[:, tp], mean[:], n2[:], start=True, stop=True).then_inc(s_var, 1)

                def add(i, p, n):
                    pe.wait_ge(s_g, i * NS + n + 1 + UB)
                    t.matmul(py[:, p], ident[:], gv[:, n % GV, :], start=False, stop=(n == NS - 1),
                             skip_group_check=True).then_inc(s_y, 1)

                in_proj(0, 0, True)
                gate_proj(0, 0, True)
                x_proj(0)
                dt_proj(0)
                for i, p, before, behind in tiles(pe):
                    pe.wait_ge(s_bc, i + 1)
                    for n in range(NS):
                        un = i * NS + n
                        pe.wait_ge(s_b, un + 1)
                        t.matmul(pb[:, n % 2, :], sel[:, n, :], bc[:, p], start=True, stop=True).then_inc(s_bb, 1)
                        pe.wait_ge(s_c, un + 1)
                        t.matmul(pc[:, n % 2, :], sel[:, NS + n, :], bc[:, p], start=True, stop=True).then_inc(s_cb, 1)
                        if n >= LAG:
                            add(i, p, n - LAG)
                        elif before:
                            add(i - 1, 1 - p, NS - LAG + n)
                        if n == LAG - 1:
                            t.matmul(py[:, p], diag_d[:], xc[:], start=True, stop=False, skip_group_check=True)
                        if behind and n == 4:
                            in_proj(i + 1, 1 - p, False)
                        if behind and n == 5:
                            gate_proj(i + 1, 1 - p, False)
                        if before and n == 6:
                            out_proj(i - 1, 1 - p)
                        if before and n == 8 and final:
                            variance(i - 1, 1 - p)
                        if behind and n == 9:
                            x_proj(i + 1)
                        if behind and n == 10:
                            dt_proj(i + 1)
                for n in range(NS - LAG, NS):
                    add(TILES - 1, 1, n)
                out_proj(TILES - 1, 1)
                if final:
                    variance(TILES - 1, 1)


def phase_axis(nc, sem, ident_in, tag, w, x_s, acc, vertical):
    with ExitStack() as ctx:
        def sb(name, shape, dtype=F32):
            return ctx.enter_context(nc.sbuf_tensor(tag + name, shape, dtype))

        def ps(name, shape):
            return ctx.enter_context(nc.psum_tensor(tag + name, shape, F32))

        JT = JB * TOK
        ident = sb("ident", [128, 128])
        inw = sb("inw", [128, 2 * JB, 128])
        wdt = sb("wdt", [128, JB, JB, 128])
        wbc = sb("wbc", [128, JB, 2 * G16, 2, 16])
        wo = sb("wo", [128, JB, 128])
        diag_d = sb("diag_d", [128, JB, 128])
        sel = sb("sel", [128, 16, 2, 64], BF16)
        cols = sb("cols", [128, JB, 7])
        TAP, CB, DTB, DP = 0, 4, 5, 6
        amat = sb("amat", [128, JB, NX])
        amh = sb("amh", [128, JB, NX])
        bn = sb("bn", [128, 4])
        bsc = sb("bsc", [128, 4])
        mask = sb("mask", [128, TOK])
        mark = sb("mark", [1, 11])
        consts = sb("consts", [128, 2])

        xt = sb("xt", [128, 2, TOK])
        xpad = sb("xpad", [128, NSEQ, HIST + SEQ])
        cvb = sb("cvb", [128, TOK])
        th = sb("th", [128, TOK])
        tz = sb("tz", [128, TOK])
        rest = th
        xc = sb("xc", [128, JB, TOK])
        gate = sb("gate", [128, 2, JB, TOK])
        dt = sb("dt", [128, 2, JB, TOK])
        dx = sb("dx", [128, 2, JB, TOK])
        sfx = sb("sfx", [128, 2, JB, TOK])
        tot = sb("tot", [128, JB, NSEQ])
        bc = sb("bc", [128, 2 * G16, TOK], BF16)
        pieces = sb("pieces", [128, 3, 3, TOK], BF16)
        bcopy = sb("bcopy", [128, TOK])
        av = sb("av", [128, 2, JT])
        bv = sb("bv", [128, 4, JT])
        rv = sb("rv", [128, 4, JT])
        pf = ps("pf", [128, TOK])
        pb = ps("pb", [128, 2, TOK])
        pc = ps("pc", [128, 2, TOK])
        py = ps("py", [128, JB, TOK])

        s_w, s_prep, s_wps, s_aexp = sem(tag + "weights"), sem(tag + "prep_step"), sem(tag + "weight_product"), sem(tag + "a_exp")
        s_x = [sem(tag + "input0"), sem(tag + "input1")]
        s_bc = [sem(tag + "bc_groups_0_3"), sem(tag + "bc_groups_4_5")]
        s_hi, s_mid, s_low, s_bp, s_bk = (sem(tag + n) for n in ("bc_high", "bc_middle", "bc_low", "dbx_gpsimd", "b_copied"))
        s_ff, s_fe = sem(tag + "front_full"), sem(tag + "front_free")
        s_cv, s_v, s_th, s_xc, s_tz = (sem(tag + n) for n in ("conv_step", "conv", "tanh", "xc", "gate_tanh"))
        s_act, s_sp, s_dt, s_pf, s_rdy = (sem(tag + n) for n in ("act_step", "softplus", "dt", "prefix", "scan_inputs"))
        s_bb, s_cb, s_a, s_t = (sem(tag + n) for n in ("b_bcast", "c_bcast", "decay", "ratio_tanh"))
        s_b, s_rc, s_h, s_g, s_y = (sem(tag + n) for n in ("dbx", "ratio_c", "states", "product", "y_added"))
        s_yz, s_o, s_ac, s_done = (sem(tag + n) for n in ("gated", "out", "consts", "tile_done"))
        BC_FILLS = [[(0, g) for g in range(4)], [(1, g) for g in range(4)], [(0, 4), (1, 4), (0, 5), (1, 5)]]
        F_X, F_DT, F_BC = 0, JB, 2 * JB
        F_Z = F_BC + len(BC_FILLS)
        FRONT = F_O = F_Z + JB
        NF = FRONT + 1
        AT = HT
        POOL = (2, 5, 8, 11, 14)
        LAG = 2
        LOOK = 2
        PN, DN = len(POOL), 16 - len(POOL)

        def pools(n):
            return sum(m < n for m in POOL)

        def tiles(eng):
            with eng.Fori(0, 2) as b2:
                with eng.Fori(0, AT // 4) as rb:
                    for p in range(2):
                        yield b2, rb, p, b2 * (AT // 2) + rb * 2 + p

        raw = av[:, :, :].rearrange("p a n -> p (a n)")
        raw2 = bv[:, :, :].rearrange("p a n -> p (a n)")
        down2 = raw[0:EX, 0:128]
        inT = raw[0:EX, 128:128 + 2 * DX]
        outw2 = raw[0:EX, 512:512 + 2 * DX].rearrange("e (j g d) -> e j g d", j=JB, g=2)
        upT = raw[0:EX, 1024:1024 + C]
        xpr2 = raw[0:RX, 1280:1280 + 2 * DX].rearrange("r (j g d) -> r j g d", j=JB, g=2)
        dtT = raw[0:RX, 1792:1792 + DX]
        xpT = raw2[:, 0:JB * 2 * NX].rearrange("p (j n) -> p j n", j=JB)
        NW = 1 + 2 + 1 + 2 + 1 + 2 + 1 + 2 * (1 + 1 + 1 + 1)

        with nc.Block() as block:
            @block.sync
            def _(sp):
                def ld(dst, src):
                    sp.dma_start(dst, src).then_inc(s_w, 16)
                ld(ident[:], ident_in)
                ld(inT, w["inT"])
                ld(upT, w["upT"])
                ld(dtT, w["dtT"])
                for g in range(2):
                    q = slice(64 * g, 64 * g + 64)
                    ld(down2[:, q], w["down"])
                    ld(outw2[:, :, g, :], w["outw"].rearrange("e (j d) -> e j d", j=JB))
                    ld(xpr2[:, :, g, :], w["xpr"].rearrange("r (j d) -> r j d", j=JB))
                    ld(xpT[q], w["xpT"].rearrange("(j d) n -> d j n", j=JB))
                    ld(cols[q], w["cols"].rearrange("(j d) n -> d j n", j=JB))
                    ld(amat[q], w["alog"].rearrange("(j d) n -> d j n", j=JB))
                    ld(bn[q], w["bn"])

                def stack_pieces(T):
                    for m, fill in enumerate(BC_FILLS):
                        sp.wait_ge(s_low, 3 * T + m + 1)
                        if m == 2:
                            sp.wait_ge(s_rc, T * NX + 2)
                        for k, (kind, g) in enumerate(fill):
                            for a in range(3):
                                sp.dma_start(bc[32 * a:32 * a + 32, kind * G16 + g, :],
                                             pieces[32 * k:32 * k + 32, m, a, :]).then_inc(s_bc[m // 2], 16)
                with sp.Fori(0, 2) as b2:
                    with sp.Fori(0, AT // 4) as rb:
                        for p in range(2):
                            i = b2 * (AT // 2) + rb * 2 + p
                            sp.wait_ge(s_done, i + 1)
                            for g in range(2):
                                src = x_s[:, g * HT * TOK:(g + 1) * HT * TOK]
                                dst = xt[64 * g:64 * g + 64, p, :]
                                if vertical:
                                    src = src.rearrange("c (b h w) -> c b h w", b=2, w=W)
                                    src = src[:, bass.ds(b2, 1), :, bass.ds((rb * 2 + p) * NSEQ, NSEQ)].squeeze(1)
                                    dst = dst.rearrange("c (h w) -> c h w", w=NSEQ)
                                else:
                                    src = src[:, bass.ds(b2 * L + (rb * 2 + p) * TOK, TOK)]
                                sp.dma_start(dst, src).then_inc(s_x[p], 16)
                            stack_pieces(i)
                sp.wait_ge(s_done, AT + 1)
                for g in range(2):
                    sp.dma_start(xt[64 * g:64 * g + 64, 0, :], x_s[:, 0:TOK]).then_inc(s_x[0], 16)
                stack_pieces(AT)
                sp.wait_ge(s_bc[0], 16 * 24 * (AT + 1))
                sp.wait_ge(s_bc[1], 16 * 12 * (AT + 1))

            @block.vector
            def _(dve):
                v = nc.vector
                k = [0]

                def step(ins):
                    k[0] += 1
                    ins.then_inc(s_prep, 1)
                    dve.wait_ge(s_prep, k[0])
                for big in (inw, wdt, wbc, wo, mask, xpad, sel, bc):
                    v.memset(big[:], 1.0 if big is mask else 0.0)
                v.memset(consts[:, 0:1], HALF_LOG)
                step(v.memset(consts[:, 1:2], 1e-5))
                v.memset(mask[:].rearrange("p (s l) -> p s l", l=SEQ)[:, :, 0], 0.0)
                dve.wait_ge(s_w, 16 * NW)
                for m in range(3):
                    rows = slice(32 * m, 32 * m + 32)
                    v.tensor_copy(sel[rows], ident[rows, rows].rearrange("p (g n) -> p n g", g=2).unsqueeze(3)
                                  .broadcast_to([32, 16, 2, 64]))
                step(v.tensor_scalar(cols[:, :, TAP:CB + 1], cols[:, :, TAP:CB + 1], 0.5, None, ALU.mult))
                for j in range(JB):
                    v.tensor_scalar(diag_d[:, j, :], ident[:], cols[:, j, DP:DP + 1], None, ALU.mult)
                for g in range(2):
                    q = slice(64 * g, 64 * g + 64)
                    for slot, (kind, m) in enumerate(f for fill in BC_FILLS for f in fill):
                        v.tensor_scalar(wbc[q, :, slot, g, :], xpT[q, :, kind * NX + m * 16:kind * NX + m * 16 + 16],
                                        0.5 if kind else 1.0, None, ALU.mult)
                dve.wait_ge(s_wps, 1)
                for g in range(2):
                    q = slice(64 * g, 64 * g + 64)
                    v.tensor_copy(inw[q, 0:JB, q], pf[q, 0:DX].rearrange("p (j d) -> p j d", j=JB))
                    last = v.tensor_scalar(inw[q, JB:2 * JB, q], pf[q, DX:2 * DX].rearrange("p (j d) -> p j d", j=JB),
                                           0.5, None, ALU.mult)
                step(last)
                dve.wait_ge(s_wps, 1 + JB)
                for kk in range(JB):
                    for g in range(2):
                        q = slice(64 * g, 64 * g + 64)
                        v.tensor_copy(wdt[q, kk, :, q], py[q, kk, 0:DX].rearrange("p (j d) -> p j d", j=JB))
                dve.wait_ge(s_wps, 4 + JB)
                for j in range(JB):
                    for g in range(2):
                        q = slice(64 * g, 64 * g + 64)
                        v.tensor_copy(wo[q, j, q], pb[q, j % 2, (j // 2) * 64:(j // 2) * 64 + 64])
                dve.wait_ge(s_aexp, 1)
                step(v.tensor_tensor(bsc[:, 0:1], bsc[:, 3:4], bn[:, 0:1], ALU.mult))
                step(v.tensor_tensor(bsc[:, 2:3], bn[:, 2:3], bsc[:, 0:1], ALU.mult))
                step(v.tensor_tensor(bsc[:, 1:2], bn[:, 1:2], bsc[:, 2:3], ALU.subtract))
                v.tensor_scalar(amat[:], amat[:], -5.0, 5.0, ALU.max, ALU.min).then_inc(s_aexp, 1)
                dve.wait_ge(s_aexp, 3)
                step(v.tensor_scalar(amat[:], amat[:], -1.0, -5.0, ALU.mult, ALU.max))
                step(v.tensor_scalar(amh[:], amat[:], -0.5, None, ALU.mult))
                for m, (s, n) in enumerate([(s_b, 2), (s_rc, 2), (s_h, 2), (s_g, 4), (s_bp, 1), (s_y, 4), (s_fe, 1), (s_done, 2)]):
                    v.memset(mark[:, m:m + 1], 0.0).then_inc(s, n)

                seqs = lambda ap: ap.rearrange("p (s l) -> p s l", l=SEQ)

                def conv(T, base, first, j):
                    if j > 0 or not first:
                        dve.wait_ge(s_xc, T * JB + j)
                    dve.wait_ge(s_fe, base + F_X + j + 2)
                    for n in range(4):
                        src = xpad[:, :, n:n + SEQ]
                        tap = cols[:, j, TAP + n:TAP + n + 1]
                        if n == 0:
                            ins = v.tensor_scalar(seqs(cvb[:]), src, tap, cols[:, j, CB:CB + 1], ALU.mult, ALU.add)
                        else:
                            dve.wait_ge(s_cv, (T * JB + j) * 3 + n)
                            ins = v.scalar_tensor_tensor(seqs(cvb[:]), src, tap, seqs(cvb[:]), ALU.mult, ALU.add)
                        ins.then_inc(s_cv if n < 3 else s_v, 1)

                def silu(T, j):
                    dve.wait_ge(s_v, T * JB + j + 1)
                    dve.wait_ge(s_th, T * JB + j + 1)
                    v.scalar_tensor_tensor(xc[:, j, :], th[:], 1.0, cvb[:], ALU.add, ALU.mult).then_inc(s_xc, 1)

                def gates(T, tp, j):
                    dve.wait_ge(s_tz, T * JB + j + 1)
                    v.scalar_tensor_tensor(gate[:, tp, j, :], tz[:], 1.0, pf[:], ALU.add, ALU.mult).then_inc(s_fe, 1)

                def steps(T, tp):
                    dtt, sf = dt[:, tp], sfx[:, tp]
                    dve.wait_ge(s_sp, T + 1)
                    v.tensor_tensor(dtt, dtt, sf, ALU.add).then_inc(s_dt, 1)
                    dve.wait_ge(s_dt, T + 1)
                    v.tensor_tensor(dx[:, tp], dtt, xc[:], ALU.mult)
                    for j in range(JB):
                        last = v.tensor_tensor_scan(sf[:, j, :], mask[:], dtt[:, j, :], 0.0, ALU.mult, ALU.add)
                    last.then_inc(s_pf, 1)
                    dve.wait_ge(s_pf, 3 * T + 1)
                    v.memset(dtt.rearrange("p j (s l) -> p j s l", l=SEQ)[:, :, :, 0], RESET)
                    s4 = sf.rearrange("p j (s l) -> p j s l", l=SEQ)
                    v.tensor_copy(tot[:], s4[:, :, :, SEQ - 1]).then_inc(s_pf, 1)
                    dve.wait_ge(s_pf, 3 * T + 2)
                    for j in range(JB):
                        last = v.tensor_tensor(s4[:, j], s4[:, j], tot[:, j, :].unsqueeze(2).broadcast_to([128, NSEQ, SEQ]),
                                               ALU.subtract)
                    last.then_inc(s_pf, 1)
                    dve.wait_ge(s_pf, 3 * T + 3)
                    v.memset(mark[:, 8:9], 0.0).then_inc(s_rdy, 1)

                def remainder(T, base, m):
                    if m > 0:
                        dve.wait_ge(s_low, 3 * T + m)
                    dve.wait_ge(s_hi, 3 * T + m + 1)
                    v.tensor_tensor(rest[:], pf[:], pieces[:, m, 0, :], ALU.subtract).then_inc(s_fe, 1)

                def low(T, m):
                    dve.wait_ge(s_mid, 3 * T + m + 1)
                    v.tensor_tensor(pieces[:, m, 2, :], rest[:], pieces[:, m, 1, :], ALU.subtract).then_inc(s_low, 1)

                def unit(i, p, q, n):
                    un, group = i * NX + q * 16 + n, i * G16 + q
                    b3 = bv[:, n % 4, :].rearrange("p (j t) -> p j t", j=JB)
                    r3 = rv[:, n % 4, :].rearrange("p (j t) -> p j t", j=JB)
                    if n not in POOL:
                        dve.wait_ge(s_bb, un + 1)
                        dve.wait_ge(s_g, un + 1)
                        v.tensor_tensor(b3, dx[:, p], pb[:, n % 2, :].unsqueeze(1).broadcast_to([128, JB, TOK]),
                                        ALU.mult).then_inc(s_b, 1)
                    dve.wait_ge(s_t, un + 1)
                    dve.wait_ge(s_cb, un + 1)
                    v.scalar_tensor_tensor(r3, r3, 1.0, pc[:, n % 2, :].unsqueeze(1).broadcast_to([128, JB, TOK]),
                                           ALU.add, ALU.mult).then_inc(s_rc, 1)
                    dve.wait_ge(s_a, un + 1)
                    if n in POOL:
                        dve.wait_ge(s_bp, group * PN + pools(n) + 2)
                    else:
                        dve.wait_ge(s_b, group * DN + n - pools(n) + 3)
                    v.tensor_tensor_scan(bv[:, n % 4, :], av[:, n % 2, :], bv[:, n % 4, :], 0.0,
                                         ALU.mult, ALU.add).then_inc(s_h, 1)

                for j in range(JB):
                    conv(0, 0, True, j)
                    silu(0, j)
                steps(0, 0)
                for m in range(3):
                    remainder(0, 0, m)
                    low(0, m)
                for j in range(JB):
                    gates(0, 0, j)
                for b2, rb, p, i in tiles(dve):
                    for n in range(16):
                        unit(i, p, 0, n)
                        for j in range(JB):
                            if n == 6 + 2 * j:
                                silu(i + 1, j)
                            if n == 4 + 2 * j:
                                conv(i + 1, FRONT + NF * i, False, j)
                    steps(i + 1, 1 - p)
                    with dve.Fori(1, G16 - 1) as q:
                        for n in range(16):
                            unit(i, p, q, n)
                    for n in range(16):
                        unit(i, p, G16 - 1, n)
                        for m in range(3):
                            if n == 1 + 3 * m:
                                remainder(i + 1, FRONT + NF * i, m)
                            if n == 3 + 3 * m:
                                low(i + 1, m)
                        for j in range(JB):
                            if n == 10 + 2 * j:
                                gates(i + 1, 1 - p, j)
                    dve.wait_ge(s_y, (i + 1) * NX + 4)
                    v.tensor_tensor(gate[:, p], gate[:, p], py[:], ALU.mult).then_inc(s_yz, 1)
                    dve.wait_ge(s_o, i + 1)
                    v.memset(mark[:, 10:11], 0.0).then_inc(s_fe, 1)
                    if vertical:
                        v.memset(mark[:, 9:10], 0.0).then_inc(s_done, 1)
                    else:
                        v.tensor_tensor(tz[:], tz[:], xt[:, p, :], ALU.add).then_inc(s_ac, 1)
                        dve.wait_ge(s_ac, i + 1)
                        image = acc[:, bass.ds(1 + b2 * (H + 1) + (rb * 2 + p) * ROWS, ROWS), 1:1 + W]
                        v.tensor_tensor(image, image, tz[:].rearrange("p (r c) -> p r c", c=W),
                                        ALU.add).then_inc(s_done, 1)

            @block.scalar
            def _(act):
                a = nc.scalar
                act.wait_ge(s_prep, 1)
                act.wait_ge(s_w, 16 * NW)
                a.activation(bsc[:, 3:4], bn[:, 3:4], ACT.Ln, bias=consts[:, 1:2]).then_inc(s_act, 1)
                act.wait_ge(s_act, 1)
                a.activation(bsc[:, 3:4], bsc[:, 3:4], ACT.Exp, scale=-0.5).then_inc(s_aexp, 1)
                act.wait_ge(s_aexp, 2)
                a.activation(amat[:], amat[:], ACT.Exp).then_inc(s_aexp, 1)
                act.wait_ge(s_done, 2)

                def copy(T, base, first, j):
                    act.wait_ge(s_ff, base + F_X + j + 1)
                    if j > 0 or not first:
                        act.wait_ge(s_v, T * JB + j)
                    a.activation(xpad[:, :, HIST:HIST + SEQ], pf[:].rearrange("p (s l) -> p s l", l=SEQ),
                                 ACT.Copy).then_inc(s_fe, 1)

                def tanh_x(T, first, j):
                    if j > 0 or not first:
                        act.wait_ge(s_xc, T * JB + j)
                    act.wait_ge(s_v, T * JB + j + 1)
                    a.activation(th[:], cvb[:], ACT.Tanh).then_inc(s_th, 1)

                def tanh_z(T, base, j):
                    act.wait_ge(s_ff, base + F_Z + j + 1)
                    act.wait_ge(s_done, T + 1)
                    a.activation(tz[:], pf[:], ACT.Tanh).then_inc(s_tz, 1)

                def softplus(T, base, tp, j):
                    act.wait_ge(s_ff, base + F_DT + j + 1)
                    a.activation(sfx[:, tp, j, :], pf[:], ACT.Abs, bias=cols[:, j, DTB:DTB + 1]).then_inc(s_act, 1)
                    a.activation(dt[:, tp, j, :], pf[:], ACT.Relu, bias=cols[:, j, DTB:DTB + 1]).then_inc(s_fe, 1)
                    act.wait_ge(s_act, 2 * JB * T + 2 * j + 2)
                    a.activation(sfx[:, tp, j, :], sfx[:, tp, j, :], ACT.Exp, scale=-1.0).then_inc(s_act, 1)

                def log(T, tp):
                    act.wait_ge(s_act, 2 * JB * T + 2 * JB + 1)
                    a.activation(sfx[:, tp], sfx[:, tp], ACT.Ln, bias=1.0).then_inc(s_sp, 1)

                def high(T, base, m):
                    act.wait_ge(s_ff, base + F_BC + m + 1)
                    a.activation(pieces[:, m, 0, :], pf[:], ACT.Copy).then_inc(s_hi, 1)

                def middle(T, base, m):
                    act.wait_ge(s_fe, base + F_BC + m + 2)
                    a.activation(pieces[:, m, 1, :], rest[:], ACT.Copy).then_inc(s_mid, 1)

                def unit(i, p, q, n):
                    un = i * NX + q * 16 + n
                    at = q * 16 + n
                    if n in POOL:
                        act.wait_ge(s_bb, un + 1)
                        act.wait_ge(s_bp, (i * G16 + q) * PN + pools(n) + 1)
                        a.activation(bcopy[:], pb[:, n % 2, :], ACT.Copy).then_inc(s_bk, 1)
                    act.wait_ge(s_y, un + 1)
                    for j in range(JB):
                        ins = a.activation(rv[:, n % 4, j * TOK:(j + 1) * TOK], sfx[:, p, j, :], ACT.Tanh,
                                           bias=consts[:, 0:1], scale=amh[:, j, bass.ds(at, 1)])
                    ins.then_inc(s_t, 1)
                    act.wait_ge(s_h, un + 1)
                    for j in range(JB):
                        ins = a.activation(av[:, n % 2, j * TOK:(j + 1) * TOK], dt[:, p, j, :], ACT.Exp,
                                           scale=amat[:, j, bass.ds(at, 1)])
                    ins.then_inc(s_a, 1)

                for j in range(JB):
                    copy(0, 0, True, j)
                    tanh_x(0, True, j)
                for j in range(JB):
                    softplus(0, 0, 0, j)
                log(0, 0)
                for m in range(3):
                    high(0, 0, m)
                    middle(0, 0, m)
                for j in range(JB):
                    tanh_z(0, 0, j)
                for b2, rb, p, i in tiles(act):
                    base = FRONT + NF * i
                    act.wait_ge(s_rdy, i + 1)
                    for n in range(16):
                        unit(i, p, 0, n)
                        for j in range(JB):
                            if n == 5 + 2 * j:
                                tanh_x(i + 1, False, j)
                            if n == 4 + 2 * j:
                                copy(i + 1, base, False, j)
                            if n == 12 + j:
                                softplus(i + 1, base, 1 - p, j)
                    log(i + 1, 1 - p)
                    with act.Fori(1, G16 - 1) as q:
                        for n in range(16):
                            unit(i, p, q, n)
                    for n in range(16):
                        unit(i, p, G16 - 1, n)
                        for m in range(3):
                            if n == 1 + 3 * m:
                                high(i + 1, base, m)
                            if n == 3 + 3 * m:
                                middle(i + 1, base, m)
                        for j in range(JB):
                            if n == 10 + 2 * j:
                                tanh_z(i + 1, base, j)
                    act.wait_ge(s_ff, base + NF)
                    if vertical:
                        rows = acc[:, bass.ds(1 + b2 * (H + 1), H), bass.ds(1 + (rb * 2 + p) * NSEQ, NSEQ)]
                        a.activation(rows.rearrange("p h w -> p w h"), pf[:].rearrange("p (w h) -> p w h", h=H),
                                     ACT.Identity, bias=bsc[:, 1:2], scale=bsc[:, 0:1]).then_inc(s_o, 1)
                    else:
                        a.activation(tz[:], pf[:], ACT.Identity, bias=bsc[:, 1:2], scale=bsc[:, 0:1]).then_inc(s_o, 1)

            @block.gpsimd
            def _(pool):
                for b2, rb, p, i in tiles(pool):
                    with pool.Fori(0, G16) as q:
                        for n in range(16):
                            un = i * NX + q * 16 + n
                            pool.wait_ge(s_rc, un + 3)
                            pool.wait_ge(s_h, un + 3)
                            nc.gpsimd.tensor_tensor(rv[:, n % 4, :], rv[:, n % 4, :], bv[:, n % 4, :],
                                                    ALU.mult).then_inc(s_g, 1)
                            if n + LOOK in POOL:
                                m = n + LOOK
                                pool.wait_ge(s_bk, (i * G16 + q) * PN + pools(m) + 1)
                                pool.wait_ge(s_g, un + LOOK + 1)
                                nc.gpsimd.tensor_tensor(bv[:, m % 4, :].rearrange("p (j t) -> p j t", j=JB), dx[:, p],
                                                        bcopy[:].unsqueeze(1).broadcast_to([128, JB, TOK]),
                                                        ALU.mult).then_inc(s_bp, 1)

            @block.tensor
            def _(pe):
                t = nc.tensor
                pe.wait_ge(s_w, 16 * NW)
                t.matmul(pf[:, 0:2 * DX], down2, inT, start=True, stop=True).then_inc(s_wps, 1)
                for kk in range(JB):
                    t.matmul(py[:, kk, 0:DX], xpr2[:, kk].rearrange("r g d -> r (g d)"), dtT, start=True,
                             stop=True).then_inc(s_wps, 1)
                for j in range(JB):
                    t.matmul(pb[:, j % 2, (j // 2) * 64:(j // 2) * 64 + 64], outw2[:, j].rearrange("e g d -> e (g d)"),
                             upT, start=True, stop=True).then_inc(s_wps, 1)

                def front_free(base, f):
                    pe.wait_ge(s_fe, base + f + 1)

                def in_proj(base, tp, j):
                    front_free(base, F_X + j if j < JB else F_Z + j - JB)
                    xin = xt[:, tp, :]
                    if vertical:
                        xin = xin.rearrange("p (h w) -> p w h", w=NSEQ)
                    t.matmul(pf[:].rearrange("p (a b) -> p a b", b=SEQ) if vertical else pf[:], inw[:, j, :], xin,
                             start=True, stop=True).then_inc(s_ff, 1)

                def dt_proj(T, base, j):
                    if j == 0:
                        pe.wait_ge(s_xc, T * JB + JB)
                    front_free(base, F_DT + j)
                    for kk in range(JB):
                        mm = t.matmul(pf[:], wdt[:, kk, j, :], xc[:, kk, :], start=(kk == 0), stop=(kk == JB - 1))
                    mm.then_inc(s_ff, 1)

                def bc_proj(base, m):
                    front_free(base, F_BC + m)
                    for kk in range(JB):
                        mm = t.matmul(pf[:], wbc[:, kk, 4 * m:4 * m + 4].rearrange("p s g n -> p (s g n)"),
                                      xc[:, kk, :], start=(kk == 0), stop=(kk == JB - 1))
                    mm.then_inc(s_ff, 1)

                def spread(i, q, n):
                    un = i * NX + q * 16 + n
                    lhsT = sel[:, n % 16].rearrange("p g d -> p (g d)")
                    if n - 2 in POOL:
                        pe.wait_ge(s_bk, (i * G16 + q) * PN + pools(n - 1))
                    else:
                        pe.wait_ge(s_b, (i * G16 + q) * DN + max(n, 1) + 1 - pools(n - 1))
                    t.matmul(pb[:, n % 2, :], lhsT, bc[:, bass.ds(q + n // 16, 1), :].squeeze(1),
                             start=True, stop=True).then_inc(s_bb, 1)
                    pe.wait_ge(s_rc, un + 1)
                    t.matmul(pc[:, n % 2, :], lhsT, bc[:, bass.ds(q + (G16 + n // 16), 1), :].squeeze(1),
                             start=True, stop=True).then_inc(s_cb, 1)

                def add(i, q, n):
                    pe.wait_ge(s_g, i * NX + q * 16 + n + 5)
                    for j in range(JB):
                        mm = t.matmul(py[:, j, :], ident[:], rv[:, n % 4, j * TOK:(j + 1) * TOK], start=False,
                                      stop=True, skip_group_check=True)
                    mm.then_inc(s_y, 1)

                def open_tile(i):
                    for j in range(JB):
                        t.matmul(py[:, j, :], diag_d[:, j, :], xc[:, j, :], start=True, stop=False, skip_group_check=True)

                pe.wait_ge(s_x[0], 32)
                pe.wait_ge(s_done, 2)
                for j in range(JB):
                    in_proj(0, 0, j)
                for j in range(JB):
                    dt_proj(0, 0, j)
                for m in range(len(BC_FILLS)):
                    bc_proj(0, m)
                for j in range(JB):
                    in_proj(0, 0, JB + j)
                open_tile(0)
                pe.wait_ge(s_bc[0], 16 * 24)
                spread(0, 0, 0)
                for b2, rb, p, i in tiles(pe):
                    base = FRONT + NF * i
                    for n in range(16):
                        if n == 15:
                            pe.wait_ge(s_bc[1], 16 * 12 * (i + 1))
                        spread(i, 0, n + 1)
                        if n >= LAG:
                            add(i, 0, n - LAG)
                        for j in range(JB):
                            if n == 3 and j == 0:
                                pe.wait_ge(s_x[1 - p], 32 * (b2 * (AT // 4) + rb) + 32 * (p + 1))
                            if n == 3 + 2 * j:
                                in_proj(base, 1 - p, j)
                            if n == 11 + j:
                                dt_proj(i + 1, base, j)
                    with pe.Fori(1, G16 - 1) as q:
                        for n in range(16):
                            spread(i, q, n + 1)
                            add(i, q, n - LAG)
                    for n in range(16):
                        if n < 15:
                            spread(i, G16 - 1, n + 1)
                        add(i, G16 - 1, n - LAG)
                        for j in range(JB):
                            if n == 9 + 2 * j:
                                in_proj(base, 1 - p, JB + j)
                            if n == 3 * j:
                                bc_proj(base, j)
                    for n in range(16 - LAG, 16):
                        add(i, G16 - 1, n)
                    pe.wait_ge(s_yz, i + 1)
                    front_free(base, F_O)
                    for j in range(JB):
                        mm = t.matmul(pf[:], wo[:, j, :], gate[:, p, j, :], start=(j == 0), stop=(j == JB - 1))
                    mm.then_inc(s_ff, 1)
                    pe.wait_ge(s_bc[0], 16 * 24 * (i + 2))
                    spread(i + 1, 0, 0)
                    open_tile(i + 1)


def phase_filter(nc, sem, ident_in, w, acc, x_s, slots_s):
    with ExitStack() as ctx:
        def sb(name, shape):
            return ctx.enter_context(nc.sbuf_tensor("f_" + name, shape, F32))

        def ps(name, shape):
            return ctx.enter_context(nc.psum_tensor("f_" + name, shape, F32))

        MID, K9, BLK = C // 2, 9, TOK // 128
        ident = sb("ident", [128, 128])
        w1T = sb("w1T", [128, K9, MID])
        w1 = sb("w1", [128, K9, 2, MID])
        w2T = sb("w2T", [2 * MID, K9])
        w2 = sb("w2", [2 * MID, 2, K9])
        b1 = sb("b1", [2 * MID, 1])
        b2r = sb("b2r", [128, K9])
        sel = sb("sel", [2 * K9, K9, 2, C])
        zero = sb("zero", [C, HIST])
        h1 = sb("h1", [2 * MID, TOK])
        h2 = sb("h2", [2 * MID, TOK])
        lg = sb("lg", [128, BLK * 2, K9])
        ex = sb("ex", [128, BLK * 2, K9])
        mx = sb("mx", [128, BLK * 2])
        sm = sb("sm", [128, BLK * 2])
        wt = sb("wt", [2 * K9, TOK])
        pr = sb("pr", [128, 2, TOK])
        total = sb("total", [128, TOK])
        ot = sb("ot", [128, TOK])
        ph = ps("ph", [128, TOK])
        pl = ps("pl", [128, 512])
        pt = ps("pt", [128, TOK])
        pw = ps("pw", [128, 2, TOK])

        s_w, s_prep, s_done, s_out = sem("f_weights"), sem("f_prep_step"), sem("f_tile_done"), sem("f_stored")
        s_h, s_h1, s_h2, s_l, s_d = sem("f_conv1"), sem("f_biased"), sem("f_leaky"), sem("f_logits"), sem("f_dve_step")
        s_lx, s_ex, s_p, s_t, s_wt = sem("f_shifted"), sem("f_exp"), sem("f_softmax"), sem("f_transposed"), sem("f_weights_t")
        s_wb, s_pr, s_sum = sem("f_weight_bcast"), sem("f_product"), sem("f_summed")
        NW = 1 + 2 * 3 + 1
        OUTS = 6

        with nc.Block() as block:
            @block.sync
            def _(sp):
                sp.dma_start(ident[:], ident_in).then_inc(s_w, 16)
                for g in range(2):
                    sp.dma_start(w1T[g * C:(g + 1) * C], w["w1T"]).then_inc(s_w, 16)
                    sp.dma_start(w2T[g * MID:(g + 1) * MID], w["w2T"]).then_inc(s_w, 16)
                    sp.dma_start(b1[g * MID:(g + 1) * MID], w["b1"]).then_inc(s_w, 16)
                sp.dma_start(b2r[:], w["b2"].partition_broadcast(128)).then_inc(s_w, 16)
                with sp.Fori(0, 2) as b2:
                    with sp.Fori(0, TPB) as rb:
                        i = b2 * TPB + rb
                        sp.wait_ge(s_done, i + 2)
                        for g in range(2):
                            q = slice(g * C, (g + 1) * C)
                            t = b2 * TPB + rb + g * HT
                            sp.dma_start(x_s[:, bass.ds(t * TOK, TOK)], ot[q, :]).then_inc(s_out, 16)
                            sp.dma_start(slots_s[:, bass.ds(t, 1), HIST:SLOT], ot[q, :].unsqueeze(1)).then_inc(s_out, 16)
                            sp.dma_start(slots_s[:, bass.ds(t + 1, 1), 0:HIST],
                                         ot[q, TOK - HIST:TOK].unsqueeze(1)).then_inc(s_out, 16)
                sp.dma_start(slots_s[:, 0, 0:HIST], zero[:]).then_inc(s_out, 16)
                sp.wait_ge(s_out, 16 * OUTS * (HT + 1) + 16)

            @block.vector
            def _(dve):
                v = nc.vector
                k = [0]

                def step(ins):
                    k[0] += 1
                    ins.then_inc(s_prep, 1)
                    dve.wait_ge(s_prep, k[0])
                v.memset(w1[:], 0.0)
                v.memset(zero[:], 0.0)
                step(v.memset(w2[:], 0.0))
                dve.wait_ge(s_w, 16 * NW)
                for g in range(2):
                    v.tensor_copy(w1[g * C:(g + 1) * C, :, g, :], w1T[g * C:(g + 1) * C])
                    v.tensor_copy(w2[g * MID:(g + 1) * MID, g, :], w2T[g * MID:(g + 1) * MID])
                v.tensor_copy(sel[:], ident[0:2 * K9, 0:2 * K9].rearrange("p (g n) -> p n g", g=2).unsqueeze(3)
                              .broadcast_to([2 * K9, K9, 2, C]))
                v.memset(mx[:], 0.0).then_inc(s_out, 16 * OUTS)
                v.memset(sm[:], 0.0).then_inc(s_done, 1)
                dve.wait_ge(s_done, 1)
                STEPS = 4
                with dve.Fori(0, 2) as b2:
                    with dve.Fori(0, TPB) as rb:
                        i = b2 * TPB + rb
                        r = image_row(b2, rb)
                        dve.wait_ge(s_h1, i + 1)
                        v.scalar_tensor_tensor(h2[:], h1[:], 0.2, h1[:], ALU.mult, ALU.max).then_inc(s_h2, 1)
                        dve.wait_ge(s_l, i + 1)
                        v.tensor_tensor(lg[:], pl[:, 0:BLK * 2 * K9].rearrange("p (m n) -> p m n", n=K9),
                                        b2r[:].unsqueeze(1).broadcast_to([128, BLK * 2, K9]), ALU.add).then_inc(s_d, 1)
                        dve.wait_ge(s_d, i * STEPS + 1)
                        v.tensor_reduce(mx[:], lg[:], AX_X, ALU.max).then_inc(s_d, 1)
                        dve.wait_ge(s_d, i * STEPS + 2)
                        v.tensor_tensor(lg[:], lg[:], mx[:].unsqueeze(2).broadcast_to([128, BLK * 2, K9]),
                                        ALU.subtract).then_inc(s_lx, 1)
                        dve.wait_ge(s_ex, i + 1)
                        v.tensor_reduce(sm[:], ex[:], AX_X, ALU.add).then_inc(s_d, 1)
                        dve.wait_ge(s_d, i * STEPS + 3)
                        v.reciprocal(mx[:], sm[:]).then_inc(s_d, 1)
                        dve.wait_ge(s_d, i * STEPS + 4)
                        v.tensor_tensor(lg[:], ex[:], mx[:].unsqueeze(2).broadcast_to([128, BLK * 2, K9]),
                                        ALU.mult).then_inc(s_p, 1)
                        for n in range(K9 + 1):
                            if n < K9:
                                dve.wait_ge(s_wb, i * K9 + n + 1)
                                if n == 0:
                                    dve.wait_ge(s_done, i + 1)
                                if n >= 3:
                                    dve.wait_ge(s_sum, i * (K9 - 1) + n - 2)
                                v.tensor_tensor((pr[:, n % 2, :] if n else total[:]).rearrange("p (r c) -> p r c", c=W),
                                                pw[:, n % 2, :].rearrange("p (r c) -> p r c", c=W),
                                                acc[:, bass.ds(r + n // 3, ROWS), n % 3:n % 3 + W],
                                                ALU.mult).then_inc(s_pr, 1)
                            if n >= 2:
                                dve.wait_ge(s_pr, i * K9 + n)
                                if n >= 3:
                                    dve.wait_ge(s_sum, i * (K9 - 1) + n - 2)
                                v.tensor_tensor(total[:], total[:], pr[:, (n - 1) % 2, :], ALU.add).then_inc(s_sum, 1)
                        dve.wait_ge(s_sum, (i + 1) * (K9 - 1))
                        dve.wait_ge(s_out, 16 * OUTS * (i + 1))
                        v.scalar_tensor_tensor(ot[:].rearrange("p (r c) -> p r c", c=W),
                                               acc[:, bass.ds(r + 1, ROWS), 1:1 + W], 2.0,
                                               total[:].rearrange("p (r c) -> p r c", c=W),
                                               ALU.mult, ALU.subtract).then_inc(s_done, 1)

            @block.scalar
            def _(act):
                a = nc.scalar
                act.wait_ge(s_w, 16 * NW)
                with act.Fori(0, HT) as i:
                    act.wait_ge(s_h, i + 1)
                    a.activation(h1[:], ph[0:2 * MID, :], ACT.Identity, bias=b1[:]).then_inc(s_h1, 1)
                    act.wait_ge(s_lx, i + 1)
                    a.activation(ex[:], lg[:], ACT.Exp).then_inc(s_ex, 1)
                    act.wait_ge(s_t, i + 1)
                    a.activation(wt[:], pt[0:2 * K9, :], ACT.Copy).then_inc(s_wt, 1)

            @block.tensor
            def _(pe):
                t = nc.tensor

                def conv(i, r):
                    if not isinstance(i, int) or i > 0:
                        pe.wait_ge(s_h1, i)
                    for n in range(K9):
                        mm = t.matmul(ph[0:2 * MID, :], w1[:, n].rearrange("p g m -> p (g m)"),
                                      acc[:, bass.ds(r + n // 3, ROWS), n % 3:n % 3 + W],
                                      start=(n == 0), stop=(n == K9 - 1))
                    mm.then_inc(s_h, 1)

                def weights(i, next_row):
                    pe.wait_ge(s_h2, i + 1)
                    for m in range(BLK):
                        mm = t.matmul(pl[:, m * 2 * K9:(m + 1) * 2 * K9], h2[:, m * 128:(m + 1) * 128],
                                      w2[:].rearrange("p g n -> p (g n)"), start=True, stop=True)
                    mm.then_inc(s_l, 1)
                    if next_row is not None:
                        conv(i + 1, next_row)
                    pe.wait_ge(s_p, i + 1)
                    for m in range(BLK):
                        mm = t.matmul(pt[0:2 * K9, m * 128:(m + 1) * 128],
                                      lg[:, 2 * m:2 * m + 2, :].rearrange("p g n -> p (g n)"), ident[:],
                                      start=True, stop=True)
                    mm.then_inc(s_t, 1)
                    pe.wait_ge(s_wt, i + 1)
                    for n in range(K9):
                        if n >= 2:
                            pe.wait_ge(s_pr, i * K9 + n - 1)
                        t.matmul(pw[:, n % 2, :], sel[:, n].rearrange("p g c -> p (g c)"), wt[:], start=True,
                                 stop=True).then_inc(s_wb, 1)

                pe.wait_ge(s_done, 1)
                conv(0, image_row(0, 0))
                for b2 in range(2):
                    with pe.Fori(0, TPB - 1) as rb:
                        weights(rb + b2 * TPB, image_row(b2, rb + 1))
                    weights((b2 + 1) * TPB - 1, image_row(1, 0) if b2 == 0 else None)


def phase_clear(nc, sem, acc):
    s_clear = sem("acc_cleared")
    with nc.Block() as block:
        @block.vector
        def _(dve):
            nc.vector.memset(acc[:], 0.0).then_inc(s_clear, 1)
            dve.wait_ge(s_clear, 1)


def build(nc, ins, out):
    seq_s = nc.dram_tensor("seq_s", [C, NT], F32).ap()
    hn_s = nc.dram_tensor("hn_s", [C, TILES + 1, SLOT], F32).ap()
    first_s = nc.dram_tensor("first_s", [C, NT], F32).ap()
    filt_s = nc.dram_tensor("filt_s", [C, NT], F32).ap()
    slots_s = nc.dram_tensor("slots_s", [C, TILES + 1, SLOT], F32).ap()
    ident = ins["ident"]

    def part(prefix):
        return {k[len(prefix):]: v for k, v in ins.items() if k.startswith(prefix)}

    def run(phase, *args, **kw):
        with nc.cleanup_on_exit():
            phase(nc, lambda name: nc.alloc_semaphore(name=name), *args, **kw)

    run(phase_conv_norm, ident, ins, ins["x"], seq_s, hn_s)
    run(phase_mamba, ident, "m0_", part("M0_"), hn_s, seq_s, first_s, reset=True, final=False)
    with nc.sbuf_tensor("acc", [128, PADR, PADW], F32) as acc:
        run(phase_clear, acc)
        run(phase_axis, ident, "h_", part("H_"), first_s, acc, vertical=True)
        run(phase_axis, ident, "w_", part("W_"), first_s, acc, vertical=False)
        run(phase_filter, ident, part("F_"), acc, filt_s, slots_s)
    run(phase_mamba, ident, "m3_", part("M3_"), slots_s, filt_s, out, reset=False, final=True)


def layouts(inputs):
    a = {k: np.asarray(v) for k, v in inputs.items()}

    def cc(*xs):
        return np.ascontiguousarray(np.concatenate([x.reshape(x.shape[0], -1) for x in xs], axis=1))

    t = np.ascontiguousarray
    out = {"x": t(a["x"].transpose(1, 0, 2, 3).reshape(C, NT)), "ident": np.eye(128, dtype=np.float32)}
    p = "L0_conv_"
    out["L0_cols"] = cc(*[a[p + n] for n in ("dwh_b", "dww_b", "conv_b", "bn_g", "bn_b", "bn_m", "bn_v", "ln_g", "ln_b",
                                             "dwh_w", "dww_w")])
    out["L0_convT"] = t(a[p + "conv_w"].reshape(C, C).T)

    def mamba(tag, p, taps, convb, dp):
        out[tag + "inT"] = t(a[p + "in_proj_w"].T)
        out[tag + "cols"] = cc(a[p + convb], a[p + "dt_proj_b"], a[p + dp], a[p + "A_log"])
        out[tag + "xpT"] = t(a[p + "x_proj_w"].T)
        out[tag + "xpr"] = t(a[p + "x_proj_w"][0:RANK])
        out[tag + "dtT"] = t(a[p + "dt_proj_w"].T)
        out[tag + "outT"] = t(a[p + "out_proj_w"].T)
        out[tag + "taps"] = t(a[p + taps].reshape(D, 4).T)

    mamba("M0_", "L0_conv_", "convd_w", "convd_b", "Dp")
    mamba("M3_", "L3_conv_", "conv_w", "conv_b", "D")
    p = "L3_conv_"
    out["M3_ocols"] = cc(a[p + "proj_b"], a[p + "ln_g"], a[p + "ln_b"])
    out["M3_opw"] = a[p + "out_proj_w"]
    out["M3_pw"] = a[p + "proj_w"]
    for tag, m, d, u, n in (("H_", "hm_", "hd_w", "hu_w", "hn_"), ("W_", "wm_", "wd_w", "wu_w", "wn_")):
        p = "L1_conv_"
        out[tag + "inT"] = t(a[p + m + "in_w"].T)
        out[tag + "down"] = a[p + d]
        out[tag + "outw"] = a[p + m + "out_w"]
        out[tag + "upT"] = t(a[p + u].T)
        out[tag + "xpr"] = t(a[p + m + "xproj_w"][0:RX])
        out[tag + "dtT"] = t(a[p + m + "dproj_w"].T)
        out[tag + "xpT"] = t(a[p + m + "xproj_w"][RX:].T)
        out[tag + "cols"] = cc(a[p + m + "conv_w"], a[p + m + "conv_b"], a[p + m + "dproj_b"], a[p + m + "D"])
        out[tag + "alog"] = a[p + m + "A_log"]
        out[tag + "bn"] = cc(*[a[p + n + k] for k in ("gamma", "beta", "mean", "var")])
    p = "L2_conv_"
    out["F_w1T"] = t(a[p + "w1"].reshape(C // 2, C, 9).transpose(1, 2, 0))
    out["F_w2T"] = t(a[p + "w2"].reshape(9, C // 2).T)
    out["F_b1"] = a[p + "b1"].reshape(C // 2, 1)
    out["F_b2"] = a[p + "b2"]
    return out


def kernel(**inputs):
    import concourse.bacc as _bacc
    from concourse.bass_utils import run_bass_kernel_spmd as _run

    nc = _bacc.Bacc("TRN2", target_bir_lowering=False, num_devices=1)
    arrays, ins = {}, {}
    for name, a in layouts(inputs).items():
        arrays[f"in_{name}"] = a
        ins[name] = nc.dram_tensor(f"in_{name}", a.shape, mybir.dt.from_np(a.dtype), kind="ExternalInput").ap()
    out = nc.dram_tensor("out_0", (C, NT), F32, kind="ExternalOutput").ap()
    build(nc, ins, out)
    r = _run(nc, [arrays], core_ids=[0])
    got = r.results[0]["out_0"]
    return np.ascontiguousarray(np.asarray(got).reshape(C, B, H, W).transpose(1, 0, 2, 3))
```
